# Optimizing a Trainium2 kernel written in Bass

```python
import numpy as np
import jax
import jax.numpy as jnp

def _softmax(x, axis=-1):
    return jax.nn.softmax(x, axis=axis)

def _gelu(x):
    return jax.nn.gelu(x, approximate=True)

def _silu(x):
    return jax.nn.silu(x)

def _sigmoid(x):
    return jax.nn.sigmoid(x)

def _layernorm(x, axis=-1, eps=1e-05):
    m = jnp.mean(x, axis=axis, keepdims=True)
    v = jnp.var(x, axis=axis, keepdims=True)
    return (x - m) / jnp.sqrt(v + eps)

def _scatter_add(tgt, idx, src, axis=0):
    return tgt.at[idx].add(src)

def _segment_sum(src, seg, n):
    return jax.ops.segment_sum(src, seg, n)
kernel_name = 'mk_decoder_postln_d2_seqx_r4_e1c7a7'

def setup_inputs(seed: int=0):
    np.random.seed(seed)
    _w = jnp.asarray

    def _rec_inputs():
        import jax
        import jax.numpy as jnp
        _rk = jax.random.key(seed)
        x = -0.0003929 + 0.9999 * jax.random.normal(jax.random.fold_in(_rk, 1), (8, 256, 256), jnp.float32)
        _lenS = 256 - jax.random.randint(jax.random.fold_in(_rk, 7), (8,), 0, max(1, 256 // 4) + 1, jnp.int32)
        _lenS2 = 120 - jax.random.randint(jax.random.fold_in(_rk, 8), (8,), 0, max(1, 120 // 4) + 1, jnp.int32)
        _ctx_1024P = jax.random.normal(jax.random.fold_in(_rk, 11), (8, 16, 256), jnp.float32)
        _ctx_1024c = jax.random.dirichlet(jax.random.fold_in(_rk, 511), 0.3 * jnp.ones((16,), jnp.float32), (8, 120))
        _ctx_1024t = jnp.einsum('bsk,bkd->bsd', _ctx_1024c, _ctx_1024P)
        _ctx_1024t = _ctx_1024t * jax.lax.rsqrt(jnp.mean(jnp.square(_ctx_1024t)) + 1e-12) * 0.953939
        ctx_1024 = 2.81802e-05 + 1.00001 * (_ctx_1024t + 0.3 * jax.random.normal(jax.random.fold_in(_rk, 611), (8, 120, 256), jnp.float32))
        _validS = jnp.arange(256)[None, :] < _lenS[:, None]
        _validS2 = jnp.arange(120)[None, :] < _lenS2[:, None]
        _causal = jnp.tril(jnp.ones((256, 256), dtype=bool))
        mask_BxSxS2_ik0 = jnp.where(jnp.broadcast_to(_validS2[:, None, :], (8, 256, 120)), 0, 1).astype(jnp.int32)
        return (x, ctx_1024, mask_BxSxS2_ik0)
    x, ctx_1024, mask_BxSxS2_ik0 = _rec_inputs()

    def _L0_attn_setup():
        import jax, jax.numpy as jnp
        import numpy as np
        BATCH, SEQ, D_EMBED, N_HEADS, D_HEAD = (1, 512, 256, 16, 64)
        MASK_VAL = 10000000000.0
        key = jax.random.key(seed)
        ks = jax.random.split(key, 5)
        s = 1.0 / np.sqrt(D_EMBED).astype(np.float32)
        return {'x': jax.random.normal(ks[0], (BATCH, SEQ, D_EMBED), jnp.float32), 'W_Q': jax.random.normal(ks[1], (N_HEADS, D_HEAD, D_EMBED), jnp.float32) * s, 'W_K': jax.random.normal(ks[2], (N_HEADS, D_HEAD, D_EMBED), jnp.float32) * s, 'W_V': jax.random.normal(ks[3], (N_HEADS, D_HEAD, D_EMBED), jnp.float32) * s, 'W_O': jax.random.normal(ks[4], (N_HEADS, D_EMBED, D_HEAD), jnp.float32) * s}
    _L0_attn_all = _L0_attn_setup()
    _L0_attn_in = {k: v for k, v in _L0_attn_all.items() if k in ('W_Q', 'W_K', 'W_V', 'W_O')}
    del _L0_attn_all

    def _L0_xattn_setup():
        import jax, jax.numpy as jnp
        import numpy as np
        NEG = -1000000000.0
        key = jax.random.key(seed)
        k1, k2, k3, k4 = jax.random.split(key, 4)
        B, Sq, Sk, D = (8, 512, 512, 256)
        query = jax.random.normal(k1, (B, Sq, D), dtype=jnp.float32)
        memories = jax.random.normal(k2, (B, Sk, D), dtype=jnp.float32)
        mask = jax.random.randint(k3, (B, Sq, Sk), 0, 2).astype(jnp.int32)
        W = jax.random.normal(k4, (D, D), dtype=jnp.float32) * (1.0 / np.sqrt(D))
        b = jnp.zeros((D,), dtype=jnp.float32)
        return {'query': query, 'memories': memories, 'mask': mask, 'W': W, 'b': b}
    _L0_xattn_all = _L0_xattn_setup()
    _L0_xattn_in = {k: v for k, v in _L0_xattn_all.items() if k in ('W', 'b')}
    del _L0_xattn_all

    def _L0_ffn_setup():
        import jax, jax.numpy as jnp
        import numpy as np
        ALPHA = 1.702
        LIMIT = 9.0
        TOP_K = 2

        def swiglu(x):
            g, v = (x[..., 0::2], x[..., 1::2])
            g = jnp.clip(g, None, LIMIT)
            v = jnp.clip(v, -LIMIT, LIMIT)
            return g * jax.nn.sigmoid(ALPHA * g) * (v + 1)
        key = jax.random.key(seed)
        ks = jax.random.split(key, 6)
        B, L, D = (2, 512, 256)
        E, F = (8, 512)
        s_gate = 1.0 / np.sqrt(D)
        s1 = 1.0 / np.sqrt(D)
        s2 = 1.0 / np.sqrt(F)
        return {'x': jax.random.normal(ks[0], (B, L, D), dtype=jnp.float32), 'gate_w': jax.random.normal(ks[1], (D, E), dtype=jnp.float32) * s_gate, 'dense_1_w': jax.random.normal(ks[2], (E, 2 * F, D), dtype=jnp.float32) * s1, 'dense_1_b': jnp.zeros((E, 2 * F), dtype=jnp.float32), 'dense_2_w': jax.random.normal(ks[3], (E, D, F), dtype=jnp.float32) * s2, 'dense_2_b': jnp.zeros((E, D), dtype=jnp.float32)}
    _L0_ffn_all = _L0_ffn_setup()
    _L0_ffn_in = {k: v for k, v in _L0_ffn_all.items() if k in ('gate_w', 'dense_1_w', 'dense_1_b', 'dense_2_w', 'dense_2_b')}
    del _L0_ffn_all

    def _L1_attn_setup():
        import math
        import jax, jax.numpy as jnp
        import numpy as np
        D_MODEL = 256
        N_HEAD = 16
        HEAD_DIM = D_MODEL // N_HEAD
        B, T = (2, 512)

        def _layernorm(x, g, b, eps=1e-05):
            mu = jnp.mean(x, axis=-1, keepdims=True)
            var = jnp.mean(jnp.square(x - mu), axis=-1, keepdims=True)
            return (x - mu) * jax.lax.rsqrt(var + eps) * g + b

        def _l2norm(x, eps=1e-12):
            n = jnp.sqrt(jnp.sum(jnp.square(x), axis=-1, keepdims=True))
            return x / jnp.maximum(n, eps)

        def _rope(x, times):
            half = x.shape[-1] // 2
            freqs = jnp.exp(-jnp.arange(half, dtype=x.dtype) * (math.log(10000.0) / half))
            theta = times[:, None] * freqs[None, :]
            cos = jnp.cos(theta)[None, :, None, :]
            sin = jnp.sin(theta)[None, :, None, :]
            xr = x.reshape(*x.shape[:-1], half, 2)
            x1, x2 = (xr[..., 0], xr[..., 1])
            r1 = x1 * cos - x2 * sin
            r2 = x1 * sin + x2 * cos
            return jnp.stack([r1, r2], axis=-1).reshape(x.shape)
        key = jax.random.key(seed)
        ks = jax.random.split(key, 16)
        s = 0.02
        f32 = jnp.float32
        inp = {'x': jax.random.normal(ks[0], (B, T, D_MODEL), f32), 'Wq': jax.random.normal(ks[1], (D_MODEL, D_MODEL), f32) * s, 'Wk': jax.random.normal(ks[2], (D_MODEL, D_MODEL), f32) * s, 'Wv': jax.random.normal(ks[3], (D_MODEL, D_MODEL), f32) * s, 'gate_w': jax.random.normal(ks[4], (D_MODEL, D_MODEL), f32) * s, 'gate_b': jnp.zeros((D_MODEL,), f32), 'p_w': jax.random.normal(ks[5], (D_MODEL, D_MODEL), f32) * s, 'p_b': jnp.zeros((D_MODEL,), f32), 'out_w': jax.random.normal(ks[6], (D_MODEL, D_MODEL), f32) * s, 'out_b': jnp.zeros((D_MODEL,), f32), 'clock_w': jax.random.normal(ks[7], (D_MODEL, N_HEAD), f32) * s, 'clock_b': jnp.zeros((N_HEAD,), f32), 'ln1_g': jnp.ones((D_MODEL,), f32), 'ln1_b': jnp.zeros((D_MODEL,), f32), 'ln2_g': jnp.ones((D_MODEL,), f32), 'ln2_b': jnp.zeros((D_MODEL,), f32), 'mlp_w1': jax.random.normal(ks[8], (D_MODEL, 4 * D_MODEL), f32) * s, 'mlp_b1': jnp.zeros((4 * D_MODEL,), f32), 'mlp_w2': jax.random.normal(ks[9], (4 * D_MODEL, D_MODEL), f32) * s, 'mlp_b2': jnp.zeros((D_MODEL,), f32)}
        return inp
    _L1_attn_all = _L1_attn_setup()
    _L1_attn_in = {k: v for k, v in _L1_attn_all.items() if k in ('Wq', 'Wk', 'Wv', 'gate_w', 'gate_b', 'p_w', 'p_b', 'out_w', 'out_b', 'clock_w', 'clock_b', 'ln1_g', 'ln1_b', 'ln2_g', 'ln2_b', 'mlp_w1', 'mlp_b1', 'mlp_w2', 'mlp_b2')}
    del _L1_attn_all

    def _L1_xattn_setup():
        import jax, jax.numpy as jnp
        import numpy as np
        D_MODEL = 256
        DK = 64
        N_HEADS = D_MODEL // DK
        MASK = True
        key = jax.random.key(seed)
        ks = jax.random.split(key, 8)
        B, S = (4, 512)
        scale = 1.0 / np.sqrt(D_MODEL)
        return {'query_data': jax.random.normal(ks[0], (B, S, D_MODEL), dtype=jnp.float32), 'key_data': jax.random.normal(ks[1], (B, S, D_MODEL), dtype=jnp.float32), 'value_data': jax.random.normal(ks[2], (B, S, D_MODEL), dtype=jnp.float32), 'Wq': jax.random.normal(ks[3], (D_MODEL, D_MODEL), dtype=jnp.float32) * scale, 'Wk': jax.random.normal(ks[4], (D_MODEL, D_MODEL), dtype=jnp.float32) * scale, 'Wv': jax.random.normal(ks[5], (D_MODEL, D_MODEL), dtype=jnp.float32) * scale, 'Wp': jax.random.normal(ks[6], (D_MODEL, D_MODEL), dtype=jnp.float32) * scale, 'bp': jnp.zeros((D_MODEL,), dtype=jnp.float32)}
    _L1_xattn_all = _L1_xattn_setup()
    _L1_xattn_in = {k: v for k, v in _L1_xattn_all.items() if k in ('Wq', 'Wk', 'Wv', 'Wp', 'bp')}
    del _L1_xattn_all

    def _L1_ffn_setup():
        import jax, jax.numpy as jnp
        import numpy as np
        DIM = 256

        def _reference_tuple_inner(x, W_r, W_k, W_v, mu_r, mu_k):
            B, T, C = x.shape
            x_prev = jnp.concatenate([jnp.zeros((B, 1, C), x.dtype), x[:, :-1, :]], axis=1)
            xr = mu_r * x + (1.0 - mu_r) * x_prev
            xk = mu_k * x + (1.0 - mu_k) * x_prev
            r = jax.nn.sigmoid(jnp.einsum('btc,dc->btd', xr, W_r))
            k = jnp.einsum('btc,dc->btd', xk, W_k)
            k_act = jnp.square(jax.nn.relu(k))
            out = r * jnp.einsum('btc,dc->btd', k_act, W_v)
            new_state = x[:, -1, :]
            return (out, new_state)
        key = jax.random.key(seed)
        ks = jax.random.split(key, 6)
        B, T, C = (8, 512, DIM)
        x = jax.random.normal(ks[0], (B, T, C), dtype=jnp.float32)
        s = 1.0 / np.sqrt(C)
        W_r = jax.random.uniform(ks[1], (C, C), jnp.float32, -s, s)
        W_k = jax.random.uniform(ks[2], (C, C), jnp.float32, -s, s)
        W_v = jax.random.uniform(ks[3], (C, C), jnp.float32, -s, s)
        mu_r = jax.random.uniform(ks[4], (C,), jnp.float32)
        mu_k = jax.random.uniform(ks[5], (C,), jnp.float32)
        return {'x': x, 'W_r': W_r, 'W_k': W_k, 'W_v': W_v, 'mu_r': mu_r, 'mu_k': mu_k}
    _L1_ffn_all = _L1_ffn_setup()
    _L1_ffn_in = {k: v for k, v in _L1_ffn_all.items() if k in ('W_r', 'W_k', 'W_v', 'mu_r', 'mu_k')}
    del _L1_ffn_all
    return {'x': x, 'ctx_1024': ctx_1024, 'mask_BxSxS2_ik0': mask_BxSxS2_ik0, 'L0_attn_W_Q': _L0_attn_in['W_Q'], 'L0_attn_W_K': _L0_attn_in['W_K'], 'L0_attn_W_V': _L0_attn_in['W_V'], 'L0_attn_W_O': _L0_attn_in['W_O'], 'L0_xattn_W': _L0_xattn_in['W'], 'L0_xattn_b': _L0_xattn_in['b'], 'L0_ffn_gate_w': _L0_ffn_in['gate_w'], 'L0_ffn_dense_1_w': _L0_ffn_in['dense_1_w'], 'L0_ffn_dense_1_b': _L0_ffn_in['dense_1_b'], 'L0_ffn_dense_2_w': _L0_ffn_in['dense_2_w'], 'L0_ffn_dense_2_b': _L0_ffn_in['dense_2_b'], 'L1_attn_Wq': _L1_attn_in['Wq'], 'L1_attn_Wk': _L1_attn_in['Wk'], 'L1_attn_Wv': _L1_attn_in['Wv'], 'L1_attn_gate_w': _L1_attn_in['gate_w'], 'L1_attn_gate_b': _L1_attn_in['gate_b'], 'L1_attn_p_w': _L1_attn_in['p_w'], 'L1_attn_p_b': _L1_attn_in['p_b'], 'L1_attn_out_w': _L1_attn_in['out_w'], 'L1_attn_out_b': _L1_attn_in['out_b'], 'L1_attn_clock_w': _L1_attn_in['clock_w'], 'L1_attn_clock_b': _L1_attn_in['clock_b'], 'L1_attn_ln1_g': _L1_attn_in['ln1_g'], 'L1_attn_ln1_b': _L1_attn_in['ln1_b'], 'L1_attn_ln2_g': _L1_attn_in['ln2_g'], 'L1_attn_ln2_b': _L1_attn_in['ln2_b'], 'L1_attn_mlp_w1': _L1_attn_in['mlp_w1'], 'L1_attn_mlp_b1': _L1_attn_in['mlp_b1'], 'L1_attn_mlp_w2': _L1_attn_in['mlp_w2'], 'L1_attn_mlp_b2': _L1_attn_in['mlp_b2'], 'L1_xattn_Wq': _L1_xattn_in['Wq'], 'L1_xattn_Wk': _L1_xattn_in['Wk'], 'L1_xattn_Wv': _L1_xattn_in['Wv'], 'L1_xattn_Wp': _L1_xattn_in['Wp'], 'L1_xattn_bp': _L1_xattn_in['bp'], 'L1_ffn_W_r': _L1_ffn_in['W_r'], 'L1_ffn_W_k': _L1_ffn_in['W_k'], 'L1_ffn_W_v': _L1_ffn_in['W_v'], 'L1_ffn_mu_r': _L1_ffn_in['mu_r'], 'L1_ffn_mu_k': _L1_ffn_in['mu_k']}

def reference(x, ctx_1024, mask_BxSxS2_ik0, L0_attn_W_Q, L0_attn_W_K, L0_attn_W_V, L0_attn_W_O, L0_xattn_W, L0_xattn_b, L0_ffn_gate_w, L0_ffn_dense_1_w, L0_ffn_dense_1_b, L0_ffn_dense_2_w, L0_ffn_dense_2_b, L1_attn_Wq, L1_attn_Wk, L1_attn_Wv, L1_attn_gate_w, L1_attn_gate_b, L1_attn_p_w, L1_attn_p_b, L1_attn_out_w, L1_attn_out_b, L1_attn_clock_w, L1_attn_clock_b, L1_attn_ln1_g, L1_attn_ln1_b, L1_attn_ln2_g, L1_attn_ln2_b, L1_attn_mlp_w1, L1_attn_mlp_b1, L1_attn_mlp_w2, L1_attn_mlp_b2, L1_xattn_Wq, L1_xattn_Wk, L1_xattn_Wv, L1_xattn_Wp, L1_xattn_bp, L1_ffn_W_r, L1_ffn_W_k, L1_ffn_W_v, L1_ffn_mu_r, L1_ffn_mu_k):
    import jax
    import jax.numpy as jnp

    def _L0_attn_ref(x, W_Q, W_K, W_V, W_O):
        import jax, jax.numpy as jnp
        import numpy as np
        BATCH, SEQ, D_EMBED, N_HEADS, D_HEAD = (1, 512, 256, 16, 64)
        MASK_VAL = 10000000000.0
        q = jnp.einsum('ahe,bce->bach', W_Q, x)
        k = jnp.einsum('ahe,bce->bach', W_K, x)
        v = jnp.einsum('ahe,bce->bach', W_V, x)
        n = x.shape[1]
        scores = jnp.einsum('bach,baCh->bacC', k, q)
        causal = jnp.tril(jnp.ones((n, n), dtype=bool))
        masked = jnp.where(causal, scores, jnp.float32(-MASK_VAL))
        attn = jax.nn.softmax(masked / np.float32(np.sqrt(D_HEAD)), axis=-1)
        z = jnp.einsum('bacC,baCh->bach', attn, v)
        out = jnp.einsum('aeh,bach->bce', W_O, z)
        return out

    def _L0_xattn_ref(query, memories, mask, W, b):
        import jax, jax.numpy as jnp
        import numpy as np
        NEG = -1000000000.0
        q = jnp.einsum('bsd,od->bso', query, W) + b
        add_mask = (1.0 - mask.astype(q.dtype)) * NEG
        attn_logits = jnp.einsum('bqd,bkd->bqk', q, memories) + add_mask
        attn_weights = jax.nn.softmax(attn_logits, axis=-1)
        attn_outputs = jnp.einsum('bqk,bkd->bqd', attn_weights, memories)
        return attn_outputs

    def _L0_ffn_ref(x, gate_w, dense_1_w, dense_1_b, dense_2_w, dense_2_b):
        import jax, jax.numpy as jnp
        import numpy as np
        ALPHA = 1.702
        LIMIT = 9.0
        TOP_K = 2

        def swiglu(x):
            g, v = (x[..., 0::2], x[..., 1::2])
            g = jnp.clip(g, None, LIMIT)
            v = jnp.clip(v, -LIMIT, LIMIT)
            return g * jax.nn.sigmoid(ALPHA * g) * (v + 1)
        B, L, D = x.shape
        xf = x.reshape(B * L, D)
        gate = xf @ gate_w
        weights, sel = jax.lax.top_k(gate, k=TOP_K)
        weights = jax.nn.softmax(weights, axis=-1)
        h = jnp.einsum('ecd,td->tec', dense_1_w, xf) + dense_1_b[None]
        h = swiglu(h)
        y = jnp.einsum('edf,tef->ted', dense_2_w, h) + dense_2_b[None]
        y_sel = jnp.take_along_axis(y, sel[:, :, None], axis=1)
        out = jnp.einsum('tkd,tk->td', y_sel, weights)
        return out.reshape(B, L, D)

    def _L1_attn_ref(x, Wq, Wk, Wv, gate_w, gate_b, p_w, p_b, out_w, out_b, clock_w, clock_b, ln1_g, ln1_b, ln2_g, ln2_b, mlp_w1, mlp_b1, mlp_w2, mlp_b2):
        import math
        import jax, jax.numpy as jnp
        import numpy as np
        D_MODEL = 256
        N_HEAD = 16
        HEAD_DIM = D_MODEL // N_HEAD
        B, T = (2, 512)

        def _layernorm(x, g, b, eps=1e-05):
            mu = jnp.mean(x, axis=-1, keepdims=True)
            var = jnp.mean(jnp.square(x - mu), axis=-1, keepdims=True)
            return (x - mu) * jax.lax.rsqrt(var + eps) * g + b

        def _l2norm(x, eps=1e-12):
            n = jnp.sqrt(jnp.sum(jnp.square(x), axis=-1, keepdims=True))
            return x / jnp.maximum(n, eps)

        def _rope(x, times):
            half = x.shape[-1] // 2
            freqs = jnp.exp(-jnp.arange(half, dtype=x.dtype) * (math.log(10000.0) / half))
            theta = times[:, None] * freqs[None, :]
            cos = jnp.cos(theta)[None, :, None, :]
            sin = jnp.sin(theta)[None, :, None, :]
            xr = x.reshape(*x.shape[:-1], half, 2)
            x1, x2 = (xr[..., 0], xr[..., 1])
            r1 = x1 * cos - x2 * sin
            r2 = x1 * sin + x2 * cos
            return jnp.stack([r1, r2], axis=-1).reshape(x.shape)
        Bx, Tx, D = x.shape
        H, Dh = (N_HEAD, HEAD_DIM)
        residual = x
        xn = _layernorm(x, ln1_g, ln1_b)
        times = jnp.arange(Tx, dtype=x.dtype)
        q = _l2norm((xn @ Wq).reshape(Bx, Tx, H, Dh))
        k = _l2norm((xn @ Wk).reshape(Bx, Tx, H, Dh))
        v = (xn @ Wv).reshape(Bx, Tx, H, Dh)
        clock = jax.nn.softplus(xn @ clock_w + clock_b).reshape(Bx, Tx, H, 1)
        q = _rope(q, times)
        k = _rope(k, times)
        gj = -jax.nn.softplus(xn @ gate_w + gate_b).reshape(Bx, Tx, H, Dh)
        gcp = jnp.exp(jnp.clip(jnp.cumsum(gj, axis=1), -60.0, 50.0))
        q = q * gcp
        k = k / (gcp + 1e-08)
        p = (xn @ p_w + p_b).reshape(Bx, Tx, H, Dh)
        p_max = jnp.max(p, axis=1, keepdims=True)
        p_exp = jnp.exp(p - p_max) * clock
        p_cs = jnp.cumsum(p_exp, axis=1)
        q = q / (p_cs + 1e-08)
        k = k * p_exp
        scores = jnp.einsum('bqhd,bkhd->bhqk', q, k) / math.sqrt(Dh)
        mask = jnp.tril(jnp.ones((Tx, Tx), dtype=bool))
        scores = jnp.where(mask[None, None], scores, -jnp.inf)
        attn = jax.nn.softmax(scores, axis=-1)
        out = jnp.einsum('bhqk,bkhd->bqhd', attn, v).reshape(Bx, Tx, D)
        out = out @ out_w + out_b
        x1 = out + residual
        h = _layernorm(x1, ln2_g, ln2_b)
        h = jax.nn.gelu(h @ mlp_w1 + mlp_b1, approximate=False) @ mlp_w2 + mlp_b2
        return x1 + h

    def _L1_xattn_ref(query_data, key_data, value_data, Wq, Wk, Wv, Wp, bp):
        import jax, jax.numpy as jnp
        import numpy as np
        D_MODEL = 256
        DK = 64
        N_HEADS = D_MODEL // DK
        MASK = True
        B, S, _ = query_data.shape

        def split_heads(x, W):
            return (x @ W.T).reshape(B, -1, N_HEADS, DK).transpose(0, 2, 1, 3)
        q = split_heads(query_data, Wq)
        k = split_heads(key_data, Wk)
        v = split_heads(value_data, Wv)
        scores = jnp.einsum('bhqd,bhkd->bhqk', q, k) / np.sqrt(DK).astype(np.float32)
        if MASK:
            Sq, Sk = (scores.shape[-2], scores.shape[-1])
            causal = jnp.triu(jnp.ones((Sq, Sk), dtype=scores.dtype), k=1) * jnp.float32(-10000000000000.0)
            scores = scores + causal
        attn = jax.nn.softmax(scores, axis=-1)
        out = jnp.einsum('bhqk,bhkd->bhqd', attn, v)
        out = out.transpose(0, 2, 1, 3).reshape(B, S, D_MODEL)
        return out @ Wp.T + bp

    def _L1_ffn_ref(x, W_r, W_k, W_v, mu_r, mu_k):
        import jax, jax.numpy as jnp
        import numpy as np
        DIM = 256

        def _reference_tuple_inner(x, W_r, W_k, W_v, mu_r, mu_k):
            B, T, C = x.shape
            x_prev = jnp.concatenate([jnp.zeros((B, 1, C), x.dtype), x[:, :-1, :]], axis=1)
            xr = mu_r * x + (1.0 - mu_r) * x_prev
            xk = mu_k * x + (1.0 - mu_k) * x_prev
            r = jax.nn.sigmoid(jnp.einsum('btc,dc->btd', xr, W_r))
            k = jnp.einsum('btc,dc->btd', xk, W_k)
            k_act = jnp.square(jax.nn.relu(k))
            out = r * jnp.einsum('btc,dc->btd', k_act, W_v)
            new_state = x[:, -1, :]
            return (out, new_state)
        return _reference_tuple_inner(x, W_r, W_k, W_v, mu_r, mu_k)[0]
    x = _layernorm(x + _L0_attn_ref(x, L0_attn_W_Q, L0_attn_W_K, L0_attn_W_V, L0_attn_W_O), axis=-1)
    x = _layernorm(x + _L0_xattn_ref(x, ctx_1024, mask_BxSxS2_ik0, L0_xattn_W, L0_xattn_b), axis=-1)
    x = _layernorm(x + _L0_ffn_ref(x, L0_ffn_gate_w, L0_ffn_dense_1_w, L0_ffn_dense_1_b, L0_ffn_dense_2_w, L0_ffn_dense_2_b), axis=-1)
    x = _layernorm(x + _L1_attn_ref(x, L1_attn_Wq, L1_attn_Wk, L1_attn_Wv, L1_attn_gate_w, L1_attn_gate_b, L1_attn_p_w, L1_attn_p_b, L1_attn_out_w, L1_attn_out_b, L1_attn_clock_w, L1_attn_clock_b, L1_attn_ln1_g, L1_attn_ln1_b, L1_attn_ln2_g, L1_attn_ln2_b, L1_attn_mlp_w1, L1_attn_mlp_b1, L1_attn_mlp_w2, L1_attn_mlp_b2), axis=-1)
    x = _layernorm(x + _L1_xattn_ref(x, ctx_1024, ctx_1024, L1_xattn_Wq, L1_xattn_Wk, L1_xattn_Wv, L1_xattn_Wp, L1_xattn_bp), axis=-1)
    x = _layernorm(x + _L1_ffn_ref(x, L1_ffn_W_r, L1_ffn_W_k, L1_ffn_W_v, L1_ffn_mu_r, L1_ffn_mu_k), axis=-1)
    return x

_drawn_inputs = setup_inputs


def setup_inputs(seed=0):
    import zlib

    import numpy as np

    out = dict(_drawn_inputs(seed))
    spreads = {'L0_xattn_b': (0.0, 0.1),
     'L0_ffn_dense_1_b': (0.0, 0.1),
     'L0_ffn_dense_2_b': (0.0, 0.1),
     'L1_attn_gate_b': (0.0, 2.0),
     'L1_attn_p_b': (0.0, 2.0),
     'L1_attn_out_b': (0.0, 0.1),
     'L1_attn_clock_b': (0.0, 2.0),
     'L1_attn_ln1_g': (1.0, 0.6),
     'L1_attn_ln1_b': (0.0, 0.8),
     'L1_attn_ln2_g': (1.0, 0.6),
     'L1_attn_ln2_b': (0.0, 0.8),
     'L1_attn_mlp_b1': (0.0, 0.511),
     'L1_attn_mlp_b2': (0.0, 0.1),
     'L1_xattn_bp': (0.0, 0.1)}
    factors = {'L1_attn_Wq': 200.0,
     'L1_attn_Wk': 200.0,
     'L1_attn_gate_w': 200.0,
     'L1_attn_p_w': 200.0,
     'L1_attn_out_w': 2.684,
     'L1_attn_clock_w': 200.0,
     'L1_ffn_mu_r': 6.803}
    for name, (base, spread) in spreads.items():
        noise = np.random.default_rng([zlib.crc32(name.encode()), seed]).standard_normal(out[name].shape)
        drawn = base * np.exp(spread * noise) if base else spread * noise
        out[name] = jnp.asarray(drawn.astype(out[name].dtype))
    for name, factor in factors.items():
        out[name] = (out[name] * factor).astype(out[name].dtype)
    return out
```

```python
import concourse.bass as bass
from concourse import mybir
from contextlib import ExitStack
import numpy as np

F32 = mybir.dt.float32
I32 = mybir.dt.int32
U32 = mybir.dt.uint32
ALU = mybir.AluOpType
ACT = mybir.ActivationFunctionType
AX = mybir.AxisListType

B, S, D = 8, 256, 256
S2 = 120
P = 128
KD = D // P
GB = 2
G = B // GB
GT = GB * S
NT = GT // P
TILES = B * S // P
EPS = 1e-5
H0, DH0 = 16, 64
E0 = H0 * DH0
PAIRS0 = H0 // 2
NE, FF = 8, 512
FC = FF // P
H1, DH1 = 16, 16
M1 = 4 * D
MC = M1 // P
HX, DHX = 4, 64

CAUSAL = P + S


class Memory:

    WORDS = 48 * 1024

    def __init__(self, nc, ctx):
        self.words = ctx.enter_context(nc.sbuf_tensor("words", [P, self.WORDS], F32))
        self.bank = [ctx.enter_context(nc.psum_tensor(f"bank{i}", [P, 512], F32)) for i in range(8)]
        self.mark = 0
        self.nc, self.ctx = nc, ctx
        self.alone = self.sem("alone")

    def sem(self, name):
        return self.ctx.enter_context(self.nc.semaphore(name))

    def take(self, shape, dt=F32):
        n = int(np.prod(shape[1:]))
        assert self.mark + n <= self.WORDS, (shape, self.mark)
        v = cut(self.words, self.mark, shape[1:], shape[0])
        self.mark += n + n % 2
        return v if dt == F32 else v.bitcast(dt)


def cut(region, start, dims, rows=P):
    v = region[0:rows, start:start + int(np.prod(dims))]
    if len(dims) == 1:
        return v
    names = "abcd"[:len(dims)]
    return v.rearrange(f"p ({' '.join(names)}) -> p {' '.join(names)}", **dict(zip(names, dims)))


class Norm:

    def __init__(self, mem, name, y=None, product=True, turned=True):
        self.stats = mem.sem(f"{name}_stats")
        self.rstd = mem.sem(f"{name}_rstd")
        self.normed = mem.sem(f"{name}_normed")
        if product:
            self.product = mem.sem(f"{name}_product")
            self.added = mem.sem(f"{name}_added")
        if turned:
            self.turned = mem.sem(f"{name}_turned")
            self.copied = mem.sem(f"{name}_copied")
        self.y = mem.take([P, NT, D]) if y is None else y
        self.bn = mem.take([P, NT, 6])
        self.mv = mem.take([P, NT, 2])
        self.var = mem.take([P, NT])
        self.inv = mem.take([P, NT])


def norm_tile_stats(dve, g, n, t):
    dve.drain()
    dve.bn_stats(n.bn[:, t, :], n.y[:, t, :])
    dve.drain()
    last = dve.bn_aggr(n.mv[:, t, :], n.bn[:, t, :])
    if t == NT - 1:
        last.then_inc(n.stats, 1)


def norm_rows(dve, g, n, out):
    dve.drain()
    dve.wait_ge(n.rstd, g + 1)
    for t in range(NT):
        dve.tensor_scalar(out(t), n.y[:, t, :], n.mv[:, t, 0:1], n.inv[:, t:t + 1],
                          ALU.subtract, ALU.mult).then_inc(n.normed, 1)


def norm_rstd(pool, g, n, eps, minus_half):
    pool.drain()
    pool.wait_ge(n.stats, g + 1)
    pool.tensor_tensor(n.var[:, :], n.mv[:, :, 1], eps, ALU.add)
    pool.drain()
    pool.tensor_tensor(n.inv[:, :], n.var[:, :], minus_half, ALU.pow).then_inc(n.rstd, 1)


def norm_turn(pe, g, n, rows, banks, ident):
    for t in range(NT):
        pe.wait_ge(n.normed, NT * g + t + 1)
        if t >= 2:
            pe.wait_ge(n.copied, NT * g + t - 1)
        for k in range(KD):
            last = pe.transpose(banks[t % 2][:, k * P:(k + 1) * P], rows(t)[:, k * P:(k + 1) * P], ident)
        last.then_inc(n.turned, 1)


def norm_copy(act, g, n, banks, out):
    for t in range(NT):
        act.wait_ge(n.turned, NT * g + t + 1)
        act.activation(out(t), banks[t % 2][:, 0:D].rearrange("p (k n) -> p k n", k=KD),
                       ACT.Copy).then_inc(n.copied, 1)


def end_of_turn(eng, g, turn, alone, engines=5):
    eng.drain()
    eng.nop().then_inc(turn, 1)
    eng.wait_ge(turn, engines * g + engines)
    eng.sem_inc(alone, 1)




def attention_layers(nc, dram, memory, keep):
    with ExitStack() as ctx:
        sb = memory.take
        bank = memory.bank

        sem = memory.sem
        alone = memory.alone
        wq, wk, wv = (sb([P, KD, E0]) for _ in range(3))
        wo = sb([P, PAIRS0, D])
        wx = sb([P, KD, D])
        bx = sb([P, KD])
        gate_w = sb([P, KD, NE])
        ident, minus_half, eps = sb([P, P]), sb([P, NT]), sb([P, NT])
        mask0 = sb([P, CAUSAL])
        expert = sb([P, NT, NE])
        xg, xt = sb([P, NT, D]), sb([P, KD, GT])
        qt, kt = sb([P, PAIRS0, GT]), sb([P, PAIRS0, GT])
        v = sb([P, NT, E0])
        prob = sb([P, 4, CAUSAL])
        mx, negmax, rowsum, inv = (sb([P, 4, 2]) for _ in range(4))
        probt = sb([P, 2, CAUSAL])
        zt = sb([P, PAIRS0, GT])
        x1, x1t = sb([P, NT, D]), sb([P, KD, GT])
        mem, memt = sb([S2, GB, D]), sb([P, KD, GB, S2])
        maski, maskf = sb([P, NT, S2], I32), sb([P, NT, S2])
        qx = sb([P, KD, GT])
        probx, probxt = sb([P, NT, S2]), sb([S2, NT, P])
        mxx, negx, sumx, invx = (sb([P, NT]) for _ in range(4))
        x2, x2t = sb([P, NT, D]), sb([P, KD, GT])
        score8, top8 = sb([P, NT, NE]), sb([P, NT, 8])
        at8, at8f = sb([P, NT, 8], U32), sb([P, NT, 8])
        gd, ge, gp, gq = (sb([P, NT]) for _ in range(4))
        pick0, pick1 = sb([P, NT, NE]), sb([P, NT, NE])

        weights, loaded, const, turn = sem("a_weights"), sem("a_loaded"), sem("a_const"), sem("a_turn")
        chunk, ev_act, ev_dve = sem("chunk"), sem("ev_act"), sem("ev_dve")
        scores, shifted, exped, probs = sem("scores"), sem("shifted"), sem("exped"), sem("probs")
        tposed, tcopied, heads, zcopied = sem("tposed"), sem("tcopied"), sem("heads"), sem("zcopied")
        xlogit, xshift, xexp, xtp, xtc = (sem(n) for n in ("xlogit", "xshift", "xexp", "xtp", "xtc"))
        gmm, gdiff, gexp, picked = sem("gmm"), sem("gdiff"), sem("gexp"), sem("picked")
        n1, n2 = Norm(memory, "n1"), Norm(memory, "n2")
        HEADS = GB * H0
        QK = 2 * PAIRS0
        VC = NT * (E0 // 512)
        NCH = QK + VC + KD
        HALF = NCH // 2
        block = ctx.enter_context(nc.Block())

        @block.sync
        def _(sp):
            for dst, src in ((wq, dram["wq0"]), (wk, dram["wk0"]), (wv, dram["wv0"]), (wx, dram["wx0"]),
                             (gate_w, dram["gate"])):
                sp.dma_start(dst[:, :, :], src.rearrange("(k p) n -> p k n", p=P)).then_inc(weights, 16)
            sp.dma_start(wo[:, :, :], dram["wo0"].rearrange("(k p) n -> p k n", p=P)).then_inc(weights, 16)
            sp.dma_start(bx[:, :], dram["bx0"]).then_inc(weights, 16)
            with sp.Fori(0, G) as g:
                sp.dma_start(xt[:, :, :], dram["xt"].rearrange("(k p) n -> p k n", p=P)[:, :, bass.ts(g, GT)]).then_inc(loaded, 16)
                sp.dma_start(xg[:, :, :], dram["x"].rearrange("(g t p) n -> g p t n", p=P, t=NT)[g]).then_inc(loaded, 16)
                sp.dma_start(maski[:, :, :], dram["mask"].rearrange("(g t p) n -> g p t n", p=P, t=NT)[g]).then_inc(loaded, 16)
                sp.dma_start(mem[:, :, :], dram["ctx"].rearrange("(g b) s n -> g s b n", b=GB)[g]).then_inc(loaded, 16)
                for b in range(GB):
                    sp.dma_start(memt[:, :, b, :], dram["ctxt"].rearrange("(g b) (k p) s -> g b p k s", b=GB, p=P)[g, b]).then_inc(loaded, 16)
                end_of_turn(sp, g, turn, alone)

        @block.gpsimd
        def _(pool):
            pool.memset(ident[:, :], 0.0)
            pool.memset(mask0[:, :], 0.0)
            pool.memset(minus_half[:, :], -0.5)
            pool.memset(eps[:, :], EPS)
            pool.iota(expert[:, :, :], pattern=[[0, NT], [1, NE]], base=0, channel_multiplier=0,
                      allow_small_or_imprecise_dtypes=True)
            pool.drain()
            pool.affine_select(out=ident[:, :], in_=ident[:, :], compare_op=ALU.not_equal, fill=1.0, base=0,
                               pattern=[[-1, P]], channel_multiplier=1)
            for c in (0, S):
                pool.affine_select(out=mask0[:, c:c + P], in_=mask0[:, c:c + P], compare_op=ALU.is_ge,
                                   fill=-1e10, base=0, pattern=[[-1, P]], channel_multiplier=1)
            pool.drain()
            pool.nop().then_inc(const, 1)
            with pool.Fori(0, G) as g:
                norm_rstd(pool, g, n1, eps[:, :], minus_half[:, :])
                norm_rstd(pool, g, n2, eps[:, :], minus_half[:, :])
                pool.wait_ge(n2.normed, NT * g + NT)
                pool.tensor_copy(keep["x"][:, bass.ts(g, NT), :], x2[:, :, :])
                pool.wait_ge(n2.copied, NT * g + NT)
                pool.tensor_copy(keep["xt"][:, :, bass.ts(g, GT)], x2t[:, :, :])
                pool.wait_ge(picked, g + 1)
                pool.tensor_copy(keep["pick"][:, bass.ts(g, NT), :], pick0[:, :, :])
                end_of_turn(pool, g, turn, alone)

        @block.tensor
        def _(pe):
            def project(g, c, pairs):
                if c >= 4:
                    pe.wait_ge((ev_act, ev_dve)[c % 2], HALF * g + (c - 4) // 2 + 1)
                for i, (w, r) in enumerate(pairs):
                    last = pe.matmul(bank[c % 4][:, :], w, r, start=i == 0, stop=i == len(pairs) - 1)
                last.then_inc(chunk, 1)

            pe.wait_ge(weights, 7 * 16)
            pe.wait_ge(const, 1)
            with pe.Fori(0, G) as g:
                pe.wait_ge(loaded, 96 * g + 96)
                for c in range(QK):
                    w = wq if c < PAIRS0 else wk
                    m = c % PAIRS0
                    project(g, c, [(w[:, k, m * P:(m + 1) * P], xt[:, k, :]) for k in range(KD)])
                for c in range(VC):
                    t, h = c // 2, c % 2
                    project(g, QK + c, [(xt[:, k, t * P:(t + 1) * P], wv[:, k, h * 512:(h + 1) * 512]) for k in range(KD)])
                pe.wait_ge(ev_act, HALF * g + (QK + VC) // 2)
                pe.wait_ge(ev_dve, HALF * g + (QK + VC) // 2)
                for i in range(HEADS + 3):
                    if i < HEADS:
                        b, h = i // H0, i % H0
                        r = slice(DH0 * (h % 2), DH0 * (h % 2) + DH0)
                        if i >= 2:
                            pe.wait_ge(shifted, HEADS * g + i - 1)
                        for t in range(2):
                            last = pe.matmul(bank[i % 2][:, t * P:t * P + P * (t + 1)],
                                             kt[r, h // 2, b * S + t * P:b * S + (t + 1) * P],
                                             qt[r, h // 2, b * S:b * S + P * (t + 1)], start=True, stop=True)
                        last.then_inc(scores, 1)
                    j = i - 2
                    if 0 <= j < HEADS:
                        pe.wait_ge(probs, HEADS * g + j + 1)
                        if j >= 2:
                            pe.wait_ge(tcopied, HEADS * g + j - 1)
                        for n, c in enumerate((0, P, S)):
                            last = pe.transpose(bank[2 + j % 2][:, n * P:(n + 1) * P],
                                                prob[:, j % 4, c:c + P], ident[:, :])
                        last.then_inc(tposed, 1)
                    j = i - 3
                    if 0 <= j < HEADS:
                        b, h = j // H0, j % H0
                        pe.wait_ge(tcopied, HEADS * g + j + 1)
                        if j % 2 == 0 and j >= 4:
                            pe.wait_ge(zcopied, HEADS // 2 * g + j // 2 - 1)
                        o = bank[4 + j // 2 % 2][DH0 * (h % 2):DH0 * (h % 2) + DH0, :]
                        pe.matmul(o[:, 0:S], v[:, 2 * b, h * DH0:(h + 1) * DH0],
                                  probt[:, j % 2, 0:S], start=True, stop=False)
                        pe.matmul(o[:, P:S], v[:, 2 * b + 1, h * DH0:(h + 1) * DH0],
                                  probt[:, j % 2, S:S + P], start=False, stop=True).then_inc(heads, 1)
                pe.wait_ge(zcopied, HEADS // 2 * g + HEADS // 2)
                for t in range(NT):
                    if t >= 2:
                        pe.wait_ge(n1.added, NT * g + t - 1)
                    for m in range(PAIRS0):
                        last = pe.matmul(bank[6 + t % 2][:, 0:D], zt[:, m, t * P:(t + 1) * P], wo[:, m, :],
                                         start=m == 0, stop=m == PAIRS0 - 1)
                    last.then_inc(n1.product, 1)
                norm_turn(pe, g, n1, lambda t: x1[:, t, :], bank[2:4], ident[:, :])
                pe.wait_ge(n1.copied, NT * g + NT)
                for c in range(KD):
                    project(g, QK + VC + c, [(wx[:, k, c * P:(c + 1) * P], x1t[:, k, :]) for k in range(KD)])
                pe.wait_ge(ev_act, HALF * g + HALF)
                pe.wait_ge(ev_dve, HALF * g + HALF)
                for t in range(NT):
                    if t >= 2:
                        pe.wait_ge(xshift, NT * g + t - 1)
                    for k in range(KD):
                        last = pe.matmul(bank[4 + t % 2][:, 0:S2], qx[:, k, t * P:(t + 1) * P],
                                         memt[:, k, t // 2, :], start=k == 0, stop=k == KD - 1)
                    last.then_inc(xlogit, 1)
                for t in range(NT):
                    pe.wait_ge(xexp, NT * g + t + 1)
                    if t >= 2:
                        pe.wait_ge(xtc, NT * g + t - 1)
                    pe.transpose(bank[6 + t % 2][0:S2, 0:P], probx[:, t, :], ident[:, :]).then_inc(xtp, 1)
                for t in range(NT):
                    pe.wait_ge(xtc, NT * g + t + 1)
                    if t >= 2:
                        pe.wait_ge(n2.added, NT * g + t - 1)
                    pe.matmul(bank[t % 2][:, 0:D], probxt[:, t, :], mem[:, t // 2, :],
                              start=True, stop=True).then_inc(n2.product, 1)
                norm_turn(pe, g, n2, lambda t: x2[:, t, :], bank[2:4], ident[:, :])
                for t in range(NT):
                    pe.wait_ge(n2.copied, NT * g + t + 1)
                    for k in range(KD):
                        last = pe.matmul(bank[4][:, t * NE:(t + 1) * NE], x2t[:, k, t * P:(t + 1) * P],
                                         gate_w[:, k, :], start=k == 0, stop=k == KD - 1)
                last.then_inc(gmm, 1)
                end_of_turn(pe, g, turn, alone)

        def target(c):
            if c < QK:
                return (qt if c < PAIRS0 else kt)[:, c % PAIRS0, :]
            c -= QK
            return v[:, c // 2, (c % 2) * 512:(c % 2 + 1) * 512]

        @block.scalar
        def _(act):
            act.wait_ge(weights, 7 * 16)
            with act.Fori(0, G) as g:
                for c in range(0, QK + VC, 2):
                    act.wait_ge(chunk, NCH * g + c + 1)
                    act.activation(target(c), bank[c % 4][:, :], ACT.Copy).then_inc(ev_act, 1)
                for i in range(HEADS + 2):
                    if i < HEADS:
                        act.wait_ge(shifted, HEADS * g + i + 1)
                        for t in range(2):
                            c = slice(t * P, t * P + P * (t + 1))
                            last = act.activation(prob[:, i % 4, c], prob[:, i % 4, c], ACT.Exp,
                                                  bias=negmax[:, i % 4, t:t + 1], scale=DH0 ** -0.5,
                                                  accum_out=rowsum[:, i % 4, t:t + 1])
                        last.then_inc(exped, 1)
                    j = i - 2
                    if 0 <= j < HEADS:
                        act.wait_ge(tposed, HEADS * g + j + 1)
                        if j >= 2:
                            act.wait_ge(heads, HEADS * g + j - 1)
                        act.activation(probt[:, j % 2, :], bank[2 + j % 2][:, 0:CAUSAL], ACT.Copy).then_inc(tcopied, 1)
                norm_copy(act, g, n1, bank[2:4], lambda t: x1t[:, :, t * P:(t + 1) * P])
                act.wait_ge(chunk, NCH * g + QK + VC + 1)
                act.activation(qx[:, 0, :], bank[(QK + VC) % 4][:, :], ACT.Identity, bias=bx[:, 0:1]).then_inc(ev_act, 1)
                for t in range(NT):
                    act.wait_ge(xshift, NT * g + t + 1)
                    act.activation(probx[:, t, :], probx[:, t, :], ACT.Exp, bias=negx[:, t:t + 1],
                                   accum_out=sumx[:, t:t + 1]).then_inc(xexp, 1)
                for t in range(NT):
                    act.wait_ge(xtp, NT * g + t + 1)
                    act.activation(probxt[:, t, :], bank[6 + t % 2][0:S2, 0:P], ACT.Copy).then_inc(xtc, 1)
                norm_copy(act, g, n2, bank[2:4], lambda t: x2t[:, :, t * P:(t + 1) * P])
                act.wait_ge(gdiff, g + 1)
                act.activation(ge[:, :], gd[:, :], ACT.Exp).then_inc(gexp, 1)
                end_of_turn(act, g, turn, alone)

        @block.vector
        def _(dve):
            dve.wait_ge(weights, 7 * 16)
            dve.wait_ge(const, 1)
            with dve.Fori(0, G) as g:
                for c in range(1, QK + VC, 2):
                    dve.wait_ge(chunk, NCH * g + c + 1)
                    dve.tensor_copy(target(c), bank[c % 4][:, :]).then_inc(ev_dve, 1)
                dve.wait_ge(loaded, 96 * g + 96)
                dve.tensor_scalar(maskf[:, :, :], maski[:, :, :], -1.0, 1e9, ALU.add, ALU.mult)
                for i in range(HEADS + 4):
                    if i < HEADS:
                        dve.wait_ge(scores, HEADS * g + i + 1)
                        if i >= 4:
                            dve.wait_ge(tposed, HEADS * g + i - 3)
                        dve.sem_inc(alone, 1)
                        for t in range(2):
                            c = slice(t * P, t * P + P * (t + 1))
                            dve.tensor_tensor_reduce(out=prob[:, i % 4, c], in0=bank[i % 2][:, c], in1=mask0[:, c],
                                                     scale=1.0, scalar=-3e38, op0=ALU.add, op1=ALU.max,
                                                     accum_out=mx[:, i % 4, t:t + 1])
                        dve.drain()
                        dve.tensor_scalar(negmax[:, i % 4, :], mx[:, i % 4, :], -DH0 ** -0.5, None,
                                          ALU.mult).then_inc(shifted, 1)
                    j = i - 1
                    if 0 <= j < HEADS:
                        dve.wait_ge(exped, HEADS * g + j + 1)
                        dve.reciprocal(inv[:, j % 4, :], rowsum[:, j % 4, :])
                        dve.drain()
                        for t in range(2):
                            c = slice(t * P, t * P + P * (t + 1))
                            last = dve.tensor_scalar(prob[:, j % 4, c], prob[:, j % 4, c], inv[:, j % 4, t:t + 1],
                                                     None, ALU.mult)
                        last.then_inc(probs, 1)
                    j = i - 4
                    if 0 <= j < HEADS and j % 2:
                        b, h = j // H0, j % H0
                        dve.wait_ge(heads, HEADS * g + j + 1)
                        dve.tensor_copy(zt[:, h // 2, b * S:(b + 1) * S], bank[4 + j // 2 % 2][:, 0:S]).then_inc(zcopied, 1)
                for t in range(NT):
                    dve.wait_ge(n1.product, NT * g + t + 1)
                    dve.tensor_tensor(n1.y[:, t, :], bank[6 + t % 2][:, 0:D], xg[:, t, :], ALU.add).then_inc(n1.added, 1)
                    norm_tile_stats(dve, g, n1, t)
                norm_rows(dve, g, n1, lambda t: x1[:, t, :])
                dve.wait_ge(chunk, NCH * g + NCH)
                dve.tensor_scalar(qx[:, 1, :], bank[(NCH - 1) % 4][:, :], bx[:, 1:2], None, ALU.add).then_inc(ev_dve, 1)
                for t in range(NT):
                    dve.drain()
                    dve.wait_ge(xlogit, NT * g + t + 1)
                    dve.sem_inc(alone, 1)
                    dve.tensor_tensor_reduce(out=probx[:, t, :], in0=bank[4 + t % 2][:, 0:S2], in1=maskf[:, t, :],
                                             scale=1.0, scalar=-3e38, op0=ALU.add, op1=ALU.max, accum_out=mxx[:, t:t + 1])
                    dve.drain()
                    dve.tensor_scalar(negx[:, t:t + 1], mxx[:, t:t + 1], -1.0, None, ALU.mult).then_inc(xshift, 1)
                dve.wait_ge(xexp, NT * g + NT)
                dve.reciprocal(invx[:, :], sumx[:, :])
                dve.drain()
                for t in range(NT):
                    dve.wait_ge(n2.product, NT * g + t + 1)
                    dve.scalar_tensor_tensor(n2.y[:, t, :], bank[t % 2][:, 0:D], invx[:, t:t + 1], x1[:, t, :],
                                             ALU.mult, ALU.add).then_inc(n2.added, 1)
                    norm_tile_stats(dve, g, n2, t)
                norm_rows(dve, g, n2, lambda t: x2[:, t, :])
                dve.wait_ge(gmm, g + 1)
                dve.tensor_copy(score8[:, :, :], bank[4][:, 0:NT * NE].rearrange("p (t e) -> p t e", t=NT))
                dve.drain()
                for t in range(NT):
                    dve.max(top8[:, t, :], score8[:, t, :])
                dve.drain()
                for t in range(NT):
                    dve.max_index(at8[:, t, :], top8[:, t, :], score8[:, t, :])
                dve.tensor_tensor(gd[:, :], top8[:, :, 1], top8[:, :, 0], ALU.subtract).then_inc(gdiff, 1)
                dve.drain()
                dve.tensor_copy(at8f[:, :, :], at8[:, :, :])
                dve.wait_ge(gexp, g + 1)
                dve.tensor_scalar(gq[:, :], ge[:, :], 1.0, None, ALU.add)
                dve.drain()
                dve.reciprocal(gp[:, :], gq[:, :])
                dve.drain()
                dve.tensor_tensor(gq[:, :], gp[:, :], ge[:, :], ALU.mult)
                dve.drain()
                for t in range(NT):
                    dve.tensor_scalar(pick0[:, t, :], expert[:, t, :], at8f[:, t, 0:1], gp[:, t:t + 1], ALU.is_equal, ALU.mult)
                    dve.tensor_scalar(pick1[:, t, :], expert[:, t, :], at8f[:, t, 1:2], gq[:, t:t + 1], ALU.is_equal, ALU.mult)
                dve.drain()
                dve.tensor_tensor(pick0[:, :, :], pick0[:, :, :], pick1[:, :, :], ALU.add).then_inc(picked, 1)
                end_of_turn(dve, g, turn, alone)


def expert_layer(nc, dram, memory, keep):
    with ExitStack() as ctx:
        sb = memory.take
        bank = memory.bank

        sem = memory.sem
        alone = memory.alone
        EP = 2
        w1 = sb([P, EP, KD, 2 * FF])
        w2 = sb([P, EP, FC, D])
        b1 = sb([P, NE, 2 * FC])
        b2 = sb([NE, D])
        ident = sb([P, P])
        pickt = sb([NE, TILES, P])
        gc, vc, sg = sb([P, 2, GT]), sb([P, 2, GT]), sb([P, 2, GT])
        ht = sb([P, 2, FC, GT])
        biases, const = sem("e_biases"), sem("e_const")
        wl = [sem(f"e_weights{s}") for s in range(EP)]
        ptp, ptc, bmm, badd = sem("ptp"), sem("ptc"), sem("bmm"), sem("badd")
        up, clipped, gated, mixed, hidden, down, summed = (sem(n) for n in ("up", "clipped", "gated", "mixed", "hidden", "down", "summed"))
        turn = sem("e_turn")
        ITEMS = EP * G
        UPS = ITEMS * FC
        DOWNS = ITEMS * NT
        block = ctx.enter_context(nc.Block())

        def load(sp, e, s):
            sp.dma_start(w1[:, s, :, :], dram["w1"].rearrange("e (k p) n -> e p k n", p=P)[e]).then_inc(wl[s], 16)
            sp.dma_start(w2[:, s, :, :], dram["w2"].rearrange("e (k p) n -> e p k n", p=P)[e]).then_inc(wl[s], 16)

        def summed_tile(dve, ep, m):
            q, t = m // NT, m % NT
            dve.drain()
            dve.wait_ge(down, DOWNS * ep + m + 1)
            tile = q % G * NT + t
            dve.scalar_tensor_tensor(keep["x"][:, tile, :], bank[4 + m % 4][:, 0:D],
                                     keep["pick"][:, tile, bass.ds(EP * ep + q // G, 1)], keep["x"][:, tile, :],
                                     ALU.mult, ALU.add).then_inc(summed, 1)

        @block.sync
        def _(sp):
            sp.dma_start(b2[:, :], dram["b2"]).then_inc(biases, 16)
            sp.dma_start(b1[:, :, :], dram["b1"]).then_inc(biases, 16)
            for s in range(EP):
                load(sp, s, s)
            with sp.Fori(0, NE // EP - 1) as ep:
                for s in range(EP):
                    sp.wait_ge(down, DOWNS * ep + (s + 1) * G * NT)
                    load(sp, EP * ep + EP + s, s)

        @block.gpsimd
        def _(pool):
            pool.memset(ident[:, :], 0.0)
            pool.drain()
            pool.affine_select(out=ident[:, :], in_=ident[:, :], compare_op=ALU.not_equal, fill=1.0, base=0,
                               pattern=[[-1, P]], channel_multiplier=1)
            pool.drain()
            pool.nop().then_inc(const, 1)
            with pool.Fori(0, NE // EP) as ep:
                for n in range(UPS):
                    pool.wait_ge(gated, UPS * ep + n + 1)
                    pool.tensor_tensor(sg[:, n % 2, :], gc[:, n % 2, :], sg[:, n % 2, :], ALU.mult).then_inc(mixed, 1)
                end_of_turn(pool, ep, turn, alone, 4)

        @block.tensor
        def _(pe):
            pe.wait_ge(const, 1)
            pe.wait_ge(biases, 32)
            for t in range(TILES):
                if t >= 2:
                    pe.wait_ge(ptc, t - 1)
                pe.transpose(bank[t % 2][0:NE, 0:P], keep["pick"][:, t, :], ident[:, :]).then_inc(ptp, 1)
            for t in range(TILES):
                pe.wait_ge(ptc, t + 1)
                if t >= 2:
                    pe.wait_ge(badd, t - 1)
                pe.matmul(bank[2 + t % 2][:, 0:D], pickt[:, t, :], b2[:, :], start=True, stop=True).then_inc(bmm, 1)
            pe.wait_ge(badd, TILES)
            with pe.Fori(0, NE // EP) as ep:
                for u in range(ITEMS + 1):
                    s, gi = u // G, u % G
                    if u < ITEMS:
                        if gi == 0:
                            pe.wait_ge(wl[s], 32 * ep + 32)
                        for fc in range(FC):
                            n = u * FC + fc
                            if n >= 2:
                                pe.wait_ge(clipped, UPS * ep + n - 1)
                            for half in range(2):
                                for k in range(KD):
                                    c = half * FF + fc * P
                                    last = pe.matmul(bank[2 * (n % 2) + half][:, :], w1[:, s, k, c:c + P],
                                                     keep["xt"][:, k, gi * GT:(gi + 1) * GT],
                                                     start=k == 0, stop=k == KD - 1)
                            last.then_inc(up, 1)
                    if u >= 1:
                        q = u - 1
                        pe.wait_ge(hidden, UPS * ep + (q + 1) * FC)
                        for t in range(NT):
                            m = q * NT + t
                            if m >= 4:
                                pe.wait_ge(summed, DOWNS * ep + m - 3)
                            for k in range(FC):
                                last = pe.matmul(bank[4 + m % 4][:, 0:D], ht[:, q % 2, k, t * P:(t + 1) * P],
                                                 w2[:, q // G, k, :], start=k == 0, stop=k == FC - 1)
                            last.then_inc(down, 1)
                end_of_turn(pe, ep, turn, alone, 4)

        @block.scalar
        def _(act):
            for t in range(TILES):
                act.wait_ge(ptp, t + 1)
                act.activation(pickt[:, t, :], bank[t % 2][0:NE, 0:P], ACT.Copy).then_inc(ptc, 1)
            with act.Fori(0, NE // EP) as ep:
                for n in range(UPS):
                    act.wait_ge(clipped, UPS * ep + n + 1)
                    act.activation(sg[:, n % 2, :], gc[:, n % 2, :], ACT.Sigmoid, scale=1.702).then_inc(gated, 1)
                end_of_turn(act, ep, turn, alone, 4)

        @block.vector
        def _(dve):
            for t in range(TILES):
                dve.wait_ge(bmm, t + 1)
                dve.tensor_tensor(keep["x"][:, t, :], bank[2 + t % 2][:, 0:D], keep["x"][:, t, :], ALU.add).then_inc(badd, 1)
            with dve.Fori(0, NE // EP) as ep:
                def finish(n):
                    dve.wait_ge(mixed, UPS * ep + n + 1)
                    dve.tensor_tensor(ht[:, n // FC % 2, n % FC, :], sg[:, n % 2, :], vc[:, n % 2, :],
                                      ALU.mult).then_inc(hidden, 1)

                for u in range(ITEMS + 1):
                    s, gi = u // G, u % G
                    e = EP * ep + s
                    for fc in range(FC):
                        n = u * FC + fc
                        if u < ITEMS:
                            dve.drain()
                            dve.wait_ge(up, UPS * ep + n + 1)
                            dve.tensor_scalar(gc[:, n % 2, :], bank[2 * (n % 2)][:, :], b1[:, bass.ds(e, 1), fc], 9.0,
                                              ALU.add, ALU.min)
                            dve.tensor_scalar(vc[:, n % 2, :], bank[2 * (n % 2) + 1][:, :], b1[:, bass.ds(e, 1), FC + fc],
                                              9.0, ALU.add, ALU.min).then_inc(clipped, 1)
                            dve.drain()
                            dve.tensor_scalar(vc[:, n % 2, :], vc[:, n % 2, :], -9.0, 1.0, ALU.max, ALU.add)
                        if 1 <= n <= UPS:
                            dve.drain()
                            finish(n - 1)
                        m = (u - 1) * NT + fc - 1
                        if 0 <= m < DOWNS:
                            summed_tile(dve, ep, m)
                summed_tile(dve, ep, DOWNS - 1)
                end_of_turn(dve, ep, turn, alone, 4)


def last_layers(nc, dram, memory, keep):
    with ExitStack() as ctx:
        sb = memory.take
        bank = memory.bank

        sem = memory.sem
        alone = memory.alone
        wqk = sb([P, KD, 2 * D])
        wv1, wgate, wpp, wclock, wout = (sb([P, KD, D]) for _ in range(5))
        wm1, wm2 = sb([P, KD, M1]), sb([P, MC, D])
        wxq, wxk, wxv, wxp = (sb([P, KD, D]) for _ in range(4))
        wr, wk2, wv2 = (sb([P, KD, D]) for _ in range(3))
        bm1 = sb([P, MC])
        cols = sb([P, 9, KD])
        BP, BCLK, BGATE, G1, B1, G2, B2, MUR, MUK = range(9)
        unmu = sb([P, 2, KD])
        brow = sb([P, 3, D])
        rope = sb([P, 2, 2 * DH1])
        parity = sb([P, 2])
        ident, minus_half, eps = sb([P, P]), sb([P, P]), sb([P, NT])
        ones = sb([P, S])
        mask1 = sb([P, CAUSAL])
        maskx = sb([P, 2, HX * S2])
        va = sb([P, NT, H1, 32])
        qf, kf = sb([P, KD, GT]), sb([P, KD, GT])
        qt, kt = sb([P, KD, GT]), sb([P, 2, KD, GT])
        x3, xn, xnt, xb = sb([P, NT, D]), sb([P, NT, D]), sb([P, KD, GT]), sb([P, NT, D])
        ya, yb = sb([P, NT, D]), sb([P, NT, D])
        ss, rn = sb([P, NT * 32]), sb([P, NT * 32])
        pmax, rden = sb([P, KD * GB]), sb([P, NT, H1])
        xmax, xsum, xinv = (sb([P, NT, HX]) for _ in range(3))
        memt = sb([P, KD, GB * S2])
        region1 = sb([P, 9400])
        region2 = sb([P, 7168])

        fm = cut(region1, 0, (6, GT))
        ee = cut(region1, 3072, (4, GT))
        uu = cut(region1, 5120, (4, GT))
        dd = cut(region1, 7168, (2, GT))
        m1t = cut(region1, 0, (MC, GT))
        sm = cut(region1, 0, (NT, HX * S2))
        pxt = cut(region1, 1920, (GB, HX, S), S2)
        zxt, qxt = cut(region1, 4096, (KD, GT)), cut(region1, 5120, (KD, GT))
        kxt, vx = cut(region1, 6144, (KD, GB * S2)), cut(region1, 6624, (GB, D), S2)
        xr, xk, rs, rl = (cut(region1, 1024 * i, (2, 512)) for i in range(4))
        rs = cut(region1, 2048, (NT, D))
        shift, ka = cut(region1, 4096, (KD, GT)), cut(region1, 5120, (KD, GT))
        x5 = cut(region1, 7168, (NT, D))
        x5t = cut(region1, 8192, (KD, GB, S + 1))
        xo = xb
        sq, qn = cut(region2, 0, (2, 512)), cut(region2, 1024, (NT, 512))
        ra, rb = cut(region2, 3072, (NT, 512)), cut(region2, 5120, (NT, 512))
        es, ut = cut(region2, 0, (4, CAUSAL)), cut(region2, 1536, (4, GT))
        og, ogt = cut(region2, 3584, (NT, D)), cut(region2, 4608, (KD, GT))
        h5, h5t, x4, x4t = xn, xnt, x3, xnt

        weights, rows, loaded, const, turn, stored = (sem(f"l_{n}") for n in ("weights", "rows", "loaded", "const", "turn", "stored"))
        qkmm, vmm, vcop, fmm, fmread, sqd, sqred, ssready, rnr = (sem(n) for n in ("qkmm", "vmm", "vcop", "fmm", "fmread", "sqd", "sqred", "ssready", "rnr"))
        qnr, rar, roped, eready, uready, lready, npm, pexp, clr, gcr = (sem(n) for n in ("qnr", "rar", "roped", "eready", "uready", "lready", "npm", "pexp", "clr", "gcr"))
        qktp, qkt, s1, s1m, s1e, av1, utc, ttp, ogr, ogtp, ogc = (sem(n) for n in ("qktp", "qkt", "s1", "s1m", "s1e", "av1", "utc", "ttp", "ogr", "ogtp", "ogc"))
        biased, m1mm, m1g = (sem(n) for n in ("biased", "m1mm", "m1g"))
        xq, xqr, xkm, xkr, xvm, xvr, xs, xsr, xsub, xe, xp, xtp, xtc, xav, xz = (sem("l_" + n) for n in (
            "xq", "xqr", "xkm", "xkr", "xvm", "xvr", "xs", "xsr", "xsub", "xe", "xp", "xtp", "xtc", "xav", "xz"))
        mixk, mixr, kmm, relu, kact, rmm, rsig = (sem(n) for n in ("mixk", "mixr", "kmm", "relu", "kact", "rmm", "rsig"))
        n3, n4 = Norm(memory, "n3", ya, product=False, turned=False), Norm(memory, "n4", x3, product=False)
        n5, n6, n7 = (Norm(memory, n, y) for n, y in (("n5", yb), ("n6", ya), ("n7", yb)))
        n8 = Norm(memory, "n8", ya, turned=False)
        HEADS = GB * H1
        NW, NR = 17, 3
        block = ctx.enter_context(nc.Block())

        def tok(t):
            return slice(t * P, (t + 1) * P)

        @block.sync
        def _(sp):
            for dst, src in ((wqk, "wqk"), (wv1, "wv1"), (wgate, "wgate"), (wpp, "wpp"), (wclock, "wclock"), (wout, "wout"),
                             (wm1, "wm1"), (wm2, "wm2"), (wxq, "wxq"), (wxk, "wxk"), (wxv, "wxv"), (wxp, "wxp"),
                             (wr, "wr"), (wk2, "wk2"), (wv2, "wv2")):
                sp.dma_start(dst[:, :, :], dram[src].rearrange("(k p) n -> p k n", p=P)).then_inc(weights, 16)
            sp.dma_start(bm1[:, :], dram["bm1"]).then_inc(weights, 16)
            sp.dma_start(cols[:, :, :], dram["cols"]).then_inc(weights, 16)
            sp.dma_start(rope[:, :, :], dram["rope"]).then_inc(rows, 16)
            sp.dma_start(parity[:, :], dram["parity"]).then_inc(rows, 16)
            sp.dma_start(brow[:, :, :], dram["rows"].rearrange("(o r) n -> o r n", o=1).to_broadcast([P, 3, D])).then_inc(rows, 16)
            with sp.Fori(0, G) as g:
                for b in range(GB):
                    sp.dma_start(memt[:, :, b * S2:(b + 1) * S2], dram["ctxt"].rearrange("(g b) (k p) s -> g b p k s", b=GB, p=P)[g, b]).then_inc(loaded, 16)
                sp.wait_ge(n8.normed, NT * g + NT)
                sp.dma_start(dram["out"].rearrange("(g t p) n -> g p t n", p=P, t=NT)[g], xo[:, :, :]).then_inc(stored, 16)
                sp.wait_ge(stored, 16 * g + 16)
                sp.sem_inc(alone, 1)
                end_of_turn(sp, g, turn, alone)

        @block.gpsimd
        def _(pool):
            pool.memset(ident[:, :], 0.0)
            pool.memset(minus_half[:, :], -0.5)
            pool.memset(eps[:, :], EPS)
            pool.memset(ones[:, :], 1.0)
            pool.memset(mask1[:, :], 3e38)
            pool.memset(maskx[:, :, :], 0.0)
            pool.memset(va[:, :, :, :], 0.0)
            pool.drain()
            pool.memset(va[:, :, :, DH1:DH1 + 1], 1.0)
            pool.affine_select(out=ident[:, :], in_=ident[:, :], compare_op=ALU.not_equal, fill=1.0, base=0,
                               pattern=[[-1, P]], channel_multiplier=1)
            for c in (0, S):
                pool.affine_select(out=mask1[:, c:c + P], in_=mask1[:, c:c + P], compare_op=ALU.is_ge,
                                   fill=-1e30, base=0, pattern=[[1, P]], channel_multiplier=-1)
            for h in range(HX):
                mh = maskx[:, 0, h * S2:(h + 1) * S2]
                pool.affine_select(out=mh, in_=mh, compare_op=ALU.is_ge, fill=-8e13, base=0,
                                   pattern=[[-1, S2]], channel_multiplier=1)
            pool.drain()
            pool.nop().then_inc(const, 1)
            pool.wait_ge(rows, NR * 16)

            def add_rows(g, src, r):
                for t in range(NT):
                    last = pool.tensor_tensor(xb[:, t, :], src[:, t, :], brow[:, r, :], ALU.add)
                return last

            with pool.Fori(0, G) as g:
                norm_rstd(pool, g, n3, eps[:, :], minus_half[:, 0:NT])
                norm_rstd(pool, g, n4, eps[:, :], minus_half[:, 0:NT])
                pool.wait_ge(n3.normed, NT * g + NT)
                add_rows(g, x3, 0).then_inc(biased, 1)
                pool.wait_ge(ssready, g + 1)
                pool.tensor_tensor(rn[:, :], ss[:, :], minus_half[:, :], ALU.pow).then_inc(rnr, 1)
                for t in range(NT):
                    pool.wait_ge(qnr, NT * g + t + 1)
                    pool.tensor_tensor(ra[:, t, :].rearrange("p (h d) -> p h d", d=DH1),
                                       qn[:, t, :].rearrange("p (h d) -> p h d", d=DH1),
                                       rope[:, t % 2:t % 2 + 1, 0:DH1].to_broadcast([P, 32, DH1]), ALU.mult).then_inc(rar, 1)
                norm_rstd(pool, g, n5, eps[:, :], minus_half[:, 0:NT])
                pool.drain()
                add_rows(g, x3, 1)
                pool.drain()
                pool.tensor_tensor(xb[:, :, :], xb[:, :, :], yb[:, :, :], ALU.add).then_inc(biased, 1)
                norm_rstd(pool, g, n6, eps[:, :], minus_half[:, 0:NT])
                pool.drain()
                pool.wait_ge(n6.normed, NT * g + NT)
                add_rows(g, x4, 2).then_inc(biased, 1)
                norm_rstd(pool, g, n7, eps[:, :], minus_half[:, 0:NT])
                norm_rstd(pool, g, n8, eps[:, :], minus_half[:, 0:NT])
                pool.wait_ge(stored, 16 * g + 16)
                pool.sem_inc(alone, 1)
                end_of_turn(pool, g, turn, alone)

        @block.tensor
        def _(pe):
            def product(out, pairs):
                for i, (w, r) in enumerate(pairs):
                    last = pe.matmul(out, w, r, start=i == 0, stop=i == len(pairs) - 1)
                return last

            pe.wait_ge(weights, NW * 16)
            pe.wait_ge(const, 1)
            with pe.Fori(0, G) as g:
                norm_turn(pe, g, n4, lambda t: xn[:, t, :], bank[6:8], ident[:, :])
                for t in range(NT):
                    pe.wait_ge(n4.copied, NT * g + t + 1)
                    product(bank[t][:, :], [(xnt[:, k, tok(t)], wqk[:, k, :]) for k in range(KD)]).then_inc(qkmm, 1)
                for c in range(6):
                    if c >= 2:
                        pe.wait_ge(fmread, 6 * g + c - 1)
                    w = (wpp, wclock, wgate)[c // 2]
                    product(bank[6 + c % 2][:, :], [(w[:, k, tok(c % 2)], xnt[:, k, :]) for k in range(KD)]).then_inc(fmm, 1)
                for t in range(NT):
                    if t >= 2:
                        pe.wait_ge(vcop, NT * g + t - 1)
                    product(bank[4 + t % 2][:, 0:D], [(xnt[:, k, tok(t)], wv1[:, k, :]) for k in range(KD)]).then_inc(vmm, 1)
                for t in range(NT):
                    pe.wait_ge(roped, NT * g + t + 1)
                    for c in range(4):
                        last = pe.transpose(bank[t][:, tok(c)], rb[:, t, tok(c)], ident[:, :])
                    last.then_inc(qktp, 1)
                pe.wait_ge(qkt, NT * g + NT)
                for i in range(HEADS + 2):
                    if i < HEADS:
                        b, h = i // H1, i % H1
                        m, r = h // 8, slice(32 * (h % 8 // 2), 32 * (h % 8 // 2) + 32)
                        if i >= 2:
                            pe.wait_ge(s1m, HEADS * g + i - 1)
                        pe.matmul(bank[i % 2][:, 0:S], kt[r, h % 2, m, b * S:b * S + P],
                                  qt[r, m, b * S:(b + 1) * S], start=True, stop=True)
                        pe.matmul(bank[i % 2][:, S:S + P], kt[r, h % 2, m, b * S + P:(b + 1) * S],
                                  qt[r, m, b * S + P:(b + 1) * S], start=True, stop=True).then_inc(s1, 1)
                    j = i - 2
                    if j >= 0:
                        b, h = j // H1, j % H1
                        pe.wait_ge(s1e, HEADS * g + j + 1)
                        if j == 0:
                            pe.wait_ge(vcop, NT * g + NT)
                        if j % 4 == 0 and j >= 8:
                            pe.wait_ge(utc, HEADS // 4 * g + j // 4 - 1)
                        o = bank[4 + j // 4 % 2][32 * (h % 4):32 * (h % 4) + 32, :]
                        pe.matmul(o[:, 0:S], va[:, 2 * b, h, :], es[:, j % 4, 0:S], start=True, stop=False)
                        pe.matmul(o[:, P:S], va[:, 2 * b + 1, h, :], es[:, j % 4, S:S + P],
                                  start=False, stop=True).then_inc(av1, 1)
                pe.wait_ge(utc, HEADS // 4 * (g + 1))
                for t in range(NT + 1):
                    if t < NT:
                        if t >= 2:
                            pe.wait_ge(ogr, NT * g + t - 1)
                        for c in range(4):
                            last = pe.transpose(bank[2 + t % 2][:, tok(c)], ut[:, c, tok(t)], ident[:, :])
                        last.then_inc(ttp, 1)
                    if t >= 1:
                        j = t - 1
                        pe.wait_ge(ogr, NT * g + j + 1)
                        if j >= 2:
                            pe.wait_ge(ogc, NT * g + j - 1)
                        for k in range(KD):
                            last = pe.transpose(bank[6 + j % 2][:, tok(k)], og[:, j, tok(k)], ident[:, :])
                        last.then_inc(ogtp, 1)
                for t in range(NT):
                    pe.wait_ge(ogc, NT * g + t + 1)
                    if t >= 2:
                        pe.wait_ge(n5.added, NT * g + t - 1)
                    product(bank[4 + t % 2][:, 0:D], [(ogt[:, k, tok(t)], wout[:, k, :]) for k in range(KD)]).then_inc(n5.product, 1)
                norm_turn(pe, g, n5, lambda t: h5[:, t, :], bank[2:4], ident[:, :])
                pe.wait_ge(n5.copied, NT * g + NT)
                for c in range(MC):
                    if c >= 4:
                        pe.wait_ge(m1g, MC * g + c - 3)
                    product(bank[(0, 1, 4, 5)[c % 4]][:, :], [(wm1[:, k, tok(c)], h5t[:, k, :]) for k in range(KD)]).then_inc(m1mm, 1)
                pe.wait_ge(m1g, MC * g + MC)
                for t in range(NT):
                    if t >= 2:
                        pe.wait_ge(n6.added, NT * g + t - 1)
                    product(bank[6 + t % 2][:, 0:D], [(m1t[:, k, tok(t)], wm2[:, k, :]) for k in range(MC)]).then_inc(n6.product, 1)
                pe.wait_ge(loaded, 32 * g + 32)
                for c in range(KD):
                    product(bank[4 + c][:, 0:GB * S2], [(wxk[:, k, tok(c)], memt[:, k, :]) for k in range(KD)]).then_inc(xkm, 1)
                norm_turn(pe, g, n6, lambda t: x4[:, t, :], bank[2:4], ident[:, :])
                for b in range(GB):
                    product(bank[6 + b][0:S2, 0:D], [(memt[:, k, b * S2:(b + 1) * S2], wxv[:, k, :]) for k in range(KD)]).then_inc(xvm, 1)
                pe.wait_ge(n6.copied, NT * g + NT)
                for c in range(KD):
                    product(bank[c][:, :], [(wxq[:, k, tok(c)], x4t[:, k, :]) for k in range(KD)]).then_inc(xq, 1)
                pe.wait_ge(xqr, KD * g + KD)
                pe.wait_ge(xkr, KD * g + KD)
                for t in range(NT + 1):
                    if t < NT:
                        if t >= 2:
                            pe.wait_ge(xsr, NT * g + t - 1)
                        for h in range(HX):
                            r = slice(DHX * (h % 2), DHX * (h % 2) + DHX)
                            last = pe.matmul(bank[t % 2 + 2 * (h % 2)][:, h // 2 * S2:(h // 2 + 1) * S2], qxt[r, h // 2, tok(t)],
                                             kxt[r, h // 2, t // 2 * S2:(t // 2 + 1) * S2], start=True, stop=True)
                        last.then_inc(xs, 1)
                    if t >= 1:
                        j = t - 1
                        pe.wait_ge(xp, NT * g + j + 1)
                        if j >= 2:
                            pe.wait_ge(xtc, NT * g + j - 1)
                        for h in range(HX):
                            last = pe.transpose(bank[4 + j % 2][0:S2, tok(h)], sm[:, j, h * S2:(h + 1) * S2], ident[:, :])
                        last.then_inc(xtp, 1)
                pe.wait_ge(xtc, NT * g + NT)
                pe.wait_ge(xvr, GB * g + GB)
                for q in range(GB * KD):
                    b, m = q // KD, q % KD
                    if q >= 2:
                        pe.wait_ge(xz, 4 * g + q - 1)
                    for hh in range(2):
                        h = 2 * m + hh
                        last = pe.matmul(bank[6 + q % 2][DHX * hh:DHX * (hh + 1), 0:S], vx[:, b, h * DHX:(h + 1) * DHX],
                                         pxt[:, b, h, :], start=True, stop=True)
                    last.then_inc(xav, 1)
                pe.wait_ge(xz, 4 * g + 4)
                for t in range(NT):
                    if t >= 2:
                        pe.wait_ge(n7.added, NT * g + t - 1)
                    product(bank[t % 2][:, 0:D], [(zxt[:, k, tok(t)], wxp[:, k, :]) for k in range(KD)]).then_inc(n7.product, 1)
                norm_turn(pe, g, n7, lambda t: x5[:, t, :], bank[2:4], ident[:, :])
                pe.wait_ge(mixk, g + 1)
                for c in range(KD):
                    product(bank[c][:, :], [(wk2[:, k, tok(c)], xk[:, k, :]) for k in range(KD)]).then_inc(kmm, 1)
                pe.wait_ge(mixr, g + 1)
                for t in range(NT):
                    if t >= 2:
                        pe.wait_ge(rsig, NT * g + t - 1)
                    product(bank[4 + t % 2][:, 0:D], [(xr[:, k, tok(t)], wr[:, k, :]) for k in range(KD)]).then_inc(rmm, 1)
                pe.wait_ge(kact, KD * g + KD)
                for t in range(NT):
                    if t >= 2:
                        pe.wait_ge(n8.added, NT * g + t - 1)
                    product(bank[6 + t % 2][:, 0:D], [(ka[:, k, tok(t)], wv2[:, k, :]) for k in range(KD)]).then_inc(n8.product, 1)
                end_of_turn(pe, g, turn, alone)

        @block.scalar
        def _(act):
            act.wait_ge(weights, NW * 16)

            def affine_copy(g, n, banks, gain, bias):
                for t in range(NT):
                    act.wait_ge(n.turned, NT * g + t + 1)
                    for k in range(KD):
                        last = act.activation(xnt[:, k, tok(t)], banks[t % 2][:, tok(k)], ACT.Identity,
                                              bias=cols[:, bias, k:k + 1], scale=cols[:, gain, k:k + 1])
                    last.then_inc(n.copied, 1)

            with act.Fori(0, G) as g:
                affine_copy(g, n4, bank[6:8], G1, B1)
                for t in range(NT):
                    act.wait_ge(qkmm, NT * g + t + 1)
                    if t >= 2:
                        act.wait_ge(sqred, NT * g + t - 1)
                    act.activation(sq[:, t % 2, :], bank[t][:, :], ACT.Square).then_inc(sqd, 1)
                for c in range(6):
                    act.wait_ge(fmm, 6 * g + c + 1)
                    act.activation(fm[:, c, :], bank[6 + c % 2][:, :], ACT.Identity,
                                   bias=cols[:, (BP, BCLK, BGATE)[c // 2], c % 2:c % 2 + 1]).then_inc(fmread, 1)
                act.drain()
                act.activation(ee, fm[:, 2:6, :], ACT.Abs)
                act.drain()
                act.activation(ee, ee, ACT.Exp, scale=-1.0).then_inc(eready, 1)
                for t in range(NT):
                    act.wait_ge(vmm, NT * g + t + 1)
                    act.activation(va[:, t, :, 0:DH1], bank[4 + t % 2][:, 0:D].rearrange("p (h d) -> p h d", d=DH1),
                                   ACT.Copy).then_inc(vcop, 1)
                act.wait_ge(npm, g + 1)
                for c in range(KD * GB):
                    pc = fm[:, c // GB, c % GB * S:(c % GB + 1) * S]
                    last = act.activation(pc, pc, ACT.Exp, bias=pmax[:, c:c + 1])
                last.then_inc(pexp, 1)
                act.wait_ge(uready, g + 1)
                act.activation(uu, uu, ACT.Ln).then_inc(lready, 1)
                act.wait_ge(clr, g + 1)
                act.activation(uu[:, 2:4, :], ee[:, 2:4, :], ACT.Exp, scale=-1.0).then_inc(gcr, 1)
                for i in range(HEADS):
                    act.wait_ge(s1m, HEADS * g + i + 1)
                    act.activation(es[:, i % 4, :], es[:, i % 4, :], ACT.Exp, scale=DH1 ** -0.5).then_inc(s1e, 1)
                for t in range(NT):
                    act.wait_ge(ogtp, NT * g + t + 1)
                    act.activation(ogt[:, :, tok(t)], bank[6 + t % 2][:, 0:D].rearrange("p (k n) -> p k n", k=KD),
                                   ACT.Copy).then_inc(ogc, 1)
                affine_copy(g, n5, bank[2:4], G2, B2)
                for c in range(MC):
                    act.wait_ge(m1mm, MC * g + c + 1)
                    act.activation(m1t[:, c, :], bank[(0, 1, 4, 5)[c % 4]][:, :], ACT.Gelu, bias=bm1[:, c:c + 1]).then_inc(m1g, 1)
                norm_copy(act, g, n6, bank[2:4], lambda t: x4t[:, :, tok(t)])
                for b in range(GB):
                    act.wait_ge(xvm, GB * g + b + 1)
                    act.activation(vx[:, b, :], bank[6 + b][0:S2, 0:D], ACT.Copy).then_inc(xvr, 1)
                for c in range(KD):
                    act.wait_ge(xq, KD * g + c + 1)
                    act.activation(qxt[:, c, :], bank[c][:, :], ACT.Copy).then_inc(xqr, 1)
                for t in range(NT + 1):
                    if t < NT:
                        act.wait_ge(xsub, NT * g + t + 1)
                        act.activation(sm[:, t, :], sm[:, t, :], ACT.Exp, scale=DHX ** -0.5).then_inc(xe, 1)
                    if t >= 1:
                        j = t - 1
                        act.wait_ge(xtp, NT * g + j + 1)
                        act.activation(pxt[:, j // 2, :, tok(j % 2)], bank[4 + j % 2][0:S2, :].rearrange("p (h n) -> p h n", h=HX),
                                       ACT.Copy).then_inc(xtc, 1)
                norm_copy(act, g, n7, bank[2:4], lambda t: x5t[:, :, t // 2, 1 + t % 2 * P:1 + (t % 2 + 1) * P])
                for c in range(KD):
                    act.wait_ge(kmm, KD * g + c + 1)
                    act.activation(rl[:, c, :], bank[c][:, :], ACT.Relu).then_inc(relu, 1)
                for t in range(NT):
                    act.wait_ge(rmm, NT * g + t + 1)
                    act.activation(rs[:, t, :], bank[4 + t % 2][:, 0:D], ACT.Sigmoid).then_inc(rsig, 1)
                end_of_turn(act, g, turn, alone)

        @block.vector
        def _(dve):
            dve.wait_ge(weights, NW * 16)
            dve.wait_ge(rows, NR * 16)
            dve.wait_ge(const, 1)
            dve.tensor_scalar(unmu[:, :, :], cols[:, MUR:MUK + 1, :], -1.0, 1.0, ALU.mult, ALU.add)

            def add_product(g, n, banks):
                for t in range(NT):
                    dve.wait_ge(n.product, NT * g + t + 1)
                    dve.tensor_tensor(n.y[:, t, :], banks[t % 2][:, 0:D], xb[:, t, :], ALU.add).then_inc(n.added, 1)
                    norm_tile_stats(dve, g, n, t)

            with dve.Fori(0, G) as g:
                dve.tensor_copy(n3.y[:, :, :], keep["x"][:, bass.ts(g, NT), :])
                for t in range(NT):
                    norm_tile_stats(dve, g, n3, t)
                norm_rows(dve, g, n3, lambda t: x3[:, t, :])
                for t in range(NT):
                    norm_tile_stats(dve, g, n4, t)
                norm_rows(dve, g, n4, lambda t: xn[:, t, :])
                for t in range(NT):
                    dve.wait_ge(sqd, NT * g + t + 1)
                    dve.tensor_reduce(ss[:, t * 32:(t + 1) * 32], sq[:, t % 2, :].rearrange("p (h d) -> p h d", d=DH1),
                                      AX.X, ALU.add).then_inc(sqred, 1)
                dve.drain()
                dve.tensor_scalar(ss[:, :], ss[:, :], 1e-24, None, ALU.max).then_inc(ssready, 1)
                dve.wait_ge(fmread, 6 * g + 2)
                dve.tensor_reduce(pmax[:, :], fm[:, 0:2, :].rearrange("p m (b s) -> p (m b) s", b=GB), AX.X, ALU.max)
                dve.drain()
                dve.tensor_scalar(pmax[:, :], pmax[:, :], -1.0, None, ALU.mult).then_inc(npm, 1)
                dve.wait_ge(eready, g + 1)
                dve.tensor_scalar(uu, ee, 1.0, None, ALU.add)
                dve.drain()
                dve.tensor_scalar(dd, uu[:, 0:2, :], -1.0, None, ALU.add).then_inc(uready, 1)
                for t in range(NT):
                    dve.wait_ge(rnr, g + 1)
                    dve.tensor_tensor(qn[:, t, :].rearrange("p (h d) -> p h d", d=DH1),
                                      bank[t][:, :].rearrange("p (h d) -> p h d", d=DH1),
                                      rn[:, t * 32:(t + 1) * 32].unsqueeze(2).to_broadcast([P, 32, DH1]), ALU.mult).then_inc(qnr, 1)
                dve.drain()
                for t in range(NT):
                    q4 = qn[:, t, :].rearrange("p (h d two) -> p h d two", d=DH1 // 2, two=2)
                    r4 = rb[:, t, :].rearrange("p (h d two) -> p h d two", d=DH1 // 2, two=2)
                    for o in range(2):
                        dve.tensor_tensor(r4[:, :, :, o], q4[:, :, :, 1 - o],
                                          rope[:, t % 2:t % 2 + 1, DH1 + 8 * o:DH1 + 8 * o + 8].to_broadcast([P, 32, 8]), ALU.mult)
                for t in range(NT):
                    dve.drain()
                    dve.wait_ge(rar, NT * g + t + 1)
                    dve.tensor_tensor(rb[:, t, :], rb[:, t, :], ra[:, t, :], ALU.add).then_inc(roped, 1)
                dve.wait_ge(lready, g + 1)
                dve.scalar_tensor_tensor(uu[:, 0:2, :], dd, 0.0, uu[:, 0:2, :], ALU.is_equal, ALU.add)
                dve.drain()
                dve.scalar_tensor_tensor(dd, dd, 0.0, dd, ALU.is_equal, ALU.add)
                dve.drain()
                dve.reciprocal(dd, dd)
                dve.drain()
                dve.tensor_tensor(uu[:, 0:2, :], uu[:, 0:2, :], dd, ALU.mult)
                dve.drain()
                dve.tensor_tensor(uu[:, 0:2, :], uu[:, 0:2, :], ee[:, 0:2, :], ALU.mult)
                dve.drain()
                dve.scalar_tensor_tensor(fm[:, 2:6, :], fm[:, 2:6, :], 0.0, uu, ALU.max, ALU.add)
                dve.drain()
                for m in range(KD):
                    for b in range(GB):
                        dve.tensor_tensor_scan(ee[:, 2 + m, b * S:(b + 1) * S], ones[:, :], fm[:, 4 + m, b * S:(b + 1) * S],
                                               0.0, ALU.mult, ALU.add)
                dve.drain()
                dve.tensor_scalar(ee[:, 2:4, :], ee[:, 2:4, :], -50.0, 60.0, ALU.max, ALU.min).then_inc(clr, 1)
                dve.wait_ge(pexp, g + 1)
                dve.tensor_tensor(fm[:, 0:2, :], fm[:, 0:2, :], fm[:, 2:4, :], ALU.mult)
                dve.drain()
                for m in range(KD):
                    for b in range(GB):
                        dve.tensor_tensor_scan(dd[:, m, b * S:(b + 1) * S], ones[:, :], fm[:, m, b * S:(b + 1) * S],
                                               0.0, ALU.mult, ALU.add)
                dve.drain()
                dve.tensor_scalar(qf[:, :, :], dd, 1e-8, None, ALU.add)
                dve.drain()
                dve.reciprocal(qf[:, :, :], qf[:, :, :])
                dve.drain()
                dve.wait_ge(gcr, g + 1)
                dve.tensor_tensor(qf[:, :, :], qf[:, :, :], uu[:, 2:4, :], ALU.mult)
                dve.tensor_scalar(kf[:, :, :], uu[:, 2:4, :], 1e-8, None, ALU.add)
                dve.drain()
                dve.reciprocal(kf[:, :, :], kf[:, :, :])
                dve.drain()
                dve.tensor_tensor(kf[:, :, :], kf[:, :, :], fm[:, 0:2, :], ALU.mult)
                dve.drain()
                for t in range(NT):
                    dve.wait_ge(qktp, NT * g + t + 1)
                    qk = bank[t][:, :].rearrange("p (c n) -> p c n", c=4)
                    dve.tensor_tensor(qt[:, :, tok(t)], qk[:, 0:2, :], qf[:, :, tok(t)], ALU.mult)
                    for o in range(2):
                        last = dve.scalar_tensor_tensor(kt[:, o, :, tok(t)], qk[:, 2:4, :], parity[:, o:o + 1], kf[:, :, tok(t)],
                                                        ALU.mult, ALU.mult)
                    last.then_inc(qkt, 1)
                for i in range(HEADS + 3):
                    if i < HEADS:
                        dve.wait_ge(s1, HEADS * g + i + 1)
                        if i >= 4:
                            dve.wait_ge(av1, HEADS * g + i - 3)
                        dve.tensor_tensor(es[:, i % 4, :], bank[i % 2][:, 0:CAUSAL], mask1[:, :], ALU.min).then_inc(s1m, 1)
                    j = i - 3
                    if j >= 0 and j % 4 == 3:
                        q = j // 4
                        dve.wait_ge(av1, HEADS * g + j + 1)
                        dve.tensor_copy(ut[:, q % 4, q // 4 * S:(q // 4 + 1) * S], bank[4 + q % 2][:, 0:S]).then_inc(utc, 1)
                for t in range(NT):
                    dve.wait_ge(ttp, NT * g + t + 1)
                    heads = bank[2 + t % 2][:, :].rearrange("p (h d) -> p h d", d=32)
                    dve.reciprocal(rden[:, t, :], heads[:, :, DH1])
                    dve.drain()
                    dve.tensor_tensor(og[:, t, :].rearrange("p (h d) -> p h d", d=DH1), heads[:, :, 0:DH1],
                                      rden[:, t, :].unsqueeze(2).to_broadcast([P, H1, DH1]), ALU.mult).then_inc(ogr, 1)
                dve.wait_ge(biased, 3 * g + 1)
                add_product(g, n5, bank[4:6])
                norm_rows(dve, g, n5, lambda t: h5[:, t, :])
                dve.wait_ge(biased, 3 * g + 2)
                add_product(g, n6, bank[6:8])
                for c in range(KD):
                    dve.wait_ge(xkm, KD * g + c + 1)
                    dve.tensor_copy(kxt[:, c, :], bank[4 + c][:, 0:GB * S2]).then_inc(xkr, 1)
                norm_rows(dve, g, n6, lambda t: x4[:, t, :])
                for t in range(NT + 1):
                    if t < NT:
                        dve.wait_ge(xs, NT * g + t + 1)
                        for o in range(2):
                            last = dve.tensor_tensor(sm[:, t, :].rearrange("p (h two n) -> p h two n", two=2, n=S2)[:, :, o, :],
                                                     bank[t % 2 + 2 * o][:, 0:2 * S2].rearrange("p (h n) -> p h n", n=S2),
                                                     maskx[:, t % 2, 0:2 * S2].rearrange("p (h n) -> p h n", n=S2), ALU.add)
                        last.then_inc(xsr, 1)
                        dve.drain()
                        s3 = sm[:, t, :].rearrange("p (h n) -> p h n", h=HX)
                        dve.tensor_reduce(xmax[:, t, :], s3, AX.X, ALU.max)
                        dve.drain()
                        dve.tensor_tensor(s3, s3, xmax[:, t, :].unsqueeze(2).to_broadcast([P, HX, S2]), ALU.subtract).then_inc(xsub, 1)
                    if t >= 1:
                        j = t - 1
                        s3 = sm[:, j, :].rearrange("p (h n) -> p h n", h=HX)
                        dve.wait_ge(xe, NT * g + j + 1)
                        dve.tensor_reduce(xsum[:, j, :], s3, AX.X, ALU.add)
                        dve.drain()
                        dve.reciprocal(xinv[:, j, :], xsum[:, j, :])
                        dve.drain()
                        dve.tensor_tensor(s3, s3, xinv[:, j, :].unsqueeze(2).to_broadcast([P, HX, S2]), ALU.mult).then_inc(xp, 1)
                for q in range(GB * KD):
                    dve.wait_ge(xav, 4 * g + q + 1)
                    dve.tensor_copy(zxt[:, q % KD, q // KD * S:(q // KD + 1) * S], bank[6 + q % 2][:, 0:S]).then_inc(xz, 1)
                dve.wait_ge(biased, 3 * g + 3)
                add_product(g, n7, bank[0:2])
                norm_rows(dve, g, n7, lambda t: x5[:, t, :])
                dve.memset(x5t[:, :, :, 0:1], 0.0)
                dve.drain()
                dve.wait_ge(n7.copied, NT * g + NT)
                for mu, dst, done in ((MUK, xk, mixk), (MUR, xr, mixr)):
                    for k in range(KD):
                        dve.tensor_scalar(shift[:, k, :].rearrange("p (b s) -> p b s", b=GB), x5t[:, k, :, 0:S],
                                          unmu[:, mu - MUR, k:k + 1], None, ALU.mult)
                    dve.drain()
                    for k in range(KD):
                        last = dve.scalar_tensor_tensor(dst[:, k, :].rearrange("p (b s) -> p b s", b=GB), x5t[:, k, :, 1:S + 1],
                                                        cols[:, mu, k:k + 1], shift[:, k, :].rearrange("p (b s) -> p b s", b=GB),
                                                        ALU.mult, ALU.add)
                    last.then_inc(done, 1)
                    dve.drain()
                for c in range(KD):
                    dve.wait_ge(relu, KD * g + c + 1)
                    dve.tensor_tensor(ka[:, c, :], bank[c][:, :], rl[:, c, :], ALU.mult).then_inc(kact, 1)
                dve.wait_ge(rsig, NT * g + NT)
                for t in range(NT):
                    dve.wait_ge(n8.product, NT * g + t + 1)
                    dve.tensor_tensor(rs[:, t, :], bank[6 + t % 2][:, 0:D], rs[:, t, :], ALU.mult).then_inc(n8.added, 1)
                    dve.drain()
                    dve.tensor_tensor(n8.y[:, t, :], rs[:, t, :], x5[:, t, :], ALU.add)
                    norm_tile_stats(dve, g, n8, t)
                norm_rows(dve, g, n8, lambda t: xo[:, t, :])
                end_of_turn(dve, g, turn, alone)


def decoder(nc, dram):
    with ExitStack() as ctx:
        memory = Memory(nc, ctx)
        keep = {"x": memory.take([P, TILES, D])}
        last = memory.mark
        keep["pick"] = memory.take([P, TILES, NE])
        keep["xt"] = memory.take([P, KD, B * S])
        first = memory.mark
        attention_layers(nc, dram, memory, keep)
        memory.mark = first
        expert_layer(nc, dram, memory, keep)
        memory.mark = last
        last_layers(nc, dram, memory, keep)


def laid_out(a):
    def t(x):
        return x.T

    def columns(v):
        return v.reshape(-1, P).T

    w1, b1 = a["L0_ffn_dense_1_w"], a["L0_ffn_dense_1_b"]
    x = a["x"].reshape(B * S, D)
    half = DH1 // 2
    freqs = np.exp(-np.arange(half, dtype=np.float32) * np.float32(np.log(10000.0) / half)).astype(np.float32)
    theta = (np.arange(S, dtype=np.float32)[:, None] * freqs[None, :]).astype(np.float32)
    cos, sin = np.cos(theta), np.sin(theta)
    rope = np.concatenate([np.repeat(cos, 2, 1), -sin, sin], 1).astype(np.float32)
    even = (np.arange(P) // DH1 % 2 == 0).astype(np.float32)
    return {
        "x": x, "xt": t(x), "mask": a["mask_BxSxS2_ik0"].reshape(B * S, S2),
        "ctx": a["ctx_1024"], "ctxt": a["ctx_1024"].transpose(0, 2, 1),
        "wq0": t(a["L0_attn_W_Q"].reshape(E0, D)), "wk0": t(a["L0_attn_W_K"].reshape(E0, D)),
        "wv0": t(a["L0_attn_W_V"].reshape(E0, D)), "wo0": a["L0_attn_W_O"].transpose(0, 2, 1).reshape(E0, D),
        "wx0": t(a["L0_xattn_W"]), "bx0": columns(a["L0_xattn_b"]), "gate": a["L0_ffn_gate_w"],
        "w1": np.concatenate([w1[:, 0::2], w1[:, 1::2]], 1).transpose(0, 2, 1),
        "w2": a["L0_ffn_dense_2_w"].transpose(0, 2, 1),
        "b1": np.concatenate([b1[:, 0::2], b1[:, 1::2]], 1).reshape(NE, 2 * FC, P).transpose(2, 0, 1),
        "b2": a["L0_ffn_dense_2_b"],
        "wqk": np.concatenate([a["L1_attn_Wq"], a["L1_attn_Wk"]], 1), "wv1": a["L1_attn_Wv"],
        "wgate": a["L1_attn_gate_w"], "wpp": a["L1_attn_p_w"], "wclock": np.repeat(a["L1_attn_clock_w"], DH1, 1),
        "wout": a["L1_attn_out_w"], "wm1": a["L1_attn_mlp_w1"], "wm2": a["L1_attn_mlp_w2"],
        "bm1": columns(a["L1_attn_mlp_b1"]),
        "cols": np.stack([columns(v) for v in (
            a["L1_attn_p_b"], np.repeat(a["L1_attn_clock_b"], DH1), a["L1_attn_gate_b"], a["L1_attn_ln1_g"],
            a["L1_attn_ln1_b"], a["L1_attn_ln2_g"], a["L1_attn_ln2_b"], a["L1_ffn_mu_r"], a["L1_ffn_mu_k"])], 1),
        "rows": np.stack([a["L1_attn_out_b"], a["L1_attn_mlp_b2"], a["L1_xattn_bp"]]),
        "wxq": t(a["L1_xattn_Wq"]), "wxk": t(a["L1_xattn_Wk"]), "wxv": t(a["L1_xattn_Wv"]), "wxp": t(a["L1_xattn_Wp"]),
        "wr": t(a["L1_ffn_W_r"]), "wk2": t(a["L1_ffn_W_k"]), "wv2": t(a["L1_ffn_W_v"]),
        "rope": rope.reshape(2, P, 2 * DH1).transpose(1, 0, 2), "parity": np.stack([even, 1 - even], 1),
    }


def kernel(**inputs):
    import concourse.bacc as bacc
    from concourse.bass_utils import run_bass_kernel_spmd

    nc = bacc.Bacc("TRN2", target_bir_lowering=False, num_devices=1)
    arrays, dram = {}, {}
    for name, a in laid_out({k: np.asarray(v) for k, v in inputs.items()}).items():
        a = np.ascontiguousarray(a)
        arrays[f"in_{name}"] = a
        dram[name] = nc.dram_tensor(f"in_{name}", a.shape, mybir.dt.from_np(a.dtype), kind="ExternalInput").ap()
    dram["out"] = nc.dram_tensor("out_x", (B * S, D), F32, kind="ExternalOutput").ap()
    decoder(nc, dram)
    result = run_bass_kernel_spmd(nc, [arrays], core_ids=[0])
    return result.results[0]["out_x"].reshape(B, S, D)
```

```python
import concourse.bass as bass
from concourse import mybir
from contextlib import ExitStack
import numpy as np

F32 = mybir.dt.float32
I32 = mybir.dt.int32
U32 = mybir.dt.uint32
ALU = mybir.AluOpType
ACT = mybir.ActivationFunctionType
AX = mybir.AxisListType

B, S, D = 8, 256, 256
S2 = 120
P = 128
KD = D // P
GB = 2
G = B // GB
GT = GB * S
NT = GT // P
TILES = B * S // P
EPS = 1e-5
H0, DH0 = 16, 64
E0 = H0 * DH0
PAIRS0 = H0 // 2
NE, FF = 8, 512
FC = FF // P
SLOT_TILES = 2 * B * S // P + NE - 1
SLOTS = SLOT_TILES * P
H1, DH1 = 16, 16
M1 = 4 * D
MC = M1 // P
HX, DHX = 4, 64

CAUSAL = P + S


class Memory:

    WORDS = 48 * 1024

    def __init__(self, nc, ctx):
        self.words = ctx.enter_context(nc.sbuf_tensor("words", [P, self.WORDS], F32))
        self.bank = [ctx.enter_context(nc.psum_tensor(f"bank{i}", [P, 512], F32)) for i in range(8)]
        self.mark = 0
        self.nc, self.ctx = nc, ctx
        self.used, self.free = [], []
        self.alone = ctx.enter_context(nc.semaphore("alone"))

    def sem(self, name):
        s = self.free.pop() if self.free else self.ctx.enter_context(self.nc.semaphore(name))
        self.used.append(s)
        return s

    def clear(self):
        used = self.used
        with self.nc.Block() as block:
            @block.gpsimd
            def _(pool):
                for s in used:
                    pool.sem_clear(s)
        self.free, self.used = self.free + used, []

    def take(self, shape, dt=F32):
        n = int(np.prod(shape[1:]))
        assert self.mark + n <= self.WORDS, (shape, self.mark)
        v = cut(self.words, self.mark, shape[1:], shape[0])
        self.mark += n + n % 2
        return v if dt == F32 else v.bitcast(dt)


def cut(region, start, dims, rows=P):
    v = region[0:rows, start:start + int(np.prod(dims))]
    if len(dims) == 1:
        return v
    names = "abcd"[:len(dims)]
    return v.rearrange(f"p ({' '.join(names)}) -> p {' '.join(names)}", **dict(zip(names, dims)))


class Norm:

    def __init__(self, mem, name, y=None, product=True, turned=True):
        self.stats = mem.sem(f"{name}_stats")
        self.rstd = mem.sem(f"{name}_rstd")
        self.normed = mem.sem(f"{name}_normed")
        if product:
            self.product = mem.sem(f"{name}_product")
            self.added = mem.sem(f"{name}_added")
        if turned:
            self.turned = mem.sem(f"{name}_turned")
            self.copied = mem.sem(f"{name}_copied")
        self.y = mem.take([P, NT, D]) if y is None else y
        self.bn = mem.take([P, NT, 6])
        self.mv = mem.take([P, NT, 2])
        self.var = mem.take([P, NT])
        self.inv = mem.take([P, NT])


def norm_tile_stats(dve, g, n, t):
    dve.drain()
    dve.bn_stats(n.bn[:, t, :], n.y[:, t, :])
    dve.drain()
    last = dve.bn_aggr(n.mv[:, t, :], n.bn[:, t, :])
    if t == NT - 1:
        last.then_inc(n.stats, 1)


def norm_rows(dve, g, n, out):
    dve.drain()
    dve.wait_ge(n.rstd, g + 1)
    for t in range(NT):
        dve.tensor_scalar(out(t), n.y[:, t, :], n.mv[:, t, 0:1], n.inv[:, t:t + 1],
                          ALU.subtract, ALU.mult).then_inc(n.normed, 1)


def norm_rstd(pool, g, n, eps, minus_half):
    pool.drain()
    pool.wait_ge(n.stats, g + 1)
    pool.tensor_tensor(n.var[:, :], n.mv[:, :, 1], eps, ALU.add)
    pool.drain()
    pool.tensor_tensor(n.inv[:, :], n.var[:, :], minus_half, ALU.pow).then_inc(n.rstd, 1)


def norm_turn(pe, g, n, rows, banks, ident):
    for t in range(NT):
        pe.wait_ge(n.normed, NT * g + t + 1)
        if t >= 2:
            pe.wait_ge(n.copied, NT * g + t - 1)
        for k in range(KD):
            last = pe.transpose(banks[t % 2][:, k * P:(k + 1) * P], rows(t)[:, k * P:(k + 1) * P], ident)
        last.then_inc(n.turned, 1)


def norm_copy(act, g, n, banks, out):
    for t in range(NT):
        act.wait_ge(n.turned, NT * g + t + 1)
        act.activation(out(t), banks[t % 2][:, 0:D].rearrange("p (k n) -> p k n", k=KD),
                       ACT.Copy).then_inc(n.copied, 1)


def end_of_turn(eng, g, turn, alone, engines=5):
    eng.drain()
    eng.nop().then_inc(turn, 1)
    eng.wait_ge(turn, engines * g + engines)
    eng.sem_inc(alone, 1)




def attention_layers(nc, dram, memory, keep):
    with ExitStack() as ctx:
        sb = memory.take
        bank = memory.bank

        sem = memory.sem
        alone = memory.alone
        wq, wk, wv = (sb([P, KD, E0]) for _ in range(3))
        wo = sb([P, PAIRS0, D])
        wx = sb([P, KD, D])
        bx = sb([P, KD])
        gate_w = sb([P, KD, NE])
        ident, minus_half, eps = sb([P, P]), sb([P, NT]), sb([P, NT])
        mask0 = sb([P, CAUSAL])
        expert = sb([P, NT, NE])
        xg, xt = sb([P, NT, D]), sb([P, KD, GT])
        qt, kt = sb([P, PAIRS0, GT]), sb([P, PAIRS0, GT])
        v = sb([P, NT, E0])
        prob = sb([P, 4, CAUSAL])
        mx, negmax, rowsum, inv = (sb([P, 4, 2]) for _ in range(4))
        probt = sb([P, 2, CAUSAL])
        zt = sb([P, PAIRS0, GT])
        x1, x1t = sb([P, NT, D]), sb([P, KD, GT])
        mem, memt = sb([S2, GB, D]), sb([P, KD, GB, S2])
        maski, maskf = sb([P, NT, S2], I32), sb([P, NT, S2])
        qx = sb([P, KD, GT])
        probx, probxt = sb([P, NT, S2]), sb([S2, NT, P])
        mxx, negx, sumx, invx = (sb([P, NT]) for _ in range(4))
        x2, x2t = sb([P, NT, D]), sb([P, KD, GT])
        score8, top8 = sb([P, NT, NE]), sb([P, NT, 8])
        at8, at8f = sb([P, NT, 8], U32), sb([P, NT, 8])
        gd, ge, gp, gq = (sb([P, NT]) for _ in range(4))
        pick0, pick1 = sb([P, NT, NE]), sb([P, NT, NE])

        weights, loaded, const, turn, rowsout = (sem(f"a_{n}") for n in ("weights", "loaded", "const", "turn", "rowsout"))
        chunk, ev_act, ev_dve = sem("chunk"), sem("ev_act"), sem("ev_dve")
        scores, shifted, exped, probs = sem("scores"), sem("shifted"), sem("exped"), sem("probs")
        tposed, tcopied, heads, zcopied = sem("tposed"), sem("tcopied"), sem("heads"), sem("zcopied")
        xlogit, xshift, xexp, xtp, xtc = (sem(n) for n in ("xlogit", "xshift", "xexp", "xtp", "xtc"))
        gmm, gdiff, gexp, picked = sem("gmm"), sem("gdiff"), sem("gexp"), sem("picked")
        n1, n2 = Norm(memory, "n1"), Norm(memory, "n2")
        HEADS = GB * H0
        QK = 2 * PAIRS0
        VC = NT * (E0 // 512)
        NCH = QK + VC + KD
        HALF = NCH // 2
        block = ctx.enter_context(nc.Block())

        @block.sync
        def _(sp):
            for dst, src in ((wq, dram["wq0"]), (wk, dram["wk0"]), (wv, dram["wv0"]), (wx, dram["wx0"]),
                             (gate_w, dram["gate"])):
                sp.dma_start(dst[:, :, :], src.rearrange("(k p) n -> p k n", p=P)).then_inc(weights, 16)
            sp.dma_start(wo[:, :, :], dram["wo0"].rearrange("(k p) n -> p k n", p=P)).then_inc(weights, 16)
            sp.dma_start(bx[:, :], dram["bx0"]).then_inc(weights, 16)
            with sp.Fori(0, G) as g:
                sp.dma_start(xt[:, :, :], dram["xt"].rearrange("(k p) n -> p k n", p=P)[:, :, bass.ts(g, GT)]).then_inc(loaded, 16)
                sp.dma_start(xg[:, :, :], dram["x"].rearrange("(g t p) n -> g p t n", p=P, t=NT)[g]).then_inc(loaded, 16)
                sp.dma_start(maski[:, :, :], dram["mask"].rearrange("(g t p) n -> g p t n", p=P, t=NT)[g]).then_inc(loaded, 16)
                sp.dma_start(mem[:, :, :], dram["ctx"].rearrange("(g b) s n -> g s b n", b=GB)[g]).then_inc(loaded, 16)
                for b in range(GB):
                    sp.dma_start(memt[:, :, b, :], dram["ctxt"].rearrange("(g b) (k p) s -> g b p k s", b=GB, p=P)[g, b]).then_inc(loaded, 16)
                sp.wait_ge(n2.normed, NT * g + NT)
                sp.dma_start(dram["x2"].rearrange("(g t p) n -> g p t n", p=P, t=NT)[g], x2[:, :, :]).then_inc(rowsout, 16)
                sp.wait_ge(rowsout, 16 * g + 16)
                sp.sem_inc(alone, 1)
                end_of_turn(sp, g, turn, alone)

        @block.gpsimd
        def _(pool):
            pool.memset(ident[:, :], 0.0)
            pool.memset(mask0[:, :], 0.0)
            pool.memset(minus_half[:, :], -0.5)
            pool.memset(eps[:, :], EPS)
            pool.iota(expert[:, :, :], pattern=[[0, NT], [1, NE]], base=0, channel_multiplier=0,
                      allow_small_or_imprecise_dtypes=True)
            pool.drain()
            pool.affine_select(out=ident[:, :], in_=ident[:, :], compare_op=ALU.not_equal, fill=1.0, base=0,
                               pattern=[[-1, P]], channel_multiplier=1)
            for c in (0, S):
                pool.affine_select(out=mask0[:, c:c + P], in_=mask0[:, c:c + P], compare_op=ALU.is_ge,
                                   fill=-1e10, base=0, pattern=[[-1, P]], channel_multiplier=1)
            pool.drain()
            pool.nop().then_inc(const, 1)
            with pool.Fori(0, G) as g:
                norm_rstd(pool, g, n1, eps[:, :], minus_half[:, :])
                norm_rstd(pool, g, n2, eps[:, :], minus_half[:, :])
                pool.wait_ge(n2.normed, NT * g + NT)
                pool.tensor_copy(keep["x"][:, bass.ts(g, NT), :], x2[:, :, :])
                pool.wait_ge(picked, g + 1)
                pool.tensor_copy(keep["pick"][:, bass.ts(g, NT), :], pick0[:, :, :])
                pool.tensor_copy(keep["at"][:, bass.ts(g, NT), :], at8f[:, :, 0:2])
                pool.tensor_copy(keep["weight"][:, bass.ts(g, NT), 0], gp[:, :])
                pool.tensor_copy(keep["weight"][:, bass.ts(g, NT), 1], gq[:, :])
                end_of_turn(pool, g, turn, alone)

        @block.tensor
        def _(pe):
            def project(g, c, pairs):
                if c >= 4:
                    pe.wait_ge((ev_act, ev_dve)[c % 2], HALF * g + (c - 4) // 2 + 1)
                for i, (w, r) in enumerate(pairs):
                    last = pe.matmul(bank[c % 4][:, :], w, r, start=i == 0, stop=i == len(pairs) - 1)
                last.then_inc(chunk, 1)

            pe.wait_ge(weights, 7 * 16)
            pe.wait_ge(const, 1)
            with pe.Fori(0, G) as g:
                pe.wait_ge(loaded, 96 * g + 96)
                for c in range(QK):
                    w = wq if c < PAIRS0 else wk
                    m = c % PAIRS0
                    project(g, c, [(w[:, k, m * P:(m + 1) * P], xt[:, k, :]) for k in range(KD)])
                for c in range(VC):
                    t, h = c // 2, c % 2
                    project(g, QK + c, [(xt[:, k, t * P:(t + 1) * P], wv[:, k, h * 512:(h + 1) * 512]) for k in range(KD)])
                pe.wait_ge(ev_act, HALF * g + (QK + VC) // 2)
                pe.wait_ge(ev_dve, HALF * g + (QK + VC) // 2)
                for i in range(HEADS + 3):
                    if i < HEADS:
                        b, h = i // H0, i % H0
                        r = slice(DH0 * (h % 2), DH0 * (h % 2) + DH0)
                        if i >= 2:
                            pe.wait_ge(shifted, HEADS * g + i - 1)
                        for t in range(2):
                            last = pe.matmul(bank[i % 2][:, t * P:t * P + P * (t + 1)],
                                             kt[r, h // 2, b * S + t * P:b * S + (t + 1) * P],
                                             qt[r, h // 2, b * S:b * S + P * (t + 1)], start=True, stop=True)
                        last.then_inc(scores, 1)
                    j = i - 2
                    if 0 <= j < HEADS:
                        pe.wait_ge(probs, HEADS * g + j + 1)
                        if j >= 2:
                            pe.wait_ge(tcopied, HEADS * g + j - 1)
                        for n, c in enumerate((0, P, S)):
                            last = pe.transpose(bank[2 + j % 2][:, n * P:(n + 1) * P],
                                                prob[:, j % 4, c:c + P], ident[:, :])
                        last.then_inc(tposed, 1)
                    j = i - 3
                    if 0 <= j < HEADS:
                        b, h = j // H0, j % H0
                        pe.wait_ge(tcopied, HEADS * g + j + 1)
                        if j % 2 == 0 and j >= 4:
                            pe.wait_ge(zcopied, HEADS // 2 * g + j // 2 - 1)
                        o = bank[4 + j // 2 % 2][DH0 * (h % 2):DH0 * (h % 2) + DH0, :]
                        pe.matmul(o[:, 0:S], v[:, 2 * b, h * DH0:(h + 1) * DH0],
                                  probt[:, j % 2, 0:S], start=True, stop=False)
                        pe.matmul(o[:, P:S], v[:, 2 * b + 1, h * DH0:(h + 1) * DH0],
                                  probt[:, j % 2, S:S + P], start=False, stop=True).then_inc(heads, 1)
                pe.wait_ge(zcopied, HEADS // 2 * g + HEADS // 2)
                for t in range(NT):
                    if t >= 2:
                        pe.wait_ge(n1.added, NT * g + t - 1)
                    for m in range(PAIRS0):
                        last = pe.matmul(bank[6 + t % 2][:, 0:D], zt[:, m, t * P:(t + 1) * P], wo[:, m, :],
                                         start=m == 0, stop=m == PAIRS0 - 1)
                    last.then_inc(n1.product, 1)
                norm_turn(pe, g, n1, lambda t: x1[:, t, :], bank[2:4], ident[:, :])
                pe.wait_ge(n1.copied, NT * g + NT)
                for c in range(KD):
                    project(g, QK + VC + c, [(wx[:, k, c * P:(c + 1) * P], x1t[:, k, :]) for k in range(KD)])
                pe.wait_ge(ev_act, HALF * g + HALF)
                pe.wait_ge(ev_dve, HALF * g + HALF)
                for t in range(NT):
                    if t >= 2:
                        pe.wait_ge(xshift, NT * g + t - 1)
                    for k in range(KD):
                        last = pe.matmul(bank[4 + t % 2][:, 0:S2], qx[:, k, t * P:(t + 1) * P],
                                         memt[:, k, t // 2, :], start=k == 0, stop=k == KD - 1)
                    last.then_inc(xlogit, 1)
                for t in range(NT):
                    pe.wait_ge(xexp, NT * g + t + 1)
                    if t >= 2:
                        pe.wait_ge(xtc, NT * g + t - 1)
                    pe.transpose(bank[6 + t % 2][0:S2, 0:P], probx[:, t, :], ident[:, :]).then_inc(xtp, 1)
                for t in range(NT):
                    pe.wait_ge(xtc, NT * g + t + 1)
                    if t >= 2:
                        pe.wait_ge(n2.added, NT * g + t - 1)
                    pe.matmul(bank[t % 2][:, 0:D], probxt[:, t, :], mem[:, t // 2, :],
                              start=True, stop=True).then_inc(n2.product, 1)
                norm_turn(pe, g, n2, lambda t: x2[:, t, :], bank[2:4], ident[:, :])
                for t in range(NT):
                    pe.wait_ge(n2.copied, NT * g + t + 1)
                    for k in range(KD):
                        last = pe.matmul(bank[4][:, t * NE:(t + 1) * NE], x2t[:, k, t * P:(t + 1) * P],
                                         gate_w[:, k, :], start=k == 0, stop=k == KD - 1)
                last.then_inc(gmm, 1)
                end_of_turn(pe, g, turn, alone)

        def target(c):
            if c < QK:
                return (qt if c < PAIRS0 else kt)[:, c % PAIRS0, :]
            c -= QK
            return v[:, c // 2, (c % 2) * 512:(c % 2 + 1) * 512]

        @block.scalar
        def _(act):
            act.wait_ge(weights, 7 * 16)
            with act.Fori(0, G) as g:
                for c in range(0, QK + VC, 2):
                    act.wait_ge(chunk, NCH * g + c + 1)
                    act.activation(target(c), bank[c % 4][:, :], ACT.Copy).then_inc(ev_act, 1)
                for i in range(HEADS + 2):
                    if i < HEADS:
                        act.wait_ge(shifted, HEADS * g + i + 1)
                        for t in range(2):
                            c = slice(t * P, t * P + P * (t + 1))
                            last = act.activation(prob[:, i % 4, c], prob[:, i % 4, c], ACT.Exp,
                                                  bias=negmax[:, i % 4, t:t + 1], scale=DH0 ** -0.5,
                                                  accum_out=rowsum[:, i % 4, t:t + 1])
                        last.then_inc(exped, 1)
                    j = i - 2
                    if 0 <= j < HEADS:
                        act.wait_ge(tposed, HEADS * g + j + 1)
                        if j >= 2:
                            act.wait_ge(heads, HEADS * g + j - 1)
                        act.activation(probt[:, j % 2, :], bank[2 + j % 2][:, 0:CAUSAL], ACT.Copy).then_inc(tcopied, 1)
                norm_copy(act, g, n1, bank[2:4], lambda t: x1t[:, :, t * P:(t + 1) * P])
                act.wait_ge(chunk, NCH * g + QK + VC + 1)
                act.activation(qx[:, 0, :], bank[(QK + VC) % 4][:, :], ACT.Identity, bias=bx[:, 0:1]).then_inc(ev_act, 1)
                for t in range(NT):
                    act.wait_ge(xshift, NT * g + t + 1)
                    act.activation(probx[:, t, :], probx[:, t, :], ACT.Exp, bias=negx[:, t:t + 1],
                                   accum_out=sumx[:, t:t + 1]).then_inc(xexp, 1)
                for t in range(NT):
                    act.wait_ge(xtp, NT * g + t + 1)
                    act.activation(probxt[:, t, :], bank[6 + t % 2][0:S2, 0:P], ACT.Copy).then_inc(xtc, 1)
                norm_copy(act, g, n2, bank[2:4], lambda t: x2t[:, :, t * P:(t + 1) * P])
                act.wait_ge(gdiff, g + 1)
                act.activation(ge[:, :], gd[:, :], ACT.Exp).then_inc(gexp, 1)
                end_of_turn(act, g, turn, alone)

        @block.vector
        def _(dve):
            dve.wait_ge(weights, 7 * 16)
            dve.wait_ge(const, 1)
            with dve.Fori(0, G) as g:
                for c in range(1, QK + VC, 2):
                    dve.wait_ge(chunk, NCH * g + c + 1)
                    dve.tensor_copy(target(c), bank[c % 4][:, :]).then_inc(ev_dve, 1)
                dve.wait_ge(loaded, 96 * g + 96)
                dve.tensor_scalar(maskf[:, :, :], maski[:, :, :], -1.0, 1e9, ALU.add, ALU.mult)
                for i in range(HEADS + 4):
                    if i < HEADS:
                        dve.wait_ge(scores, HEADS * g + i + 1)
                        if i >= 4:
                            dve.wait_ge(tposed, HEADS * g + i - 3)
                        dve.sem_inc(alone, 1)
                        for t in range(2):
                            c = slice(t * P, t * P + P * (t + 1))
                            dve.tensor_tensor_reduce(out=prob[:, i % 4, c], in0=bank[i % 2][:, c], in1=mask0[:, c],
                                                     scale=1.0, scalar=-3e38, op0=ALU.add, op1=ALU.max,
                                                     accum_out=mx[:, i % 4, t:t + 1])
                        dve.drain()
                        dve.tensor_scalar(negmax[:, i % 4, :], mx[:, i % 4, :], -DH0 ** -0.5, None,
                                          ALU.mult).then_inc(shifted, 1)
                    j = i - 1
                    if 0 <= j < HEADS:
                        dve.wait_ge(exped, HEADS * g + j + 1)
                        dve.reciprocal(inv[:, j % 4, :], rowsum[:, j % 4, :])
                        dve.drain()
                        for t in range(2):
                            c = slice(t * P, t * P + P * (t + 1))
                            last = dve.tensor_scalar(prob[:, j % 4, c], prob[:, j % 4, c], inv[:, j % 4, t:t + 1],
                                                     None, ALU.mult)
                        last.then_inc(probs, 1)
                    j = i - 4
                    if 0 <= j < HEADS and j % 2:
                        b, h = j // H0, j % H0
                        dve.wait_ge(heads, HEADS * g + j + 1)
                        dve.tensor_copy(zt[:, h // 2, b * S:(b + 1) * S], bank[4 + j // 2 % 2][:, 0:S]).then_inc(zcopied, 1)
                for t in range(NT):
                    dve.wait_ge(n1.product, NT * g + t + 1)
                    dve.tensor_tensor(n1.y[:, t, :], bank[6 + t % 2][:, 0:D], xg[:, t, :], ALU.add).then_inc(n1.added, 1)
                    norm_tile_stats(dve, g, n1, t)
                norm_rows(dve, g, n1, lambda t: x1[:, t, :])
                dve.wait_ge(chunk, NCH * g + NCH)
                dve.tensor_scalar(qx[:, 1, :], bank[(NCH - 1) % 4][:, :], bx[:, 1:2], None, ALU.add).then_inc(ev_dve, 1)
                for t in range(NT):
                    dve.drain()
                    dve.wait_ge(xlogit, NT * g + t + 1)
                    dve.sem_inc(alone, 1)
                    dve.tensor_tensor_reduce(out=probx[:, t, :], in0=bank[4 + t % 2][:, 0:S2], in1=maskf[:, t, :],
                                             scale=1.0, scalar=-3e38, op0=ALU.add, op1=ALU.max, accum_out=mxx[:, t:t + 1])
                    dve.drain()
                    dve.tensor_scalar(negx[:, t:t + 1], mxx[:, t:t + 1], -1.0, None, ALU.mult).then_inc(xshift, 1)
                dve.wait_ge(xexp, NT * g + NT)
                dve.reciprocal(invx[:, :], sumx[:, :])
                dve.drain()
                for t in range(NT):
                    dve.wait_ge(n2.product, NT * g + t + 1)
                    dve.scalar_tensor_tensor(n2.y[:, t, :], bank[t % 2][:, 0:D], invx[:, t:t + 1], x1[:, t, :],
                                             ALU.mult, ALU.add).then_inc(n2.added, 1)
                    norm_tile_stats(dve, g, n2, t)
                norm_rows(dve, g, n2, lambda t: x2[:, t, :])
                dve.wait_ge(gmm, g + 1)
                dve.tensor_copy(score8[:, :, :], bank[4][:, 0:NT * NE].rearrange("p (t e) -> p t e", t=NT))
                dve.drain()
                for t in range(NT):
                    dve.max(top8[:, t, :], score8[:, t, :])
                dve.drain()
                for t in range(NT):
                    dve.max_index(at8[:, t, :], top8[:, t, :], score8[:, t, :])
                dve.tensor_tensor(gd[:, :], top8[:, :, 1], top8[:, :, 0], ALU.subtract).then_inc(gdiff, 1)
                dve.drain()
                dve.tensor_copy(at8f[:, :, :], at8[:, :, :])
                dve.wait_ge(gexp, g + 1)
                dve.tensor_scalar(gq[:, :], ge[:, :], 1.0, None, ALU.add)
                dve.drain()
                dve.reciprocal(gp[:, :], gq[:, :])
                dve.drain()
                dve.tensor_tensor(gq[:, :], gp[:, :], ge[:, :], ALU.mult)
                dve.drain()
                for t in range(NT):
                    dve.tensor_scalar(pick0[:, t, :], expert[:, t, :], at8f[:, t, 0:1], gp[:, t:t + 1], ALU.is_equal, ALU.mult)
                    dve.tensor_scalar(pick1[:, t, :], expert[:, t, :], at8f[:, t, 1:2], gq[:, t:t + 1], ALU.is_equal, ALU.mult)
                dve.drain()
                dve.tensor_tensor(pick0[:, :, :], pick0[:, :, :], pick1[:, :, :], ALU.add).then_inc(picked, 1)
                end_of_turn(dve, g, turn, alone)


def expert_layer(nc, dram, memory, keep):
    with ExitStack() as ctx:
        sb = memory.take
        bank = memory.bank

        sem = memory.sem
        alone = memory.alone
        W1, W2 = KD * 2 * FF, FC * D
        w1, w2 = sb([P, NE * W1]), sb([P, NE * W2])
        b1 = sb([P, NE * 2 * FF])
        b2 = sb([NE, D])
        ident, before, ones = sb([P, P]), sb([P, P]), sb([P, P])
        lane, number = sb([P, P]), sb([P, SLOT_TILES])
        expert, token = sb([P, TILES, NE]), sb([P, TILES])
        pickt = sb([NE, TILES, P])
        chosen, both = sb([P, 2, TILES, NE]), sb([P, TILES, NE])
        total = sb([P, TILES + 1, NE])
        length, end, base = sb([P, NE]), sb([P, NE]), sb([P, NE])
        rank, high, low = (sb([P, 2, TILES]) for _ in range(3))
        ranki = sb([P, 2, TILES], I32)
        owner, owneri = sb([P, SLOT_TILES]), sb([P, SLOT_TILES], I32)
        source = sb([P, SLOT_TILES], I32)
        at = sb([P, 2], I32)
        ohlow, ohhigh = sb([P, 4, P]), sb([P, 4, SLOT_TILES])
        rows, rowst = sb([P, 2, D]), sb([P, 2, KD, P])
        gate, value, sig, hidden = (sb([P, FF]) for _ in range(4))
        hiddent = sb([P, FC, P])
        y = sb([P, 2, D])
        back = sb([P, 8, D])
        const, biases, expload, ready = sem("e_const"), sem("e_biases"), [sem("e_load0"), sem("e_load1")], sem("e_ready")
        ptp, ptc, bmm, badd = sem("ptp"), sem("ptc"), sem("bmm"), sem("badd")
        chosens, counts, onehots, placed, sourced = (sem(n) for n in ("chosens", "counts", "onehots", "placed", "sourced"))
        rturned, rcopied = sem("rturned"), sem("rcopied")
        gathered, ystored = ([sem(f"{n}{s}") for s in range(2)] for n in ("gathered", "ystored"))
        upgate, upvalue, clipped, gated, mixed, hready = (sem(n) for n in ("upgate", "upvalue", "clipped", "gated", "mixed", "hready"))
        hturned, hcopied, down, yread = (sem(n) for n in ("hturned", "hcopied", "down", "yread"))
        backed, added = [sem(f"backed{n}") for n in range(8)], sem("added")
        ROUND = 1.5 * 2 ** 23
        BANKG, BANKV, BANKH, BANKY, BANKR = (0, 1), (2, 3), 4, 5, (6, 7)
        block = ctx.enter_context(nc.Block())

        @block.sync
        def _(sp):
            sp.dma_start(b2[:, :], dram["b2"]).then_inc(biases, 16)
            for e in range(NE):
                sp.dma_start(w1[:, e * W1:(e + 1) * W1].rearrange("p (k n) -> p k n", k=KD),
                             dram["w1"].rearrange("e (k p) n -> e p k n", p=P)[e]).then_inc(expload[e % 2], 16)
                sp.dma_start(w2[:, e * W2:(e + 1) * W2].rearrange("p (k n) -> p k n", k=FC),
                             dram["w2"].rearrange("e (k p) n -> e p k n", p=P)[e]).then_inc(expload[e % 2], 16)
                sp.dma_start(b1[:, e * 2 * FF:(e + 1) * 2 * FF],
                             dram["b1"][e:e + 1, :].to_broadcast([P, 2 * FF])).then_inc(expload[e % 2], 16)
                if e >= 1:
                    sp.wait_ge(expload[(e - 1) % 2], 48 * ((e - 1) // 2 + 1))
                    sp.sem_inc(ready, 1)
            sp.wait_ge(expload[(NE - 1) % 2], 48 * ((NE - 1) // 2 + 1))
            sp.sem_inc(ready, 1)

        @block.gpsimd
        def _(pool):
            pool.memset(ident[:, :], 0.0)
            pool.memset(before[:, :], 1.0)
            pool.memset(ones[:, :], 1.0)
            for v, pattern, step in ((lane, [[1, P]], 0), (number, [[1, SLOT_TILES]], 0), (token, [[P, TILES]], 1)):
                pool.iota(v[:, :], pattern=pattern, base=0, channel_multiplier=step, allow_small_or_imprecise_dtypes=True)
            pool.iota(expert[:, :, :], pattern=[[0, TILES], [1, NE]], base=0, channel_multiplier=0,
                      allow_small_or_imprecise_dtypes=True)
            pool.drain()
            pool.affine_select(out=ident[:, :], in_=ident[:, :], compare_op=ALU.not_equal, fill=1.0, base=0,
                               pattern=[[-1, P]], channel_multiplier=1)
            pool.affine_select(out=before[:, :], in_=before[:, :], compare_op=ALU.is_ge, fill=0.0, base=-1,
                               pattern=[[1, P]], channel_multiplier=-1)
            pool.drain()
            pool.nop().then_inc(const, 1)

            def gather(j, s):
                pool.tensor_copy(at[:, s:s + 1], source[:, bass.ds(j, 1)])
                pool.drain()
                pool.indirect_dma_start(rows[:, s, :], None, dram["x2"][:, :],
                                        bass.IndirectOffsetOnAxis(ap=at[:, s:s + 1], axis=0)).then_inc(gathered[s], 16)

            def mix(j):
                pool.wait_ge(gated, j + 1)
                pool.tensor_tensor(sig[:, :], gate[:, :], sig[:, :], ALU.mult).then_inc(mixed, 1)

            pool.wait_ge(sourced, 1)
            gather(0, 0)
            gather(1, 1)
            last = SLOT_TILES - 3
            with pool.Fori(0, last // 2) as i:
                for s in range(2):
                    mix(2 * i + s)
                    gather(2 * i + s + 2, s)
            mix(last)
            gather(SLOT_TILES - 1, last % 2)
            mix(last + 1)
            mix(last + 2)
            for s in range(2):
                pool.wait_ge(ystored[s], 16 * ((SLOT_TILES + 1 - s) // 2))
            for n in range(2 * TILES):
                if n >= 8:
                    pool.wait_ge(added, n - 7)
                pool.indirect_dma_start(back[:, n % 8, :], None, dram["y2"][:, :],
                                        bass.IndirectOffsetOnAxis(ap=ranki[:, n % 2, n // 2:n // 2 + 1], axis=0)).then_inc(backed[n % 8], 16)

        @block.tensor
        def _(pe):
            pe.wait_ge(const, 1)
            pe.wait_ge(chosens, 1)
            pe.matmul(bank[6][:, 0:TILES * NE], before[:, :], both[:, :, :].rearrange("p t e -> p (t e)"), start=True, stop=True)
            pe.matmul(bank[7][:, 0:TILES * NE], ones[:, :], both[:, :, :].rearrange("p t e -> p (t e)"),
                      start=True, stop=True).then_inc(counts, 1)
            for n in range(2 * TILES):
                pe.wait_ge(onehots, n + 1)
                pe.matmul(bank[5][:, 0:SLOT_TILES], ohlow[:, n % 4, :], ohhigh[:, n % 4, :],
                          start=n == 0, stop=n == 2 * TILES - 1).then_inc(placed, 1)

            def turn_rows(i, s):
                pe.wait_ge(gathered[s], 16 * i + 16)
                pe.sem_inc(alone, 1)
                for k in range(KD):
                    last = pe.transpose(bank[BANKR[s]][:, k * P:(k + 1) * P], rows[:, s, k * P:(k + 1) * P], ident[:, :])
                last.then_inc(rturned, 1)

            def up(e, s, half):
                for k in range(KD):
                    last = pe.matmul(bank[(BANKG, BANKV)[half][s]][:, :], rowst[:, s, k, :],
                                     w1[:, bass.ds(e * W1 + k * 2 * FF + half * FF, FF)], start=k == 0, stop=k == KD - 1)
                last.then_inc((upgate, upvalue)[half], 1)

            def start(j):
                e = pe.value_load(owneri[0:1, bass.ds(j, 1)], min_val=0, max_val=NE - 1)
                pe.wait_ge(ready, e + 1)
                pe.sem_inc(alone, 1)
                pe.wait_ge(rcopied, j + 1)
                pe.sem_inc(alone, 1)
                return e

            def step(i, s, ahead=2):
                j = 2 * i + s
                if ahead >= 1:
                    following = start(j + 1)
                    up(following, 1 - s, 0)
                pe.wait_ge(hready, j + 1)
                pe.sem_inc(alone, 1)
                for k in range(FC):
                    last = pe.transpose(bank[BANKH][:, k * P:(k + 1) * P], hidden[:, k * P:(k + 1) * P], ident[:, :])
                last.then_inc(hturned, 1)
                if ahead >= 1:
                    up(following, 1 - s, 1)
                if ahead >= 2:
                    turn_rows(i + 1, s)
                pe.wait_ge(hcopied, j + 1)
                pe.sem_inc(alone, 1)
                pe.wait_ge(yread, j + 1)
                pe.sem_inc(alone, 1)
                e = pe.value_load(owneri[0:1, bass.ds(j, 1)], min_val=0, max_val=NE - 1)
                for k in range(FC):
                    last = pe.matmul(bank[BANKY][:, 0:D], hiddent[:, k, :], w2[:, bass.ds(e * W2 + k * D, D)],
                                     start=k == 0, stop=k == FC - 1)
                last.then_inc(down, 1)

            pe.wait_ge(sourced, 1)
            turn_rows(0, 0)
            turn_rows(0, 1)
            e = start(0)
            up(e, 0, 0)
            up(e, 0, 1)
            tail = (SLOT_TILES - 2) // 2 * 2
            with pe.Fori(0, tail // 2) as i:
                for s in range(2):
                    step(i, s)
            for j in range(tail, SLOT_TILES):
                step(j // 2, j % 2, SLOT_TILES - 1 - j)
            pe.wait_ge(biases, 16)
            for t in range(TILES):
                if t >= 2:
                    pe.wait_ge(ptc, t - 1)
                pe.transpose(bank[t % 2][0:NE, 0:P], keep["pick"][:, t, :], ident[:, :]).then_inc(ptp, 1)
            for t in range(TILES):
                pe.wait_ge(ptc, t + 1)
                if t >= 2:
                    pe.wait_ge(badd, t - 1)
                pe.matmul(bank[2 + t % 2][:, 0:D], pickt[:, t, :], b2[:, :], start=True, stop=True).then_inc(bmm, 1)

        @block.scalar
        def _(act):
            act.nop().then_inc(yread, 1)

            def copy_rows(j, s):
                act.wait_ge(rturned, j + 1)
                act.activation(rowst[:, s, :, :], bank[BANKR[s]][:, 0:D].rearrange("p (k n) -> p k n", k=KD), ACT.Copy).then_inc(rcopied, 1)

            def sigmoid(j):
                act.wait_ge(clipped, j + 1)
                act.activation(sig[:, :], gate[:, :], ACT.Sigmoid, scale=1.702).then_inc(gated, 1)

            def step(i, s, ahead=2, first=False):
                j = 2 * i + s
                act.wait_ge(hturned, j + 1)
                act.activation(hiddent[:, :, :], bank[BANKH][:, :].rearrange("p (k n) -> p k n", k=FC), ACT.Copy).then_inc(hcopied, 1)
                if ahead >= 1:
                    sigmoid(j + 1)
                if ahead >= 2:
                    copy_rows(j + 2, s)
                if not first:
                    act.wait_ge(ystored[s], 16 * i)
                    act.sem_inc(alone, 1)
                act.wait_ge(down, j + 1)
                act.activation(y[:, s, :], bank[BANKY][:, 0:D], ACT.Copy).then_inc(yread, 1)
                act.wait_ge(yread, j + 2)
                act.sem_inc(alone, 1)
                act.dma_start(dram["y2"].rearrange("(j p) n -> p j n", p=P)[:, bass.ds(j, 1), :], y[:, s:s + 1, :]).then_inc(ystored[s], 16)

            copy_rows(0, 0)
            copy_rows(1, 1)
            sigmoid(0)
            step(0, 0, first=True)
            step(0, 1, first=True)
            tail = (SLOT_TILES - 2) // 2 * 2
            with act.Fori(1, tail // 2) as i:
                for s in range(2):
                    step(i, s)
            for j in range(tail, SLOT_TILES):
                step(j // 2, j % 2, SLOT_TILES - 1 - j)
            for t in range(TILES):
                act.wait_ge(ptp, t + 1)
                act.activation(pickt[:, t, :], bank[t % 2][0:NE, 0:P], ACT.Copy).then_inc(ptc, 1)

        @block.vector
        def _(dve):
            dve.wait_ge(const, 1)
            for r in range(2):
                dve.tensor_tensor(chosen[:, r, :, :], expert[:, :, :], keep["at"][:, :, r:r + 1].to_broadcast([P, TILES, NE]), ALU.is_equal)
            dve.memset(total[:, 0, :], 0.0)
            dve.drain()
            dve.tensor_tensor(both[:, :, :], chosen[:, 0, :, :], chosen[:, 1, :, :], ALU.add).then_inc(chosens, 1)
            dve.wait_ge(counts, 1)
            for t in range(TILES):
                dve.tensor_tensor(total[:, t + 1, :], total[:, t, :], bank[7][:, t * NE:(t + 1) * NE], ALU.add)
                dve.drain()
            dve.tensor_scalar(length[:, :], total[:, TILES, :], (P - 1) / 2, 1 / P, ALU.add, ALU.mult)
            dve.drain()
            dve.tensor_scalar(length[:, :], length[:, :], ROUND, None, ALU.add)
            dve.drain()
            dve.tensor_scalar(length[:, :], length[:, :], -ROUND, None, ALU.add)
            dve.drain()
            dve.tensor_tensor_scan(end[:, :], ones[:, 0:NE], length[:, :], 0.0, ALU.mult, ALU.add)
            dve.drain()
            dve.tensor_tensor(base[:, :], end[:, :], length[:, :], ALU.subtract)
            dve.tensor_scalar(owner[:, :], number[:, :], end[:, 0:1], None, ALU.is_ge)
            dve.drain()
            dve.tensor_scalar(base[:, :], base[:, :], float(P), None, ALU.mult)
            for e in range(1, NE - 1):
                dve.drain()
                dve.scalar_tensor_tensor(owner[:, :], number[:, :], end[:, e:e + 1], owner[:, :], ALU.is_ge, ALU.add)
            rest = total[:, 0:TILES, :]
            dve.tensor_tensor(rest, rest, base[:, :].unsqueeze(1).to_broadcast([P, TILES, NE]), ALU.add)
            dve.drain()
            dve.tensor_copy(owneri[:, :], owner[:, :])
            dve.tensor_tensor(rest, rest, bank[6][:, 0:TILES * NE].rearrange("p (t e) -> p t e", t=TILES), ALU.add)
            dve.drain()
            for r in range(2):
                dve.tensor_tensor(chosen[:, r, :, :], chosen[:, r, :, :], rest, ALU.mult)
            dve.drain()
            for r in range(2):
                dve.tensor_reduce(rank[:, r, :], chosen[:, r, :, :], AX.X, ALU.add)
            dve.drain()
            dve.tensor_copy(ranki[:, :, :], rank[:, :, :])
            dve.tensor_scalar(high[:, :, :], rank[:, :, :], -(P - 1) / 2, 1 / P, ALU.add, ALU.mult)
            dve.drain()
            dve.tensor_scalar(high[:, :, :], high[:, :, :], ROUND, None, ALU.add)
            dve.drain()
            dve.tensor_scalar(high[:, :, :], high[:, :, :], -ROUND, None, ALU.add)
            dve.drain()
            dve.scalar_tensor_tensor(low[:, :, :], high[:, :, :], -float(P), rank[:, :, :], ALU.mult, ALU.add)
            dve.drain()
            for n in range(2 * TILES):
                r, t = n % 2, n // 2
                if n >= 4:
                    dve.wait_ge(placed, n - 3)
                dve.tensor_scalar(ohlow[:, n % 4, :], lane[:, :], low[:, r, t:t + 1], None, ALU.is_equal)
                dve.tensor_scalar(ohhigh[:, n % 4, :], number[:, :], high[:, r, t:t + 1], token[:, t:t + 1],
                                  ALU.is_equal, ALU.mult).then_inc(onehots, 1)
            dve.wait_ge(placed, 2 * TILES)
            dve.tensor_copy(source[:, :], bank[5][:, 0:SLOT_TILES]).then_inc(sourced, 1)

            def step(j, s):
                e = dve.value_load(owneri[0:1, bass.ds(j, 1)], min_val=0, max_val=NE - 1)
                dve.drain()
                dve.wait_ge(upgate, j + 1)
                dve.tensor_tensor(gate[:, :], bank[BANKG[s]][:, :], b1[:, bass.ds(e * 2 * FF, FF)], ALU.add)
                dve.drain()
                dve.tensor_scalar(gate[:, :], gate[:, :], 9.0, None, ALU.min).then_inc(clipped, 1)
                dve.wait_ge(upvalue, j + 1)
                dve.tensor_tensor(value[:, :], bank[BANKV[s]][:, :], b1[:, bass.ds(e * 2 * FF + FF, FF)], ALU.add)
                dve.drain()
                dve.tensor_scalar(value[:, :], value[:, :], 9.0, -9.0, ALU.min, ALU.max)
                dve.drain()
                dve.wait_ge(mixed, j + 1)
                dve.scalar_tensor_tensor(hidden[:, :], value[:, :], 1.0, sig[:, :], ALU.add, ALU.mult).then_inc(hready, 1)

            with dve.Fori(0, SLOT_TILES // 2) as i:
                for s in range(2):
                    step(2 * i + s, s)
            step(SLOT_TILES - 1, 0)
            for t in range(TILES):
                dve.wait_ge(bmm, t + 1)
                dve.tensor_tensor(keep["x"][:, t, :], bank[2 + t % 2][:, 0:D], keep["x"][:, t, :], ALU.add).then_inc(badd, 1)
            for n in range(2 * TILES):
                t = n // 2
                dve.drain()
                dve.wait_ge(backed[n % 8], 16 * (n // 8) + 16)
                dve.scalar_tensor_tensor(keep["x"][:, t, :], back[:, n % 8, :], keep["weight"][:, t, n % 2:n % 2 + 1],
                                         keep["x"][:, t, :], ALU.mult, ALU.add).then_inc(added, 1)


def last_layers(nc, dram, memory, keep):
    with ExitStack() as ctx:
        sb = memory.take
        bank = memory.bank

        sem = memory.sem
        alone = memory.alone
        wqk = sb([P, KD, 2 * D])
        wv1, wgate, wpp, wclock, wout = (sb([P, KD, D]) for _ in range(5))
        wm1, wm2 = sb([P, KD, M1]), sb([P, MC, D])
        wxq, wxk, wxv, wxp = (sb([P, KD, D]) for _ in range(4))
        wr, wk2, wv2 = (sb([P, KD, D]) for _ in range(3))
        bm1 = sb([P, MC])
        cols = sb([P, 9, KD])
        BP, BCLK, BGATE, G1, B1, G2, B2, MUR, MUK = range(9)
        unmu = sb([P, 2, KD])
        brow = sb([P, 3, D])
        rope = sb([P, 2, 2 * DH1])
        parity = sb([P, 2])
        ident, minus_half, eps = sb([P, P]), sb([P, NT]), sb([P, NT])
        ones = sb([P, S])
        mask1 = sb([P, CAUSAL])
        maskx = sb([P, 2, HX * S2])
        va = sb([P, NT, H1, 32])
        qf, kf = sb([P, KD, GT]), sb([P, KD, GT])
        qt, kt = sb([P, KD, GT]), sb([P, 2, KD, GT])
        x3, xn, xnt, xb = sb([P, NT, D]), sb([P, NT, D]), sb([P, KD, GT]), sb([P, NT, D])
        ya, yb = sb([P, NT, D]), sb([P, NT, D])
        ss, rn, r2 = sb([P, NT * 32]), sb([P, NT * 32]), sb([P, NT * 32])
        pmax, rden = sb([P, KD * GB]), sb([P, NT, H1])
        xmax, xsum, xinv = (sb([P, NT, HX]) for _ in range(3))
        memt = sb([P, KD, GB * S2])
        region1 = sb([P, 8192 + 4 * (S + 1)])
        region2 = sb([P, 7168])

        fm = cut(region1, 0, (6, GT))
        ee = cut(region1, 3072, (4, GT))
        uu = cut(region1, 5120, (4, GT))
        dd = cut(region1, 7168, (2, GT))
        m1t = cut(region1, 0, (MC, GT))
        sm = cut(region1, 0, (NT, HX * S2))
        pxt = cut(region1, 1920, (GB, HX, S), S2)
        zxt, qxt = cut(region1, 4096, (KD, GT)), cut(region1, 5120, (KD, GT))
        kxt, vx = cut(region1, 6144, (KD, GB * S2)), cut(region1, 6624, (GB, D), S2)
        xr, xk, rs, rl = (cut(region1, 1024 * i, (2, 512)) for i in range(4))
        rs = cut(region1, 2048, (NT, D))
        shift, ka = cut(region1, 4096, (KD, GT)), cut(region1, 5120, (KD, GT))
        x5 = cut(region1, 7168, (NT, D))
        x5t = cut(region1, 8192, (KD, GB, S + 1))
        xo = xb
        sq, qn = cut(region2, 0, (2, 512)), cut(region2, 1024, (NT, 512))
        ra, rb = cut(region2, 3072, (NT, 512)), cut(region2, 5120, (NT, 512))
        es, ut = cut(region2, 0, (4, CAUSAL)), cut(region2, 1536, (4, GT))
        og, ogt = cut(region2, 3584, (NT, D)), cut(region2, 4608, (KD, GT))
        h5, h5t, x4, x4t = xn, xnt, x3, xnt

        weights, rows, loaded, const, turn, stored = (sem(f"l_{n}") for n in ("weights", "rows", "loaded", "const", "turn", "stored"))
        qkmm, vmm, vcop, fmm, fmread, sqd, sqred, ssready, rnr = (sem(n) for n in ("qkmm", "vmm", "vcop", "fmm", "fmread", "sqd", "sqred", "ssready", "rnr"))
        qnr, rar, roped, eready, uready, lready, npm, pexp, clr, gcr = (sem(n) for n in ("qnr", "rar", "roped", "eready", "uready", "lready", "npm", "pexp", "clr", "gcr"))
        qktp, qkt, s1, s1m, s1e, av1, utc, ttp, ogr, ogtp, ogc = (sem(n) for n in ("qktp", "qkt", "s1", "s1m", "s1e", "av1", "utc", "ttp", "ogr", "ogtp", "ogc"))
        biased, m1mm, m1g = (sem(n) for n in ("biased", "m1mm", "m1g"))
        xq, xqr, xkm, xkr, xvm, xvr, xs, xsr, xsub, xe, xp, xtp, xtc, xav, xz = (sem("l_" + n) for n in (
            "xq", "xqr", "xkm", "xkr", "xvm", "xvr", "xs", "xsr", "xsub", "xe", "xp", "xtp", "xtc", "xav", "xz"))
        mixk, mixr, kmm, relu, kact, rmm, rsig = (sem(n) for n in ("mixk", "mixr", "kmm", "relu", "kact", "rmm", "rsig"))
        n3, n4 = Norm(memory, "n3", ya, product=False, turned=False), Norm(memory, "n4", x3, product=False)
        n5, n6, n7 = (Norm(memory, n, y) for n, y in (("n5", yb), ("n6", ya), ("n7", yb)))
        n8 = Norm(memory, "n8", ya, turned=False)
        HEADS = GB * H1
        NW, NR = 17, 3
        block = ctx.enter_context(nc.Block())

        def tok(t):
            return slice(t * P, (t + 1) * P)

        @block.sync
        def _(sp):
            for dst, src in ((wqk, "wqk"), (wv1, "wv1"), (wgate, "wgate"), (wpp, "wpp"), (wclock, "wclock"), (wout, "wout"),
                             (wm1, "wm1"), (wm2, "wm2"), (wxq, "wxq"), (wxk, "wxk"), (wxv, "wxv"), (wxp, "wxp"),
                             (wr, "wr"), (wk2, "wk2"), (wv2, "wv2")):
                sp.dma_start(dst[:, :, :], dram[src].rearrange("(k p) n -> p k n", p=P)).then_inc(weights, 16)
            sp.dma_start(bm1[:, :], dram["bm1"]).then_inc(weights, 16)
            sp.dma_start(cols[:, :, :], dram["cols"]).then_inc(weights, 16)
            sp.dma_start(rope[:, :, :], dram["rope"]).then_inc(rows, 16)
            sp.dma_start(parity[:, :], dram["parity"]).then_inc(rows, 16)
            sp.dma_start(brow[:, :, :], dram["rows"].rearrange("(o r) n -> o r n", o=1).to_broadcast([P, 3, D])).then_inc(rows, 16)
            with sp.Fori(0, G) as g:
                for b in range(GB):
                    sp.dma_start(memt[:, :, b * S2:(b + 1) * S2], dram["ctxt"].rearrange("(g b) (k p) s -> g b p k s", b=GB, p=P)[g, b]).then_inc(loaded, 16)
                sp.wait_ge(n8.normed, NT * g + NT)
                sp.dma_start(dram["out"].rearrange("(g t p) n -> g p t n", p=P, t=NT)[g], xo[:, :, :]).then_inc(stored, 16)
                sp.wait_ge(stored, 16 * g + 16)
                sp.sem_inc(alone, 1)
                end_of_turn(sp, g, turn, alone)

        @block.gpsimd
        def _(pool):
            pool.memset(ident[:, :], 0.0)
            pool.memset(minus_half[:, :], -0.5)
            pool.memset(eps[:, :], EPS)
            pool.memset(ones[:, :], 1.0)
            pool.memset(mask1[:, :], 3e38)
            pool.memset(maskx[:, :, :], 0.0)
            pool.memset(va[:, :, :, :], 0.0)
            pool.drain()
            pool.memset(va[:, :, :, DH1:DH1 + 1], 1.0)
            pool.affine_select(out=ident[:, :], in_=ident[:, :], compare_op=ALU.not_equal, fill=1.0, base=0,
                               pattern=[[-1, P]], channel_multiplier=1)
            for c in (0, S):
                pool.affine_select(out=mask1[:, c:c + P], in_=mask1[:, c:c + P], compare_op=ALU.is_ge,
                                   fill=-1e30, base=0, pattern=[[1, P]], channel_multiplier=-1)
            for h in range(HX):
                mh = maskx[:, 0, h * S2:(h + 1) * S2]
                pool.affine_select(out=mh, in_=mh, compare_op=ALU.is_ge, fill=-8e13, base=0,
                                   pattern=[[-1, S2]], channel_multiplier=1)
            pool.drain()
            pool.nop().then_inc(const, 1)
            pool.wait_ge(rows, NR * 16)

            def add_rows(g, src, r):
                for t in range(NT):
                    last = pool.tensor_tensor(xb[:, t, :], src[:, t, :], brow[:, r, :], ALU.add)
                return last

            with pool.Fori(0, G) as g:
                norm_rstd(pool, g, n3, eps[:, :], minus_half[:, 0:NT])
                norm_rstd(pool, g, n4, eps[:, :], minus_half[:, 0:NT])
                pool.wait_ge(n3.normed, NT * g + NT)
                add_rows(g, x3, 0).then_inc(biased, 1)
                for t in range(NT):
                    pool.wait_ge(qnr, NT * g + t + 1)
                    pool.tensor_tensor(ra[:, t, :].rearrange("p (h d) -> p h d", d=DH1),
                                       qn[:, t, :].rearrange("p (h d) -> p h d", d=DH1),
                                       rope[:, t % 2:t % 2 + 1, 0:DH1].to_broadcast([P, 32, DH1]), ALU.mult).then_inc(rar, 1)
                norm_rstd(pool, g, n5, eps[:, :], minus_half[:, 0:NT])
                pool.drain()
                add_rows(g, x3, 1)
                pool.drain()
                pool.tensor_tensor(xb[:, :, :], xb[:, :, :], yb[:, :, :], ALU.add).then_inc(biased, 1)
                norm_rstd(pool, g, n6, eps[:, :], minus_half[:, 0:NT])
                pool.drain()
                pool.wait_ge(n6.normed, NT * g + NT)
                add_rows(g, x4, 2).then_inc(biased, 1)
                norm_rstd(pool, g, n7, eps[:, :], minus_half[:, 0:NT])
                norm_rstd(pool, g, n8, eps[:, :], minus_half[:, 0:NT])
                pool.wait_ge(stored, 16 * g + 16)
                pool.sem_inc(alone, 1)
                end_of_turn(pool, g, turn, alone)

        @block.tensor
        def _(pe):
            def product(out, pairs):
                for i, (w, r) in enumerate(pairs):
                    last = pe.matmul(out, w, r, start=i == 0, stop=i == len(pairs) - 1)
                return last

            pe.wait_ge(weights, NW * 16)
            pe.wait_ge(const, 1)
            with pe.Fori(0, G) as g:
                norm_turn(pe, g, n4, lambda t: xn[:, t, :], bank[6:8], ident[:, :])
                for t in range(NT):
                    pe.wait_ge(n4.copied, NT * g + t + 1)
                    product(bank[t][:, :], [(xnt[:, k, tok(t)], wqk[:, k, :]) for k in range(KD)]).then_inc(qkmm, 1)
                for c in range(6):
                    if c >= 2:
                        pe.wait_ge(fmread, 6 * g + c - 1)
                    w = (wpp, wclock, wgate)[c // 2]
                    product(bank[6 + c % 2][:, :], [(w[:, k, tok(c % 2)], xnt[:, k, :]) for k in range(KD)]).then_inc(fmm, 1)
                for t in range(NT):
                    if t >= 2:
                        pe.wait_ge(vcop, NT * g + t - 1)
                    product(bank[4 + t % 2][:, 0:D], [(xnt[:, k, tok(t)], wv1[:, k, :]) for k in range(KD)]).then_inc(vmm, 1)
                for t in range(NT):
                    pe.wait_ge(roped, NT * g + t + 1)
                    for c in range(4):
                        last = pe.transpose(bank[t][:, tok(c)], rb[:, t, tok(c)], ident[:, :])
                    last.then_inc(qktp, 1)
                pe.wait_ge(qkt, NT * g + NT)
                for i in range(HEADS + 2):
                    if i < HEADS:
                        b, h = i // H1, i % H1
                        m, r = h // 8, slice(32 * (h % 8 // 2), 32 * (h % 8 // 2) + 32)
                        if i >= 2:
                            pe.wait_ge(s1m, HEADS * g + i - 1)
                        pe.matmul(bank[i % 2][:, 0:S], kt[r, h % 2, m, b * S:b * S + P],
                                  qt[r, m, b * S:(b + 1) * S], start=True, stop=True)
                        pe.matmul(bank[i % 2][:, S:S + P], kt[r, h % 2, m, b * S + P:(b + 1) * S],
                                  qt[r, m, b * S + P:(b + 1) * S], start=True, stop=True).then_inc(s1, 1)
                    j = i - 2
                    if j >= 0:
                        b, h = j // H1, j % H1
                        pe.wait_ge(s1e, HEADS * g + j + 1)
                        if j == 0:
                            pe.wait_ge(vcop, NT * g + NT)
                        if j % 4 == 0 and j >= 8:
                            pe.wait_ge(utc, HEADS // 4 * g + j // 4 - 1)
                        o = bank[4 + j // 4 % 2][32 * (h % 4):32 * (h % 4) + 32, :]
                        pe.matmul(o[:, 0:S], va[:, 2 * b, h, :], es[:, j % 4, 0:S], start=True, stop=False)
                        pe.matmul(o[:, P:S], va[:, 2 * b + 1, h, :], es[:, j % 4, S:S + P],
                                  start=False, stop=True).then_inc(av1, 1)
                pe.wait_ge(utc, HEADS // 4 * (g + 1))
                for t in range(NT + 1):
                    if t < NT:
                        if t >= 2:
                            pe.wait_ge(ogr, NT * g + t - 1)
                        for c in range(4):
                            last = pe.transpose(bank[2 + t % 2][:, tok(c)], ut[:, c, tok(t)], ident[:, :])
                        last.then_inc(ttp, 1)
                    if t >= 1:
                        j = t - 1
                        pe.wait_ge(ogr, NT * g + j + 1)
                        if j >= 2:
                            pe.wait_ge(ogc, NT * g + j - 1)
                        for k in range(KD):
                            last = pe.transpose(bank[6 + j % 2][:, tok(k)], og[:, j, tok(k)], ident[:, :])
                        last.then_inc(ogtp, 1)
                for t in range(NT):
                    pe.wait_ge(ogc, NT * g + t + 1)
                    if t >= 2:
                        pe.wait_ge(n5.added, NT * g + t - 1)
                    product(bank[4 + t % 2][:, 0:D], [(ogt[:, k, tok(t)], wout[:, k, :]) for k in range(KD)]).then_inc(n5.product, 1)
                norm_turn(pe, g, n5, lambda t: h5[:, t, :], bank[2:4], ident[:, :])
                pe.wait_ge(n5.copied, NT * g + NT)
                for c in range(MC):
                    if c >= 4:
                        pe.wait_ge(m1g, MC * g + c - 3)
                    product(bank[(0, 1, 4, 5)[c % 4]][:, :], [(wm1[:, k, tok(c)], h5t[:, k, :]) for k in range(KD)]).then_inc(m1mm, 1)
                pe.wait_ge(m1g, MC * g + MC)
                for t in range(NT):
                    if t >= 2:
                        pe.wait_ge(n6.added, NT * g + t - 1)
                    product(bank[6 + t % 2][:, 0:D], [(m1t[:, k, tok(t)], wm2[:, k, :]) for k in range(MC)]).then_inc(n6.product, 1)
                pe.wait_ge(loaded, 32 * g + 32)
                for c in range(KD):
                    product(bank[4 + c][:, 0:GB * S2], [(wxk[:, k, tok(c)], memt[:, k, :]) for k in range(KD)]).then_inc(xkm, 1)
                norm_turn(pe, g, n6, lambda t: x4[:, t, :], bank[2:4], ident[:, :])
                for b in range(GB):
                    product(bank[6 + b][0:S2, 0:D], [(memt[:, k, b * S2:(b + 1) * S2], wxv[:, k, :]) for k in range(KD)]).then_inc(xvm, 1)
                pe.wait_ge(n6.copied, NT * g + NT)
                for c in range(KD):
                    product(bank[c][:, :], [(wxq[:, k, tok(c)], x4t[:, k, :]) for k in range(KD)]).then_inc(xq, 1)
                pe.wait_ge(xqr, KD * g + KD)
                pe.wait_ge(xkr, KD * g + KD)
                for t in range(NT + 1):
                    if t < NT:
                        if t >= 2:
                            pe.wait_ge(xsr, NT * g + t - 1)
                        for h in range(HX):
                            r = slice(DHX * (h % 2), DHX * (h % 2) + DHX)
                            last = pe.matmul(bank[t % 2 + 2 * (h % 2)][:, h // 2 * S2:(h // 2 + 1) * S2], qxt[r, h // 2, tok(t)],
                                             kxt[r, h // 2, t // 2 * S2:(t // 2 + 1) * S2], start=True, stop=True)
                        last.then_inc(xs, 1)
                    if t >= 1:
                        j = t - 1
                        pe.wait_ge(xp, NT * g + j + 1)
                        if j >= 2:
                            pe.wait_ge(xtc, NT * g + j - 1)
                        for h in range(HX):
                            last = pe.transpose(bank[4 + j % 2][0:S2, tok(h)], sm[:, j, h * S2:(h + 1) * S2], ident[:, :])
                        last.then_inc(xtp, 1)
                pe.wait_ge(xtc, NT * g + NT)
                pe.wait_ge(xvr, GB * g + GB)
                for q in range(GB * KD):
                    b, m = q // KD, q % KD
                    if q >= 2:
                        pe.wait_ge(xz, 4 * g + q - 1)
                    for hh in range(2):
                        h = 2 * m + hh
                        last = pe.matmul(bank[6 + q % 2][DHX * hh:DHX * (hh + 1), 0:S], vx[:, b, h * DHX:(h + 1) * DHX],
                                         pxt[:, b, h, :], start=True, stop=True)
                    last.then_inc(xav, 1)
                pe.wait_ge(xz, 4 * g + 4)
                for t in range(NT):
                    if t >= 2:
                        pe.wait_ge(n7.added, NT * g + t - 1)
                    product(bank[t % 2][:, 0:D], [(zxt[:, k, tok(t)], wxp[:, k, :]) for k in range(KD)]).then_inc(n7.product, 1)
                norm_turn(pe, g, n7, lambda t: x5[:, t, :], bank[2:4], ident[:, :])
                pe.wait_ge(mixk, g + 1)
                for c in range(KD):
                    product(bank[c][:, :], [(wk2[:, k, tok(c)], xk[:, k, :]) for k in range(KD)]).then_inc(kmm, 1)
                pe.wait_ge(mixr, g + 1)
                for t in range(NT):
                    if t >= 2:
                        pe.wait_ge(rsig, NT * g + t - 1)
                    product(bank[4 + t % 2][:, 0:D], [(xr[:, k, tok(t)], wr[:, k, :]) for k in range(KD)]).then_inc(rmm, 1)
                pe.wait_ge(kact, KD * g + KD)
                for t in range(NT):
                    if t >= 2:
                        pe.wait_ge(n8.added, NT * g + t - 1)
                    product(bank[6 + t % 2][:, 0:D], [(ka[:, k, tok(t)], wv2[:, k, :]) for k in range(KD)]).then_inc(n8.product, 1)
                end_of_turn(pe, g, turn, alone)

        @block.scalar
        def _(act):
            act.wait_ge(weights, NW * 16)

            def affine_copy(g, n, banks, gain, bias):
                for t in range(NT):
                    act.wait_ge(n.turned, NT * g + t + 1)
                    for k in range(KD):
                        last = act.activation(xnt[:, k, tok(t)], banks[t % 2][:, tok(k)], ACT.Identity,
                                              bias=cols[:, bias, k:k + 1], scale=cols[:, gain, k:k + 1])
                    last.then_inc(n.copied, 1)

            with act.Fori(0, G) as g:
                affine_copy(g, n4, bank[6:8], G1, B1)
                for t in range(NT):
                    act.wait_ge(qkmm, NT * g + t + 1)
                    if t >= 2:
                        act.wait_ge(sqred, NT * g + t - 1)
                    act.activation(sq[:, t % 2, :], bank[t][:, :], ACT.Square).then_inc(sqd, 1)
                for c in range(6):
                    act.wait_ge(fmm, 6 * g + c + 1)
                    act.activation(fm[:, c, :], bank[6 + c % 2][:, :], ACT.Identity,
                                   bias=cols[:, (BP, BCLK, BGATE)[c // 2], c % 2:c % 2 + 1]).then_inc(fmread, 1)
                act.drain()
                act.activation(ee, fm[:, 2:6, :], ACT.Abs)
                act.drain()
                act.activation(ee, ee, ACT.Exp, scale=-1.0).then_inc(eready, 1)
                for t in range(NT):
                    act.wait_ge(vmm, NT * g + t + 1)
                    act.activation(va[:, t, :, 0:DH1], bank[4 + t % 2][:, 0:D].rearrange("p (h d) -> p h d", d=DH1),
                                   ACT.Copy).then_inc(vcop, 1)
                act.wait_ge(ssready, g + 1)
                act.activation(rn[:, :], ss[:, :], ACT.Sqrt).then_inc(rnr, 1)
                act.wait_ge(npm, g + 1)
                for c in range(KD * GB):
                    pc = fm[:, c // GB, c % GB * S:(c % GB + 1) * S]
                    last = act.activation(pc, pc, ACT.Exp, bias=pmax[:, c:c + 1])
                last.then_inc(pexp, 1)
                act.wait_ge(uready, g + 1)
                act.activation(uu, uu, ACT.Ln).then_inc(lready, 1)
                act.wait_ge(clr, g + 1)
                act.activation(uu[:, 2:4, :], ee[:, 2:4, :], ACT.Exp, scale=-1.0).then_inc(gcr, 1)
                for i in range(HEADS):
                    act.wait_ge(s1m, HEADS * g + i + 1)
                    act.activation(es[:, i % 4, :], es[:, i % 4, :], ACT.Exp, scale=DH1 ** -0.5).then_inc(s1e, 1)
                for t in range(NT):
                    act.wait_ge(ogtp, NT * g + t + 1)
                    act.activation(ogt[:, :, tok(t)], bank[6 + t % 2][:, 0:D].rearrange("p (k n) -> p k n", k=KD),
                                   ACT.Copy).then_inc(ogc, 1)
                affine_copy(g, n5, bank[2:4], G2, B2)
                for c in range(MC):
                    act.wait_ge(m1mm, MC * g + c + 1)
                    act.activation(m1t[:, c, :], bank[(0, 1, 4, 5)[c % 4]][:, :], ACT.Gelu, bias=bm1[:, c:c + 1]).then_inc(m1g, 1)
                norm_copy(act, g, n6, bank[2:4], lambda t: x4t[:, :, tok(t)])
                for b in range(GB):
                    act.wait_ge(xvm, GB * g + b + 1)
                    act.activation(vx[:, b, :], bank[6 + b][0:S2, 0:D], ACT.Copy).then_inc(xvr, 1)
                for c in range(KD):
                    act.wait_ge(xq, KD * g + c + 1)
                    act.activation(qxt[:, c, :], bank[c][:, :], ACT.Copy).then_inc(xqr, 1)
                for t in range(NT + 1):
                    if t < NT:
                        act.wait_ge(xsub, NT * g + t + 1)
                        act.activation(sm[:, t, :], sm[:, t, :], ACT.Exp, scale=DHX ** -0.5).then_inc(xe, 1)
                    if t >= 1:
                        j = t - 1
                        act.wait_ge(xtp, NT * g + j + 1)
                        act.activation(pxt[:, j // 2, :, tok(j % 2)], bank[4 + j % 2][0:S2, :].rearrange("p (h n) -> p h n", h=HX),
                                       ACT.Copy).then_inc(xtc, 1)
                norm_copy(act, g, n7, bank[2:4], lambda t: x5t[:, :, t // 2, 1 + t % 2 * P:1 + (t % 2 + 1) * P])
                for c in range(KD):
                    act.wait_ge(kmm, KD * g + c + 1)
                    act.activation(rl[:, c, :], bank[c][:, :], ACT.Relu).then_inc(relu, 1)
                for t in range(NT):
                    act.wait_ge(rmm, NT * g + t + 1)
                    act.activation(rs[:, t, :], bank[4 + t % 2][:, 0:D], ACT.Sigmoid).then_inc(rsig, 1)
                end_of_turn(act, g, turn, alone)

        @block.vector
        def _(dve):
            dve.wait_ge(weights, NW * 16)
            dve.wait_ge(rows, NR * 16)
            dve.wait_ge(const, 1)
            dve.tensor_scalar(unmu[:, :, :], cols[:, MUR:MUK + 1, :], -1.0, 1.0, ALU.mult, ALU.add)

            def add_product(g, n, banks):
                for t in range(NT):
                    dve.wait_ge(n.product, NT * g + t + 1)
                    dve.tensor_tensor(n.y[:, t, :], banks[t % 2][:, 0:D], xb[:, t, :], ALU.add).then_inc(n.added, 1)
                    norm_tile_stats(dve, g, n, t)

            with dve.Fori(0, G) as g:
                dve.tensor_copy(n3.y[:, :, :], keep["x"][:, bass.ts(g, NT), :])
                for t in range(NT):
                    norm_tile_stats(dve, g, n3, t)
                norm_rows(dve, g, n3, lambda t: x3[:, t, :])
                for t in range(NT):
                    norm_tile_stats(dve, g, n4, t)
                norm_rows(dve, g, n4, lambda t: xn[:, t, :])
                for t in range(NT):
                    dve.wait_ge(sqd, NT * g + t + 1)
                    dve.tensor_reduce(ss[:, t * 32:(t + 1) * 32], sq[:, t % 2, :].rearrange("p (h d) -> p h d", d=DH1),
                                      AX.X, ALU.add).then_inc(sqred, 1)
                dve.drain()
                dve.tensor_scalar(ss[:, :], ss[:, :], 1e-24, None, ALU.max).then_inc(ssready, 1)
                dve.wait_ge(fmread, 6 * g + 2)
                dve.tensor_reduce(pmax[:, :], fm[:, 0:2, :].rearrange("p m (b s) -> p (m b) s", b=GB), AX.X, ALU.max)
                dve.drain()
                dve.tensor_scalar(pmax[:, :], pmax[:, :], -1.0, None, ALU.mult).then_inc(npm, 1)
                dve.wait_ge(eready, g + 1)
                dve.tensor_scalar(uu, ee, 1.0, None, ALU.add)
                dve.drain()
                dve.tensor_scalar(dd, uu[:, 0:2, :], -1.0, None, ALU.add).then_inc(uready, 1)
                dve.wait_ge(rnr, g + 1)
                dve.reciprocal(rn[:, :], rn[:, :])
                dve.drain()
                dve.tensor_tensor(r2[:, :], rn[:, :], rn[:, :], ALU.mult)
                dve.drain()
                dve.tensor_tensor(r2[:, :], r2[:, :], ss[:, :], ALU.mult)
                dve.drain()
                dve.tensor_scalar(r2[:, :], r2[:, :], -0.5, 1.5, ALU.mult, ALU.add)
                dve.drain()
                dve.tensor_tensor(rn[:, :], rn[:, :], r2[:, :], ALU.mult)
                dve.drain()
                for t in range(NT):
                    dve.tensor_tensor(qn[:, t, :].rearrange("p (h d) -> p h d", d=DH1),
                                      bank[t][:, :].rearrange("p (h d) -> p h d", d=DH1),
                                      rn[:, t * 32:(t + 1) * 32].unsqueeze(2).to_broadcast([P, 32, DH1]), ALU.mult).then_inc(qnr, 1)
                dve.drain()
                for t in range(NT):
                    q4 = qn[:, t, :].rearrange("p (h d two) -> p h d two", d=DH1 // 2, two=2)
                    r4 = rb[:, t, :].rearrange("p (h d two) -> p h d two", d=DH1 // 2, two=2)
                    for o in range(2):
                        dve.tensor_tensor(r4[:, :, :, o], q4[:, :, :, 1 - o],
                                          rope[:, t % 2:t % 2 + 1, DH1 + 8 * o:DH1 + 8 * o + 8].to_broadcast([P, 32, 8]), ALU.mult)
                for t in range(NT):
                    dve.drain()
                    dve.wait_ge(rar, NT * g + t + 1)
                    dve.tensor_tensor(rb[:, t, :], rb[:, t, :], ra[:, t, :], ALU.add).then_inc(roped, 1)
                dve.tensor_tensor(dd, ee[:, 0:2, :], dd, ALU.subtract)
                dve.wait_ge(lready, g + 1)
                dve.scalar_tensor_tensor(fm[:, 4:6, :], fm[:, 4:6, :], 0.0, uu[:, 2:4, :], ALU.max, ALU.add)
                dve.drain()
                for m in range(KD):
                    for b in range(GB):
                        dve.tensor_tensor_scan(ee[:, 2 + m, b * S:(b + 1) * S], ones[:, :], fm[:, 4 + m, b * S:(b + 1) * S],
                                               0.0, ALU.mult, ALU.add)
                dve.drain()
                dve.tensor_scalar(ee[:, 2:4, :], ee[:, 2:4, :], -50.0, 60.0, ALU.max, ALU.min).then_inc(clr, 1)
                dve.scalar_tensor_tensor(fm[:, 2:4, :], fm[:, 2:4, :], 0.0, uu[:, 0:2, :], ALU.max, ALU.add)
                dve.drain()
                dve.tensor_tensor(fm[:, 2:4, :], fm[:, 2:4, :], dd, ALU.add)
                dve.drain()
                dve.wait_ge(pexp, g + 1)
                dve.tensor_tensor(fm[:, 0:2, :], fm[:, 0:2, :], fm[:, 2:4, :], ALU.mult)
                dve.drain()
                for m in range(KD):
                    for b in range(GB):
                        dve.tensor_tensor_scan(dd[:, m, b * S:(b + 1) * S], ones[:, :], fm[:, m, b * S:(b + 1) * S],
                                               0.0, ALU.mult, ALU.add)
                dve.drain()
                dve.tensor_scalar(qf[:, :, :], dd, 1e-8, None, ALU.add)
                dve.drain()
                dve.reciprocal(qf[:, :, :], qf[:, :, :])
                dve.drain()
                dve.wait_ge(gcr, g + 1)
                dve.tensor_tensor(qf[:, :, :], qf[:, :, :], uu[:, 2:4, :], ALU.mult)
                dve.tensor_scalar(kf[:, :, :], uu[:, 2:4, :], 1e-8, None, ALU.add)
                dve.drain()
                dve.reciprocal(kf[:, :, :], kf[:, :, :])
                dve.drain()
                dve.tensor_tensor(kf[:, :, :], kf[:, :, :], fm[:, 0:2, :], ALU.mult)
                dve.drain()
                for t in range(NT):
                    dve.wait_ge(qktp, NT * g + t + 1)
                    qk = bank[t][:, :].rearrange("p (c n) -> p c n", c=4)
                    dve.tensor_tensor(qt[:, :, tok(t)], qk[:, 0:2, :], qf[:, :, tok(t)], ALU.mult)
                    for o in range(2):
                        last = dve.scalar_tensor_tensor(kt[:, o, :, tok(t)], qk[:, 2:4, :], parity[:, o:o + 1], kf[:, :, tok(t)],
                                                        ALU.mult, ALU.mult)
                    last.then_inc(qkt, 1)
                for i in range(HEADS + 3):
                    if i < HEADS:
                        dve.wait_ge(s1, HEADS * g + i + 1)
                        if i >= 4:
                            dve.wait_ge(av1, HEADS * g + i - 3)
                        dve.tensor_tensor(es[:, i % 4, :], bank[i % 2][:, 0:CAUSAL], mask1[:, :], ALU.min).then_inc(s1m, 1)
                    j = i - 3
                    if j >= 0 and j % 4 == 3:
                        q = j // 4
                        dve.wait_ge(av1, HEADS * g + j + 1)
                        dve.tensor_copy(ut[:, q % 4, q // 4 * S:(q // 4 + 1) * S], bank[4 + q % 2][:, 0:S]).then_inc(utc, 1)
                for t in range(NT):
                    dve.wait_ge(ttp, NT * g + t + 1)
                    heads = bank[2 + t % 2][:, :].rearrange("p (h d) -> p h d", d=32)
                    dve.reciprocal(rden[:, t, :], heads[:, :, DH1])
                    dve.drain()
                    dve.tensor_tensor(og[:, t, :].rearrange("p (h d) -> p h d", d=DH1), heads[:, :, 0:DH1],
                                      rden[:, t, :].unsqueeze(2).to_broadcast([P, H1, DH1]), ALU.mult).then_inc(ogr, 1)
                dve.wait_ge(biased, 3 * g + 1)
                add_product(g, n5, bank[4:6])
                norm_rows(dve, g, n5, lambda t: h5[:, t, :])
                dve.wait_ge(biased, 3 * g + 2)
                add_product(g, n6, bank[6:8])
                for c in range(KD):
                    dve.wait_ge(xkm, KD * g + c + 1)
                    dve.tensor_copy(kxt[:, c, :], bank[4 + c][:, 0:GB * S2]).then_inc(xkr, 1)
                norm_rows(dve, g, n6, lambda t: x4[:, t, :])
                for t in range(NT + 1):
                    if t < NT:
                        dve.wait_ge(xs, NT * g + t + 1)
                        for o in range(2):
                            last = dve.tensor_tensor(sm[:, t, :].rearrange("p (h two n) -> p h two n", two=2, n=S2)[:, :, o, :],
                                                     bank[t % 2 + 2 * o][:, 0:2 * S2].rearrange("p (h n) -> p h n", n=S2),
                                                     maskx[:, t % 2, 0:2 * S2].rearrange("p (h n) -> p h n", n=S2), ALU.add)
                        last.then_inc(xsr, 1)
                        dve.drain()
                        s3 = sm[:, t, :].rearrange("p (h n) -> p h n", h=HX)
                        dve.tensor_reduce(xmax[:, t, :], s3, AX.X, ALU.max)
                        dve.drain()
                        dve.tensor_tensor(s3, s3, xmax[:, t, :].unsqueeze(2).to_broadcast([P, HX, S2]), ALU.subtract).then_inc(xsub, 1)
                    if t >= 1:
                        j = t - 1
                        s3 = sm[:, j, :].rearrange("p (h n) -> p h n", h=HX)
                        dve.wait_ge(xe, NT * g + j + 1)
                        dve.tensor_reduce(xsum[:, j, :], s3, AX.X, ALU.add)
                        dve.drain()
                        dve.reciprocal(xinv[:, j, :], xsum[:, j, :])
                        dve.drain()
                        dve.tensor_tensor(s3, s3, xinv[:, j, :].unsqueeze(2).to_broadcast([P, HX, S2]), ALU.mult).then_inc(xp, 1)
                for q in range(GB * KD):
                    dve.wait_ge(xav, 4 * g + q + 1)
                    dve.tensor_copy(zxt[:, q % KD, q // KD * S:(q // KD + 1) * S], bank[6 + q % 2][:, 0:S]).then_inc(xz, 1)
                dve.wait_ge(biased, 3 * g + 3)
                add_product(g, n7, bank[0:2])
                norm_rows(dve, g, n7, lambda t: x5[:, t, :])
                dve.memset(x5t[:, :, :, 0:1], 0.0)
                dve.drain()
                dve.wait_ge(n7.copied, NT * g + NT)
                for mu, dst, done in ((MUK, xk, mixk), (MUR, xr, mixr)):
                    for k in range(KD):
                        dve.tensor_scalar(shift[:, k, :].rearrange("p (b s) -> p b s", b=GB), x5t[:, k, :, 0:S],
                                          unmu[:, mu - MUR, k:k + 1], None, ALU.mult)
                    dve.drain()
                    for k in range(KD):
                        last = dve.scalar_tensor_tensor(dst[:, k, :].rearrange("p (b s) -> p b s", b=GB), x5t[:, k, :, 1:S + 1],
                                                        cols[:, mu, k:k + 1], shift[:, k, :].rearrange("p (b s) -> p b s", b=GB),
                                                        ALU.mult, ALU.add)
                    last.then_inc(done, 1)
                    dve.drain()
                for c in range(KD):
                    dve.wait_ge(relu, KD * g + c + 1)
                    dve.tensor_tensor(ka[:, c, :], bank[c][:, :], rl[:, c, :], ALU.mult).then_inc(kact, 1)
                dve.wait_ge(rsig, NT * g + NT)
                for t in range(NT):
                    dve.wait_ge(n8.product, NT * g + t + 1)
                    dve.tensor_tensor(rs[:, t, :], bank[6 + t % 2][:, 0:D], rs[:, t, :], ALU.mult).then_inc(n8.added, 1)
                    dve.drain()
                    dve.tensor_tensor(n8.y[:, t, :], rs[:, t, :], x5[:, t, :], ALU.add)
                    norm_tile_stats(dve, g, n8, t)
                norm_rows(dve, g, n8, lambda t: xo[:, t, :])
                end_of_turn(dve, g, turn, alone)


def decoder(nc, dram):
    with ExitStack() as ctx:
        memory = Memory(nc, ctx)
        keep = {"x": memory.take([P, TILES, D])}
        last = memory.mark
        keep["pick"] = memory.take([P, TILES, NE])
        keep["at"] = memory.take([P, TILES, 2])
        keep["weight"] = memory.take([P, TILES, 2])
        first = memory.mark
        attention_layers(nc, dram, memory, keep)
        memory.mark = first
        memory.clear()
        expert_layer(nc, dram, memory, keep)
        memory.mark = last
        last_layers(nc, dram, memory, keep)


def laid_out(a):
    def t(x):
        return x.T

    def columns(v):
        return v.reshape(-1, P).T

    w1, b1 = a["L0_ffn_dense_1_w"], a["L0_ffn_dense_1_b"]
    x = a["x"].reshape(B * S, D)
    half = DH1 // 2
    freqs = np.exp(-np.arange(half, dtype=np.float32) * np.float32(np.log(10000.0) / half)).astype(np.float32)
    theta = (np.arange(S, dtype=np.float32)[:, None] * freqs[None, :]).astype(np.float32)
    cos, sin = np.cos(theta), np.sin(theta)
    rope = np.concatenate([np.repeat(cos, 2, 1), -sin, sin], 1).astype(np.float32)
    even = (np.arange(P) // DH1 % 2 == 0).astype(np.float32)
    return {
        "x": x, "xt": t(x), "mask": a["mask_BxSxS2_ik0"].reshape(B * S, S2),
        "ctx": a["ctx_1024"], "ctxt": a["ctx_1024"].transpose(0, 2, 1),
        "wq0": t(a["L0_attn_W_Q"].reshape(E0, D)), "wk0": t(a["L0_attn_W_K"].reshape(E0, D)),
        "wv0": t(a["L0_attn_W_V"].reshape(E0, D)), "wo0": a["L0_attn_W_O"].transpose(0, 2, 1).reshape(E0, D),
        "wx0": t(a["L0_xattn_W"]), "bx0": columns(a["L0_xattn_b"]), "gate": a["L0_ffn_gate_w"],
        "w1": np.concatenate([w1[:, 0::2], w1[:, 1::2]], 1).transpose(0, 2, 1),
        "w2": a["L0_ffn_dense_2_w"].transpose(0, 2, 1),
        "b1": np.concatenate([b1[:, 0::2], b1[:, 1::2]], 1),
        "b2": a["L0_ffn_dense_2_b"],
        "wqk": np.concatenate([a["L1_attn_Wq"], a["L1_attn_Wk"]], 1), "wv1": a["L1_attn_Wv"],
        "wgate": a["L1_attn_gate_w"], "wpp": a["L1_attn_p_w"], "wclock": np.repeat(a["L1_attn_clock_w"], DH1, 1),
        "wout": a["L1_attn_out_w"], "wm1": a["L1_attn_mlp_w1"], "wm2": a["L1_attn_mlp_w2"],
        "bm1": columns(a["L1_attn_mlp_b1"]),
        "cols": np.stack([columns(v) for v in (
            a["L1_attn_p_b"], np.repeat(a["L1_attn_clock_b"], DH1), a["L1_attn_gate_b"], a["L1_attn_ln1_g"],
            a["L1_attn_ln1_b"], a["L1_attn_ln2_g"], a["L1_attn_ln2_b"], a["L1_ffn_mu_r"], a["L1_ffn_mu_k"])], 1),
        "rows": np.stack([a["L1_attn_out_b"], a["L1_attn_mlp_b2"], a["L1_xattn_bp"]]),
        "wxq": t(a["L1_xattn_Wq"]), "wxk": t(a["L1_xattn_Wk"]), "wxv": t(a["L1_xattn_Wv"]), "wxp": t(a["L1_xattn_Wp"]),
        "wr": t(a["L1_ffn_W_r"]), "wk2": t(a["L1_ffn_W_k"]), "wv2": t(a["L1_ffn_W_v"]),
        "rope": rope.reshape(2, P, 2 * DH1).transpose(1, 0, 2), "parity": np.stack([even, 1 - even], 1),
    }


def kernel(**inputs):
    import concourse.bacc as bacc
    from concourse.bass_utils import run_bass_kernel_spmd

    nc = bacc.Bacc("TRN2", target_bir_lowering=False, num_devices=1)
    arrays, dram = {}, {}
    for name, a in laid_out({k: np.asarray(v) for k, v in inputs.items()}).items():
        a = np.ascontiguousarray(a)
        arrays[f"in_{name}"] = a
        dram[name] = nc.dram_tensor(f"in_{name}", a.shape, mybir.dt.from_np(a.dtype), kind="ExternalInput").ap()
    dram["x2"] = nc.dram_tensor("x2_rows", (B * S, D), F32, kind="Internal").ap()
    dram["y2"] = nc.dram_tensor("y2_slots", (SLOTS, D), F32, kind="Internal").ap()
    dram["out"] = nc.dram_tensor("out_x", (B * S, D), F32, kind="ExternalOutput").ap()
    decoder(nc, dram)
    result = run_bass_kernel_spmd(nc, [arrays], core_ids=[0])
    return result.results[0]["out_x"].reshape(B, S, D)
```

```python
import concourse.bass as bass
from concourse import mybir
from contextlib import ExitStack
import numpy as np

F32 = mybir.dt.float32
I32 = mybir.dt.int32
U32 = mybir.dt.uint32
ALU = mybir.AluOpType
ACT = mybir.ActivationFunctionType
AX = mybir.AxisListType

B, S, D = 8, 256, 256
S2 = 120
P = 128
KD = D // P
GB = 2
G = B // GB
GT = GB * S
NT = GT // P
TILES = B * S // P
EPS = 1e-5
H0, DH0 = 16, 64
E0 = H0 * DH0
PAIRS0 = H0 // 2
NE, FF = 8, 512
FC = FF // P
SLOT_TILES = 2 * B * S // P + NE - 1
SLOTS = SLOT_TILES * P
H1, DH1 = 16, 16
M1 = 4 * D
MC = M1 // P
HX, DHX = 4, 64

CAUSAL = P + S


class Memory:

    WORDS = 48 * 1024

    def __init__(self, nc, ctx):
        self.words = ctx.enter_context(nc.sbuf_tensor("words", [P, self.WORDS], F32))
        self.bank = [ctx.enter_context(nc.psum_tensor(f"bank{i}", [P, 512], F32)) for i in range(8)]
        self.mark = 0
        self.nc, self.ctx = nc, ctx
        self.used, self.free = [], []
        self.alone = ctx.enter_context(nc.semaphore("alone"))

    def sem(self, name):
        s = self.free.pop() if self.free else self.ctx.enter_context(self.nc.semaphore(name))
        self.used.append(s)
        return s

    def clear(self):
        used = self.used
        with self.nc.Block() as block:
            @block.gpsimd
            def _(pool):
                for s in used:
                    pool.sem_clear(s)
        self.free, self.used = self.free + used, []

    def take(self, shape, dt=F32):
        n = int(np.prod(shape[1:]))
        assert self.mark + n <= self.WORDS, (shape, self.mark)
        v = cut(self.words, self.mark, shape[1:], shape[0])
        self.mark += n + n % 2
        return v if dt == F32 else v.bitcast(dt)


def cut(region, start, dims, rows=P):
    v = region[0:rows, start:start + int(np.prod(dims))]
    if len(dims) == 1:
        return v
    names = "abcd"[:len(dims)]
    return v.rearrange(f"p ({' '.join(names)}) -> p {' '.join(names)}", **dict(zip(names, dims)))


class Norm:

    def __init__(self, mem, name, y=None, product=True, turned=True):
        self.stats = mem.sem(f"{name}_stats")
        self.rstd = mem.sem(f"{name}_rstd")
        self.normed = mem.sem(f"{name}_normed")
        if product:
            self.product = mem.sem(f"{name}_product")
            self.added = mem.sem(f"{name}_added")
        if turned:
            self.turned = mem.sem(f"{name}_turned")
            self.copied = mem.sem(f"{name}_copied")
        self.y = mem.take([P, NT, D]) if y is None else y
        self.bn = mem.take([P, NT, 6])
        self.mv = mem.take([P, NT, 2])
        self.var = mem.take([P, NT])
        self.inv = mem.take([P, NT])


def norm_tile_stats(dve, g, n, t):
    dve.drain()
    dve.bn_stats(n.bn[:, t, :], n.y[:, t, :])
    dve.drain()
    last = dve.bn_aggr(n.mv[:, t, :], n.bn[:, t, :])
    if t == NT - 1:
        last.then_inc(n.stats, 1)


def norm_rows(dve, g, n, out):
    dve.drain()
    dve.wait_ge(n.rstd, g + 1)
    for t in range(NT):
        dve.tensor_scalar(out(t), n.y[:, t, :], n.mv[:, t, 0:1], n.inv[:, t:t + 1],
                          ALU.subtract, ALU.mult).then_inc(n.normed, 1)


def norm_rstd(pool, g, n, eps, minus_half):
    pool.drain()
    pool.wait_ge(n.stats, g + 1)
    pool.tensor_tensor(n.var[:, :], n.mv[:, :, 1], eps, ALU.add)
    pool.drain()
    pool.tensor_tensor(n.inv[:, :], n.var[:, :], minus_half, ALU.pow).then_inc(n.rstd, 1)


def norm_turn(pe, g, n, rows, banks, ident):
    for t in range(NT):
        pe.wait_ge(n.normed, NT * g + t + 1)
        if t >= 2:
            pe.wait_ge(n.copied, NT * g + t - 1)
        for k in range(KD):
            last = pe.transpose(banks[t % 2][:, k * P:(k + 1) * P], rows(t)[:, k * P:(k + 1) * P], ident)
        last.then_inc(n.turned, 1)


def norm_copy(act, g, n, banks, out):
    for t in range(NT):
        act.wait_ge(n.turned, NT * g + t + 1)
        act.activation(out(t), banks[t % 2][:, 0:D].rearrange("p (k n) -> p k n", k=KD),
                       ACT.Copy).then_inc(n.copied, 1)


def end_of_turn(eng, g, turn, alone, engines=5):
    eng.drain()
    eng.nop().then_inc(turn, 1)
    eng.wait_ge(turn, engines * g + engines)
    eng.sem_inc(alone, 1)




def attention_layers(nc, dram, memory, keep):
    with ExitStack() as ctx:
        sb = memory.take
        bank = memory.bank

        sem = memory.sem
        alone = memory.alone
        wq, wk, wv = (sb([P, KD, E0]) for _ in range(3))
        wo = sb([P, PAIRS0, D])
        wx = sb([P, KD, D])
        bx = sb([P, KD])
        gate_w = sb([P, KD, NE])
        ident, minus_half, eps = sb([P, P]), sb([P, NT]), sb([P, NT])
        mask0 = sb([P, CAUSAL])
        expert = sb([P, NT, NE])
        xg, xt = sb([P, NT, D]), sb([P, KD, GT])
        qt, kt = sb([P, PAIRS0, GT]), sb([P, PAIRS0, GT])
        v = sb([P, NT, E0])
        SLOTS0 = 6
        prob = sb([P, SLOTS0, CAUSAL])
        mx, negmax, rowsum, inv = (sb([P, SLOTS0, 2]) for _ in range(4))
        probt = sb([P, 2, CAUSAL])
        zt = sb([P, PAIRS0, GT])
        x1, x1t = sb([P, NT, D]), sb([P, KD, GT])
        mem, memt = sb([S2, GB, D]), sb([P, KD, GB, S2])
        maski, maskf = sb([P, NT, S2], I32), sb([P, NT, S2])
        qx = sb([P, KD, GT])
        probx, probxt = sb([P, NT, S2]), sb([S2, NT, P])
        mxx, negx, sumx, invx = (sb([P, NT]) for _ in range(4))
        x2, x2t = sb([P, NT, D]), sb([P, KD, GT])
        score8, top8 = sb([P, NT, NE]), sb([P, NT, 8])
        at8, at8f = sb([P, NT, 8], U32), sb([P, NT, 8])
        gd, ge, gp, gq = (sb([P, NT]) for _ in range(4))
        pick0, pick1 = sb([P, NT, NE]), sb([P, NT, NE])

        qweights, kweights, vweights = (sem(f"a_{n}weights") for n in "qkv")
        weights, xloaded, loaded, const, turn, rowsout = (sem(f"a_{n}") for n in ("weights", "xloaded", "loaded", "const", "turn", "rowsout"))
        chunk, ev_act, ev_dve = sem("chunk"), sem("ev_act"), sem("ev_dve")
        scores, shifted, exped, probs = sem("scores"), sem("shifted"), sem("exped"), sem("probs")
        tposed, tcopied, heads, zcopied = sem("tposed"), sem("tcopied"), sem("heads"), sem("zcopied")
        xlogit, xshift, xexp, xtp, xtc = (sem(n) for n in ("xlogit", "xshift", "xexp", "xtp", "xtc"))
        gmm, gdiff, gexp, picked = sem("gmm"), sem("gdiff"), sem("gexp"), sem("picked")
        n1, n2 = Norm(memory, "n1"), Norm(memory, "n2")
        HEADS = GB * H0
        SCORES = (0, 1, 6, 7)
        QK = 2 * PAIRS0
        VC = NT * (E0 // 512)
        NCH = QK + VC + KD
        HALF = NCH // 2
        block = ctx.enter_context(nc.Block())

        @block.sync
        def _(sp):
            def load_x(g):
                sp.dma_start(xt[:, :, :], dram["xt"].rearrange("(k p) n -> p k n", p=P)[:, :, bass.ts(g, GT)]).then_inc(xloaded, 16)

            load_x(0)
            for dst, src, done in ((wq, dram["wq0"], qweights), (wk, dram["wk0"], kweights), (wv, dram["wv0"], vweights),
                                   (wo, dram["wo0"], weights), (wx, dram["wx0"], weights), (gate_w, dram["gate"], weights)):
                sp.dma_start(dst[:, :, :], src.rearrange("(k p) n -> p k n", p=P)).then_inc(done, 16)
            sp.dma_start(bx[:, :], dram["bx0"]).then_inc(weights, 16)
            with sp.Fori(0, G) as g:
                sp.dma_start(xg[:, :, :], dram["x"].rearrange("(g t p) n -> g p t n", p=P, t=NT)[g]).then_inc(loaded, 16)
                sp.dma_start(maski[:, :, :], dram["mask"].rearrange("(g t p) n -> g p t n", p=P, t=NT)[g]).then_inc(loaded, 16)
                sp.dma_start(mem[:, :, :], dram["ctx"].rearrange("(g b) s n -> g s b n", b=GB)[g]).then_inc(loaded, 16)
                for b in range(GB):
                    sp.dma_start(memt[:, :, b, :], dram["ctxt"].rearrange("(g b) (k p) s -> g b p k s", b=GB, p=P)[g, b]).then_inc(loaded, 16)
                sp.wait_ge(chunk, NCH * g + QK + VC)
                sp.sem_inc(alone, 1)
                load_x((g + 1) % G)
                sp.wait_ge(n2.normed, NT * g + NT)
                sp.dma_start(dram["x2"].rearrange("(g t p) n -> g p t n", p=P, t=NT)[g], x2[:, :, :]).then_inc(rowsout, 16)
                end_of_turn(sp, g, turn, alone)
                sp.wait_ge(rowsout, 16 * g + 16)
                sp.sem_inc(alone, 1)
            sp.wait_ge(xloaded, 16 * G + 16)

        @block.gpsimd
        def _(pool):
            pool.memset(ident[:, :], 0.0)
            pool.memset(mask0[:, :], 0.0)
            pool.memset(minus_half[:, :], -0.5)
            pool.memset(eps[:, :], EPS)
            pool.iota(expert[:, :, :], pattern=[[0, NT], [1, NE]], base=0, channel_multiplier=0,
                      allow_small_or_imprecise_dtypes=True)
            pool.drain()
            pool.affine_select(out=ident[:, :], in_=ident[:, :], compare_op=ALU.not_equal, fill=1.0, base=0,
                               pattern=[[-1, P]], channel_multiplier=1)
            for c in (0, S):
                pool.affine_select(out=mask0[:, c:c + P], in_=mask0[:, c:c + P], compare_op=ALU.is_ge,
                                   fill=-1e10, base=0, pattern=[[-1, P]], channel_multiplier=1)
            pool.drain()
            pool.nop().then_inc(const, 1)
            with pool.Fori(0, G) as g:
                norm_rstd(pool, g, n1, eps[:, :], minus_half[:, :])
                norm_rstd(pool, g, n2, eps[:, :], minus_half[:, :])
                pool.wait_ge(n2.normed, NT * g + NT)
                pool.tensor_copy(keep["x"][:, bass.ts(g, NT), :], x2[:, :, :])
                pool.wait_ge(picked, g + 1)
                pool.tensor_copy(keep["pick"][:, bass.ts(g, NT), :], pick0[:, :, :])
                pool.tensor_copy(keep["at"][:, bass.ts(g, NT), :], at8f[:, :, 0:2])
                pool.tensor_copy(keep["weight"][:, bass.ts(g, NT), 0], gp[:, :])
                pool.tensor_copy(keep["weight"][:, bass.ts(g, NT), 1], gq[:, :])
                end_of_turn(pool, g, turn, alone)

        @block.tensor
        def _(pe):
            def project(g, c, pairs):
                if c >= 4:
                    pe.wait_ge((ev_act, ev_dve)[c % 2], HALF * g + (c - 4) // 2 + 1)
                for i, (w, r) in enumerate(pairs):
                    last = pe.matmul(bank[c % 4][:, :], w, r, start=i == 0, stop=i == len(pairs) - 1)
                last.then_inc(chunk, 1)

            pe.wait_ge(const, 1)
            with pe.Fori(0, G) as g:
                pe.wait_ge(xloaded, 16 * g + 16)
                pe.sem_inc(alone, 1)
                for c in range(QK):
                    w = wq if c < PAIRS0 else wk
                    m = c % PAIRS0
                    if m == 0:
                        pe.wait_ge((qweights, kweights)[c // PAIRS0], 16)
                    project(g, c, [(w[:, k, m * P:(m + 1) * P], xt[:, k, :]) for k in range(KD)])
                pe.wait_ge(vweights, 16)
                for c in range(VC):
                    t, h = c // 2, c % 2
                    project(g, QK + c, [(xt[:, k, t * P:(t + 1) * P], wv[:, k, h * 512:(h + 1) * 512]) for k in range(KD)])
                pe.wait_ge(ev_act, HALF * g + (QK + VC) // 2)
                pe.wait_ge(ev_dve, HALF * g + (QK + VC) // 2)
                for i in range(HEADS + 5):
                    if i < HEADS:
                        b, h = i // H0, i % H0
                        r = slice(DH0 * (h % 2), DH0 * (h % 2) + DH0)
                        if i >= 4:
                            pe.wait_ge(shifted, HEADS * g + i - 3)
                        for t in range(2):
                            last = pe.matmul(bank[SCORES[i % 4]][:, t * P:t * P + P * (t + 1)],
                                             kt[r, h // 2, b * S + t * P:b * S + (t + 1) * P],
                                             qt[r, h // 2, b * S:b * S + P * (t + 1)], start=True, stop=True)
                        last.then_inc(scores, 1)
                    j = i - 4
                    if 0 <= j < HEADS:
                        pe.wait_ge(probs, HEADS * g + j + 1)
                        if j >= 2:
                            pe.wait_ge(tcopied, HEADS * g + j - 1)
                        for n, c in enumerate((0, P, S)):
                            last = pe.transpose(bank[2 + j % 2][:, n * P:(n + 1) * P],
                                                prob[:, j % SLOTS0, c:c + P], ident[:, :])
                        last.then_inc(tposed, 1)
                    j = i - 5
                    if 0 <= j < HEADS:
                        b, h = j // H0, j % H0
                        pe.wait_ge(tcopied, HEADS * g + j + 1)
                        if j % 2 == 0 and j >= 4:
                            pe.wait_ge(zcopied, HEADS // 2 * g + j // 2 - 1)
                        o = bank[4 + j // 2 % 2][DH0 * (h % 2):DH0 * (h % 2) + DH0, :]
                        pe.matmul(o[:, 0:S], v[:, 2 * b, h * DH0:(h + 1) * DH0],
                                  probt[:, j % 2, 0:S], start=True, stop=False)
                        pe.matmul(o[:, P:S], v[:, 2 * b + 1, h * DH0:(h + 1) * DH0],
                                  probt[:, j % 2, S:S + P], start=False, stop=True).then_inc(heads, 1)
                pe.wait_ge(zcopied, HEADS // 2 * g + HEADS // 2)
                pe.wait_ge(weights, 4 * 16)
                for t in range(NT):
                    if t >= 2:
                        pe.wait_ge(n1.added, NT * g + t - 1)
                    for m in range(PAIRS0):
                        last = pe.matmul(bank[6 + t % 2][:, 0:D], zt[:, m, t * P:(t + 1) * P], wo[:, m, :],
                                         start=m == 0, stop=m == PAIRS0 - 1)
                    last.then_inc(n1.product, 1)
                norm_turn(pe, g, n1, lambda t: x1[:, t, :], bank[2:4], ident[:, :])
                pe.wait_ge(n1.copied, NT * g + NT)
                for c in range(KD):
                    project(g, QK + VC + c, [(wx[:, k, c * P:(c + 1) * P], x1t[:, k, :]) for k in range(KD)])
                pe.wait_ge(ev_act, HALF * g + HALF)
                pe.wait_ge(ev_dve, HALF * g + HALF)
                pe.wait_ge(loaded, 80 * g + 80)
                pe.sem_inc(alone, 1)
                for t in range(NT):
                    if t >= 2:
                        pe.wait_ge(xshift, NT * g + t - 1)
                    for k in range(KD):
                        last = pe.matmul(bank[4 + t % 2][:, 0:S2], qx[:, k, t * P:(t + 1) * P],
                                         memt[:, k, t // 2, :], start=k == 0, stop=k == KD - 1)
                    last.then_inc(xlogit, 1)
                for t in range(NT):
                    pe.wait_ge(xexp, NT * g + t + 1)
                    if t >= 2:
                        pe.wait_ge(xtc, NT * g + t - 1)
                    pe.transpose(bank[6 + t % 2][0:S2, 0:P], probx[:, t, :], ident[:, :]).then_inc(xtp, 1)
                for t in range(NT):
                    pe.wait_ge(xtc, NT * g + t + 1)
                    if t >= 2:
                        pe.wait_ge(n2.added, NT * g + t - 1)
                    pe.matmul(bank[t % 2][:, 0:D], probxt[:, t, :], mem[:, t // 2, :],
                              start=True, stop=True).then_inc(n2.product, 1)
                norm_turn(pe, g, n2, lambda t: x2[:, t, :], bank[2:4], ident[:, :])
                for t in range(NT):
                    pe.wait_ge(n2.copied, NT * g + t + 1)
                    for k in range(KD):
                        last = pe.matmul(bank[4][:, t * NE:(t + 1) * NE], x2t[:, k, t * P:(t + 1) * P],
                                         gate_w[:, k, :], start=k == 0, stop=k == KD - 1)
                last.then_inc(gmm, 1)
                end_of_turn(pe, g, turn, alone)

        def target(c):
            if c < QK:
                return (qt if c < PAIRS0 else kt)[:, c % PAIRS0, :]
            c -= QK
            return v[:, c // 2, (c % 2) * 512:(c % 2 + 1) * 512]

        @block.scalar
        def _(act):
            with act.Fori(0, G) as g:
                for c in range(0, QK + VC, 2):
                    act.wait_ge(chunk, NCH * g + c + 1)
                    act.activation(target(c), bank[c % 4][:, :], ACT.Copy).then_inc(ev_act, 1)
                for i in range(HEADS + 6):
                    j = i - 4
                    if 0 <= j < HEADS:
                        act.wait_ge(tposed, HEADS * g + j + 1)
                        if j >= 2:
                            act.wait_ge(heads, HEADS * g + j - 1)
                        act.activation(probt[:, j % 2, :], bank[2 + j % 2][:, 0:CAUSAL], ACT.Copy).then_inc(tcopied, 1)
                    if i < HEADS:
                        act.wait_ge(shifted, HEADS * g + i + 1)
                        for t in range(2):
                            c = slice(t * P, t * P + P * (t + 1))
                            last = act.activation(prob[:, i % SLOTS0, c], prob[:, i % SLOTS0, c], ACT.Exp,
                                                  bias=negmax[:, i % SLOTS0, t:t + 1], scale=DH0 ** -0.5,
                                                  accum_out=rowsum[:, i % SLOTS0, t:t + 1])
                        last.then_inc(exped, 1)
                    j = i - 6
                    if 0 <= j < HEADS and j % 2:
                        b, h = j // H0, j % H0
                        act.wait_ge(heads, HEADS * g + j + 1)
                        act.activation(zt[:, h // 2, b * S:(b + 1) * S], bank[4 + j // 2 % 2][:, 0:S], ACT.Copy).then_inc(zcopied, 1)
                norm_copy(act, g, n1, bank[2:4], lambda t: x1t[:, :, t * P:(t + 1) * P])
                act.wait_ge(weights, 4 * 16)
                act.wait_ge(chunk, NCH * g + QK + VC + 1)
                act.activation(qx[:, 0, :], bank[(QK + VC) % 4][:, :], ACT.Identity, bias=bx[:, 0:1]).then_inc(ev_act, 1)
                for t in range(NT):
                    act.wait_ge(xshift, NT * g + t + 1)
                    act.activation(probx[:, t, :], probx[:, t, :], ACT.Exp, bias=negx[:, t:t + 1],
                                   accum_out=sumx[:, t:t + 1]).then_inc(xexp, 1)
                for t in range(NT):
                    act.wait_ge(xtp, NT * g + t + 1)
                    act.activation(probxt[:, t, :], bank[6 + t % 2][0:S2, 0:P], ACT.Copy).then_inc(xtc, 1)
                norm_copy(act, g, n2, bank[2:4], lambda t: x2t[:, :, t * P:(t + 1) * P])
                act.wait_ge(gdiff, g + 1)
                act.activation(ge[:, :], gd[:, :], ACT.Exp).then_inc(gexp, 1)
                end_of_turn(act, g, turn, alone)

        @block.vector
        def _(dve):
            dve.wait_ge(const, 1)
            with dve.Fori(0, G) as g:
                for c in range(1, QK + VC, 2):
                    dve.wait_ge(chunk, NCH * g + c + 1)
                    dve.tensor_copy(target(c), bank[c % 4][:, :]).then_inc(ev_dve, 1)
                dve.wait_ge(loaded, 80 * g + 80)
                dve.tensor_scalar(maskf[:, :, :], maski[:, :, :], -1.0, 1e9, ALU.add, ALU.mult)
                for i in range(HEADS + 2):
                    if i < HEADS:
                        dve.wait_ge(scores, HEADS * g + i + 1)
                        if i >= SLOTS0:
                            dve.wait_ge(tposed, HEADS * g + i - SLOTS0 + 1)
                        dve.sem_inc(alone, 1)
                        for t in range(2):
                            c = slice(t * P, t * P + P * (t + 1))
                            dve.tensor_tensor_reduce(out=prob[:, i % SLOTS0, c], in0=bank[SCORES[i % 4]][:, c], in1=mask0[:, c],
                                                     scale=1.0, scalar=-3e38, op0=ALU.add, op1=ALU.max,
                                                     accum_out=mx[:, i % SLOTS0, t:t + 1])
                        dve.drain()
                        dve.tensor_scalar(negmax[:, i % SLOTS0, :], mx[:, i % SLOTS0, :], -DH0 ** -0.5, None,
                                          ALU.mult).then_inc(shifted, 1)
                    j = i - 2
                    if 0 <= j < HEADS:
                        dve.wait_ge(exped, HEADS * g + j + 1)
                        dve.reciprocal(inv[:, j % SLOTS0, :], rowsum[:, j % SLOTS0, :])
                        dve.drain()
                        for t in range(2):
                            c = slice(t * P, t * P + P * (t + 1))
                            last = dve.tensor_scalar(prob[:, j % SLOTS0, c], prob[:, j % SLOTS0, c], inv[:, j % SLOTS0, t:t + 1],
                                                     None, ALU.mult)
                        last.then_inc(probs, 1)
                for t in range(NT):
                    dve.wait_ge(n1.product, NT * g + t + 1)
                    dve.tensor_tensor(n1.y[:, t, :], bank[6 + t % 2][:, 0:D], xg[:, t, :], ALU.add).then_inc(n1.added, 1)
                    norm_tile_stats(dve, g, n1, t)
                norm_rows(dve, g, n1, lambda t: x1[:, t, :])
                dve.wait_ge(weights, 4 * 16)
                dve.wait_ge(chunk, NCH * g + NCH)
                dve.tensor_scalar(qx[:, 1, :], bank[(NCH - 1) % 4][:, :], bx[:, 1:2], None, ALU.add).then_inc(ev_dve, 1)
                for t in range(NT):
                    dve.drain()
                    dve.wait_ge(xlogit, NT * g + t + 1)
                    dve.sem_inc(alone, 1)
                    dve.tensor_tensor_reduce(out=probx[:, t, :], in0=bank[4 + t % 2][:, 0:S2], in1=maskf[:, t, :],
                                             scale=1.0, scalar=-3e38, op0=ALU.add, op1=ALU.max, accum_out=mxx[:, t:t + 1])
                    dve.drain()
                    dve.tensor_scalar(negx[:, t:t + 1], mxx[:, t:t + 1], -1.0, None, ALU.mult).then_inc(xshift, 1)
                dve.wait_ge(xexp, NT * g + NT)
                dve.reciprocal(invx[:, :], sumx[:, :])
                dve.drain()
                for t in range(NT):
                    dve.wait_ge(n2.product, NT * g + t + 1)
                    dve.scalar_tensor_tensor(n2.y[:, t, :], bank[t % 2][:, 0:D], invx[:, t:t + 1], x1[:, t, :],
                                             ALU.mult, ALU.add).then_inc(n2.added, 1)
                    norm_tile_stats(dve, g, n2, t)
                norm_rows(dve, g, n2, lambda t: x2[:, t, :])
                dve.wait_ge(gmm, g + 1)
                dve.tensor_copy(score8[:, :, :], bank[4][:, 0:NT * NE].rearrange("p (t e) -> p t e", t=NT))
                dve.drain()
                for t in range(NT):
                    dve.max(top8[:, t, :], score8[:, t, :])
                dve.drain()
                for t in range(NT):
                    dve.max_index(at8[:, t, :], top8[:, t, :], score8[:, t, :])
                dve.tensor_tensor(gd[:, :], top8[:, :, 1], top8[:, :, 0], ALU.subtract).then_inc(gdiff, 1)
                dve.drain()
                dve.tensor_copy(at8f[:, :, :], at8[:, :, :])
                dve.wait_ge(gexp, g + 1)
                dve.tensor_scalar(gq[:, :], ge[:, :], 1.0, None, ALU.add)
                dve.drain()
                dve.reciprocal(gp[:, :], gq[:, :])
                dve.drain()
                dve.tensor_tensor(gq[:, :], gp[:, :], ge[:, :], ALU.mult)
                dve.drain()
                for t in range(NT):
                    dve.tensor_scalar(pick0[:, t, :], expert[:, t, :], at8f[:, t, 0:1], gp[:, t:t + 1], ALU.is_equal, ALU.mult)
                    dve.tensor_scalar(pick1[:, t, :], expert[:, t, :], at8f[:, t, 1:2], gq[:, t:t + 1], ALU.is_equal, ALU.mult)
                dve.drain()
                dve.tensor_tensor(pick0[:, :, :], pick0[:, :, :], pick1[:, :, :], ALU.add).then_inc(picked, 1)
                end_of_turn(dve, g, turn, alone)


def expert_layer(nc, dram, memory, keep):
    with ExitStack() as ctx:
        sb = memory.take
        bank = memory.bank

        sem = memory.sem
        alone = memory.alone
        W1, W2 = KD * 2 * FF, FC * D
        w1, w2 = sb([P, NE * W1]), sb([P, NE * W2])
        b1 = sb([P, NE * 2 * FF])
        b2 = sb([NE, D])
        ident, before, ones = sb([P, P]), sb([P, P]), sb([P, P])
        lane, number = sb([P, P]), sb([P, SLOT_TILES])
        expert, token = sb([P, TILES, NE]), sb([P, TILES])
        pickt = sb([NE, TILES, P])
        chosen, both = sb([P, 2, TILES, NE]), sb([P, TILES, NE])
        total = sb([P, TILES + 1, NE])
        length, end, base = sb([P, NE]), sb([P, NE]), sb([P, NE])
        rank, high, low = (sb([P, 2, TILES]) for _ in range(3))
        owner, owneri = sb([P, SLOT_TILES]), sb([P, SLOT_TILES], I32)
        source = sb([P, SLOT_TILES], I32)
        at = sb([P, 2], I32)
        OH = 8
        ohlow, ohhigh = sb([P, 2, OH, P]), sb([P, 2, OH, SLOT_TILES])
        rows, rowst = sb([P, 2, D]), sb([P, 2, KD, P])
        gate, value, sig, hidden = (sb([P, FF]) for _ in range(4))
        hiddent = sb([P, FC, P])
        y = sb([P, 2, D])
        const, biases, expload, ready = sem("e_const"), sem("e_biases"), [sem("e_load0"), sem("e_load1")], sem("e_ready")
        ptp, ptc, bmm, badd = sem("ptp"), sem("ptc"), sem("bmm"), sem("badd")
        chosens, counts, onehots, placed, sourced = (sem(n) for n in ("chosens", "counts", "onehots", "placed", "sourced"))
        rturned, rcopied = sem("rturned"), sem("rcopied")
        gathered, ystored = ([sem(f"{n}{s}") for s in range(2)] for n in ("gathered", "ystored"))
        upgate, upvalue, clipped, gated, mixed, hready = (sem(n) for n in ("upgate", "upvalue", "clipped", "gated", "mixed", "hready"))
        hturned, hcopied, down, yread = (sem(n) for n in ("hturned", "hcopied", "down", "yread"))
        ROUND = 1.5 * 2 ** 23
        BANKG, BANKV, BANKH, BANKY, BANKR = (0, 1), (2, 3), 4, 5, (6, 7)
        block = ctx.enter_context(nc.Block())

        @block.sync
        def _(sp):
            sp.dma_start(b2[:, :], dram["b2"]).then_inc(biases, 16)
            for e in range(NE):
                sp.dma_start(w1[:, e * W1:(e + 1) * W1].rearrange("p (k n) -> p k n", k=KD),
                             dram["w1"].rearrange("e (k p) n -> e p k n", p=P)[e]).then_inc(expload[e % 2], 16)
                sp.dma_start(w2[:, e * W2:(e + 1) * W2].rearrange("p (k n) -> p k n", k=FC),
                             dram["w2"].rearrange("e (k p) n -> e p k n", p=P)[e]).then_inc(expload[e % 2], 16)
                sp.dma_start(b1[:, e * 2 * FF:(e + 1) * 2 * FF],
                             dram["b1"][e:e + 1, :].to_broadcast([P, 2 * FF])).then_inc(expload[e % 2], 16)
                if e >= 1:
                    sp.wait_ge(expload[(e - 1) % 2], 48 * ((e - 1) // 2 + 1))
                    sp.sem_inc(ready, 1)
            sp.wait_ge(expload[(NE - 1) % 2], 48 * ((NE - 1) // 2 + 1))
            sp.sem_inc(ready, 1)

        @block.gpsimd
        def _(pool):
            pool.memset(ident[:, :], 0.0)
            pool.memset(before[:, :], 1.0)
            pool.memset(ones[:, :], 1.0)
            for v, pattern, step in ((lane, [[1, P]], 0), (number, [[1, SLOT_TILES]], 0), (token, [[P, TILES]], 1)):
                pool.iota(v[:, :], pattern=pattern, base=0, channel_multiplier=step, allow_small_or_imprecise_dtypes=True)
            pool.iota(expert[:, :, :], pattern=[[0, TILES], [1, NE]], base=0, channel_multiplier=0,
                      allow_small_or_imprecise_dtypes=True)
            pool.drain()
            pool.affine_select(out=ident[:, :], in_=ident[:, :], compare_op=ALU.not_equal, fill=1.0, base=0,
                               pattern=[[-1, P]], channel_multiplier=1)
            pool.affine_select(out=before[:, :], in_=before[:, :], compare_op=ALU.is_ge, fill=0.0, base=-1,
                               pattern=[[1, P]], channel_multiplier=-1)
            pool.drain()
            pool.nop().then_inc(const, 1)

            def gather(j, s):
                pool.tensor_copy(at[:, s:s + 1], source[:, bass.ds(j, 1)])
                pool.drain()
                pool.indirect_dma_start(rows[:, s, :], None, dram["x2"][:, :],
                                        bass.IndirectOffsetOnAxis(ap=at[:, s:s + 1], axis=0)).then_inc(gathered[s], 16)

            def mix(j):
                pool.wait_ge(gated, j + 1)
                pool.tensor_tensor(sig[:, :], gate[:, :], sig[:, :], ALU.mult).then_inc(mixed, 1)

            pool.wait_ge(sourced, 1)
            gather(0, 0)
            gather(1, 1)
            last = SLOT_TILES - 3
            with pool.Fori(0, last // 2) as i:
                for s in range(2):
                    mix(2 * i + s)
                    gather(2 * i + s + 2, s)
            mix(last)
            gather(SLOT_TILES - 1, last % 2)
            mix(last + 1)
            mix(last + 2)
            for s in range(2):
                pool.wait_ge(ystored[s], 16 * ((SLOT_TILES + 1 - s) // 2))

        @block.tensor
        def _(pe):
            pe.wait_ge(const, 1)
            pe.wait_ge(chosens, 1)
            pe.matmul(bank[6][:, 0:TILES * NE], before[:, :], both[:, :, :].rearrange("p t e -> p (t e)"), start=True, stop=True)
            pe.matmul(bank[7][:, 0:TILES * NE], ones[:, :], both[:, :, :].rearrange("p t e -> p (t e)"),
                      start=True, stop=True).then_inc(counts, 1)
            pe.wait_ge(biases, 16)
            for t in range(TILES):
                if t >= 2:
                    pe.wait_ge(ptc, t - 1)
                pe.transpose(bank[t % 2][0:NE, 0:P], keep["pick"][:, t, :], ident[:, :]).then_inc(ptp, 1)
            chunks = 2 * TILES // OH
            for c in range(chunks):
                pe.wait_ge(onehots, c + 1)
                for n in range(OH):
                    last = pe.matmul(bank[5][:, 0:SLOT_TILES], ohlow[:, c % 2, n, :], ohhigh[:, c % 2, n, :],
                                     start=c == 0 and n == 0, stop=c == chunks - 1 and n == OH - 1)
                last.then_inc(placed, 1)
                for t in range(c * TILES // chunks, (c + 1) * TILES // chunks):
                    pe.wait_ge(ptc, t + 1)
                    if t >= 2:
                        pe.wait_ge(badd, t - 1)
                    pe.matmul(bank[2 + t % 2][:, 0:D], pickt[:, t, :], b2[:, :], start=True, stop=True).then_inc(bmm, 1)

            def turn_rows(i, s):
                pe.wait_ge(gathered[s], 16 * i + 16)
                pe.sem_inc(alone, 1)
                for k in range(KD):
                    last = pe.transpose(bank[BANKR[s]][:, k * P:(k + 1) * P], rows[:, s, k * P:(k + 1) * P], ident[:, :])
                last.then_inc(rturned, 1)

            def up(e, s, half):
                for k in range(KD):
                    last = pe.matmul(bank[(BANKG, BANKV)[half][s]][:, :], rowst[:, s, k, :],
                                     w1[:, bass.ds(e * W1 + k * 2 * FF + half * FF, FF)], start=k == 0, stop=k == KD - 1)
                last.then_inc((upgate, upvalue)[half], 1)

            def start(j):
                e = pe.value_load(owneri[0:1, bass.ds(j, 1)], min_val=0, max_val=NE - 1)
                pe.wait_ge(ready, e + 1)
                pe.sem_inc(alone, 1)
                pe.wait_ge(rcopied, j + 1)
                pe.sem_inc(alone, 1)
                return e

            def step(i, s, ahead=2):
                j = 2 * i + s
                if ahead >= 1:
                    following = start(j + 1)
                    up(following, 1 - s, 0)
                pe.wait_ge(hready, j + 1)
                pe.sem_inc(alone, 1)
                for k in range(FC):
                    last = pe.transpose(bank[BANKH][:, k * P:(k + 1) * P], hidden[:, k * P:(k + 1) * P], ident[:, :])
                last.then_inc(hturned, 1)
                if ahead >= 1:
                    up(following, 1 - s, 1)
                if ahead >= 2:
                    turn_rows(i + 1, s)
                pe.wait_ge(hcopied, j + 1)
                pe.sem_inc(alone, 1)
                pe.wait_ge(yread, j + 1)
                pe.sem_inc(alone, 1)
                e = pe.value_load(owneri[0:1, bass.ds(j, 1)], min_val=0, max_val=NE - 1)
                for k in range(FC):
                    last = pe.matmul(bank[BANKY][:, 0:D], hiddent[:, k, :], w2[:, bass.ds(e * W2 + k * D, D)],
                                     start=k == 0, stop=k == FC - 1)
                last.then_inc(down, 1)

            pe.wait_ge(sourced, 1)
            turn_rows(0, 0)
            e = start(0)
            pe.wait_ge(badd, TILES)
            up(e, 0, 0)
            up(e, 0, 1)
            turn_rows(0, 1)
            tail = (SLOT_TILES - 2) // 2 * 2
            with pe.Fori(0, tail // 2) as i:
                for s in range(2):
                    step(i, s)
            for j in range(tail, SLOT_TILES):
                step(j // 2, j % 2, SLOT_TILES - 1 - j)

        @block.scalar
        def _(act):
            act.nop().then_inc(yread, 1)
            for t in range(TILES):
                act.wait_ge(ptp, t + 1)
                act.activation(pickt[:, t, :], bank[t % 2][0:NE, 0:P], ACT.Copy).then_inc(ptc, 1)

            def copy_rows(j, s):
                act.wait_ge(rturned, j + 1)
                act.activation(rowst[:, s, :, :], bank[BANKR[s]][:, 0:D].rearrange("p (k n) -> p k n", k=KD), ACT.Copy).then_inc(rcopied, 1)

            def sigmoid(j):
                act.wait_ge(clipped, j + 1)
                act.activation(sig[:, :], gate[:, :], ACT.Sigmoid, scale=1.702).then_inc(gated, 1)

            def step(i, s, ahead=2, first=False):
                j = 2 * i + s
                act.wait_ge(hturned, j + 1)
                act.activation(hiddent[:, :, :], bank[BANKH][:, :].rearrange("p (k n) -> p k n", k=FC), ACT.Copy).then_inc(hcopied, 1)
                if ahead >= 1:
                    sigmoid(j + 1)
                if ahead >= 2:
                    copy_rows(j + 2, s)
                if not first:
                    act.wait_ge(ystored[s], 16 * i)
                    act.sem_inc(alone, 1)
                act.wait_ge(down, j + 1)
                act.activation(y[:, s, :], bank[BANKY][:, 0:D], ACT.Copy).then_inc(yread, 1)
                act.wait_ge(yread, j + 2)
                act.sem_inc(alone, 1)
                act.dma_start(dram["y2"].rearrange("(j p) n -> p j n", p=P)[:, bass.ds(j, 1), :], y[:, s:s + 1, :]).then_inc(ystored[s], 16)

            copy_rows(0, 0)
            sigmoid(0)
            copy_rows(1, 1)
            step(0, 0, first=True)
            step(0, 1, first=True)
            tail = (SLOT_TILES - 2) // 2 * 2
            with act.Fori(1, tail // 2) as i:
                for s in range(2):
                    step(i, s)
            for j in range(tail, SLOT_TILES):
                step(j // 2, j % 2, SLOT_TILES - 1 - j)

        @block.vector
        def _(dve):
            dve.wait_ge(const, 1)
            for r in range(2):
                dve.tensor_tensor(chosen[:, r, :, :], expert[:, :, :], keep["at"][:, :, r:r + 1].to_broadcast([P, TILES, NE]), ALU.is_equal)
            dve.memset(total[:, 0, :], 0.0)
            dve.drain()
            dve.tensor_tensor(both[:, :, :], chosen[:, 0, :, :], chosen[:, 1, :, :], ALU.add).then_inc(chosens, 1)
            dve.wait_ge(counts, 1)
            for t in range(TILES):
                dve.tensor_tensor(total[:, t + 1, :], total[:, t, :], bank[7][:, t * NE:(t + 1) * NE], ALU.add)
                dve.drain()
            dve.tensor_scalar(length[:, :], total[:, TILES, :], (P - 1) / 2, 1 / P, ALU.add, ALU.mult)
            dve.drain()
            dve.tensor_scalar(length[:, :], length[:, :], ROUND, None, ALU.add)
            dve.drain()
            dve.tensor_scalar(length[:, :], length[:, :], -ROUND, None, ALU.add)
            dve.drain()
            dve.tensor_tensor_scan(end[:, :], ones[:, 0:NE], length[:, :], 0.0, ALU.mult, ALU.add)
            dve.drain()
            dve.tensor_tensor(base[:, :], end[:, :], length[:, :], ALU.subtract)
            dve.tensor_scalar(owner[:, :], number[:, :], end[:, 0:1], None, ALU.is_ge)
            dve.drain()
            dve.tensor_scalar(base[:, :], base[:, :], float(P), None, ALU.mult)
            for e in range(1, NE - 1):
                dve.drain()
                dve.scalar_tensor_tensor(owner[:, :], number[:, :], end[:, e:e + 1], owner[:, :], ALU.is_ge, ALU.add)
            rest = total[:, 0:TILES, :]
            dve.tensor_tensor(rest, rest, base[:, :].unsqueeze(1).to_broadcast([P, TILES, NE]), ALU.add)
            dve.drain()
            dve.tensor_copy(owneri[:, :], owner[:, :])
            dve.tensor_tensor(rest, rest, bank[6][:, 0:TILES * NE].rearrange("p (t e) -> p t e", t=TILES), ALU.add)
            dve.drain()
            for r in range(2):
                dve.tensor_tensor(chosen[:, r, :, :], chosen[:, r, :, :], rest, ALU.mult)
            dve.drain()
            for r in range(2):
                dve.tensor_reduce(rank[:, r, :], chosen[:, r, :, :], AX.X, ALU.add)
            dve.drain()
            dve.tensor_copy(keep["slot"][:, :, :], rank[:, :, :])
            dve.tensor_scalar(high[:, :, :], rank[:, :, :], -(P - 1) / 2, 1 / P, ALU.add, ALU.mult)
            dve.drain()
            dve.tensor_scalar(high[:, :, :], high[:, :, :], ROUND, None, ALU.add)
            dve.drain()
            dve.tensor_scalar(high[:, :, :], high[:, :, :], -ROUND, None, ALU.add)
            dve.drain()
            dve.scalar_tensor_tensor(low[:, :, :], high[:, :, :], -float(P), rank[:, :, :], ALU.mult, ALU.add)
            dve.drain()
            chunks = 2 * TILES // OH

            def add_biases(c):
                for t in range(c * TILES // chunks, (c + 1) * TILES // chunks):
                    dve.wait_ge(bmm, t + 1)
                    dve.tensor_tensor(keep["x"][:, t, :], bank[2 + t % 2][:, 0:D], keep["x"][:, t, :], ALU.add).then_inc(badd, 1)

            for c in range(chunks):
                r, t = c * OH // TILES, c * OH % TILES
                if c >= 2:
                    dve.wait_ge(placed, c - 1)
                dve.tensor_tensor(ohhigh[:, c % 2, :, :], number[:, :].unsqueeze(1).to_broadcast([P, OH, SLOT_TILES]),
                                  high[:, r, t:t + OH].unsqueeze(2).to_broadcast([P, OH, SLOT_TILES]), ALU.is_equal)
                dve.tensor_tensor(ohlow[:, c % 2, :, :], lane[:, :].unsqueeze(1).to_broadcast([P, OH, P]),
                                  low[:, r, t:t + OH].unsqueeze(2).to_broadcast([P, OH, P]), ALU.is_equal)
                dve.drain()
                dve.tensor_tensor(ohhigh[:, c % 2, :, :], ohhigh[:, c % 2, :, :],
                                  token[:, t:t + OH].unsqueeze(2).to_broadcast([P, OH, SLOT_TILES]), ALU.mult).then_inc(onehots, 1)
                if c >= 1:
                    add_biases(c - 1)
            add_biases(chunks - 1)
            dve.wait_ge(placed, chunks)
            dve.tensor_copy(source[:, :], bank[5][:, 0:SLOT_TILES]).then_inc(sourced, 1)

            def step(j, s):
                e = dve.value_load(owneri[0:1, bass.ds(j, 1)], min_val=0, max_val=NE - 1)
                dve.drain()
                dve.wait_ge(upgate, j + 1)
                dve.tensor_tensor(gate[:, :], bank[BANKG[s]][:, :], b1[:, bass.ds(e * 2 * FF, FF)], ALU.add)
                dve.drain()
                dve.tensor_scalar(gate[:, :], gate[:, :], 9.0, None, ALU.min).then_inc(clipped, 1)
                dve.wait_ge(upvalue, j + 1)
                dve.tensor_tensor(value[:, :], bank[BANKV[s]][:, :], b1[:, bass.ds(e * 2 * FF + FF, FF)], ALU.add)
                dve.drain()
                dve.tensor_scalar(value[:, :], value[:, :], 9.0, -9.0, ALU.min, ALU.max)
                dve.drain()
                dve.wait_ge(mixed, j + 1)
                dve.scalar_tensor_tensor(hidden[:, :], value[:, :], 1.0, sig[:, :], ALU.add, ALU.mult).then_inc(hready, 1)

            with dve.Fori(0, SLOT_TILES // 2) as i:
                for s in range(2):
                    step(2 * i + s, s)
            step(SLOT_TILES - 1, 0)


def last_layers(nc, dram, memory, keep):
    with ExitStack() as ctx:
        sb = memory.take
        bank = memory.bank

        sem = memory.sem
        alone = memory.alone
        wqk = sb([P, KD, 2 * D])
        wv1, wgate, wpp, wclock, wout = (sb([P, KD, D]) for _ in range(5))
        wm1, wm2 = sb([P, KD, M1]), sb([P, MC, D])
        wxq, wxk, wxv, wxp = (sb([P, KD, D]) for _ in range(4))
        wr, wk2, wv2 = (sb([P, KD, D]) for _ in range(3))
        bm1 = sb([P, MC])
        cols = sb([P, 9, KD])
        BP, BCLK, BGATE, G1, B1, G2, B2, MUR, MUK = range(9)
        unmu = sb([P, 2, KD])
        brow = sb([P, 3, D])
        rope = sb([P, 2, 2 * DH1])
        headmask = sb([P, 8])
        ident, minus_half, eps = sb([P, P]), sb([P, NT]), sb([P, NT])
        ones, tiny = sb([P, S]), sb([P, 1])
        mask1 = sb([P, CAUSAL])
        maskx = sb([P, 2, HX * S2])
        va = sb([P, NT, H1, 32])
        qf, kf = sb([P, KD, GT]), sb([P, KD, GT])
        qt, kt = sb([P, KD, GT]), sb([P, KD, GT])
        x4, xn, xnt, xb = sb([P, NT, D]), sb([P, NT, D]), sb([P, KD, GT]), sb([P, NT, D])
        ya, yb = sb([P, NT, D]), sb([P, NT, D])
        ss, rn, r2 = sb([P, NT * 32]), sb([P, NT * 32]), sb([P, NT * 32])
        pmax, rden = sb([P, KD * GB]), sb([P, NT, H1])
        xmax, xsum, xinv = (sb([P, NT, HX]) for _ in range(3))
        memt = sb([P, KD, GB * S2])
        at = sb([P, 2, NT], I32)
        region1 = sb([P, 8192 + 4 * (S + 1)])
        region2 = sb([P, 7168])

        fm = cut(region1, 0, (6, GT))
        ee = cut(region1, 3072, (4, GT))
        uu = cut(region1, 5120, (4, GT))
        dd = cut(region1, 7168, (2, GT))
        ktm = cut(region1, 0, (8, KD * GT))
        m1t = cut(region1, 0, (MC, GT))
        sm = cut(region1, 0, (NT, HX * S2))
        pxt = cut(region1, 1920, (GB, HX, S), S2)
        zxt, qxt = cut(region1, 4096, (KD, GT)), cut(region1, 5120, (KD, GT))
        kxt, vx = cut(region1, 6144, (KD, GB * S2)), cut(region1, 6624, (GB, D), S2)
        xr, xk, rs, rl = (cut(region1, 1024 * i, dims) for i, dims in enumerate(((KD, GT), (KD, GT), (NT, D), (KD, GT))))
        shift, ka = cut(region1, 4096, (KD, GT)), cut(region1, 5120, (KD, GT))
        x5 = cut(region1, 7168, (NT, D))
        x5t = cut(region1, 8192, (KD, GB, S + 1))
        xo = xb
        back = cut(region2, 0, (2 * NT, D))
        sq, qn = cut(region2, 0, (2, 512)), cut(region2, 1024, (NT, 512))
        ra, rb = cut(region2, 3072, (NT, 512)), cut(region2, 5120, (NT, 512))
        es, ut = cut(region2, 0, (4, CAUSAL)), cut(region2, 1536, (4, GT))
        og, ogt = cut(region2, 3584, (NT, D)), cut(region2, 4608, (KD, GT))
        h5, h5t, x4t = xn, xnt, xnt

        early = sem("l_early")
        weights, rows, loaded, const, turn, stored, free = (sem(f"l_{n}") for n in ("weights", "rows", "loaded", "const", "turn", "stored", "free"))
        qkmm, vmm, vcop, fmm, fmread, sqd, sqred, ssready, rnr = (sem(n) for n in ("qkmm", "vmm", "vcop", "fmm", "fmread", "sqd", "sqred", "ssready", "rnr"))
        qnr, rar, roped, eready, egate, ugate, lgate, uready, lready, npm, pexp, clr, gcr, sumr, first = (sem(n) for n in ("qnr", "rar", "roped", "eready", "egate", "ugate", "lgate", "uready", "lready", "npm", "pexp", "clr", "gcr", "sumr", "first"))
        qktp, qkt, kmdve, kmact, s1, s1m, s1e, av1, utc, ttp, ogr, ogtp, ogc = (sem(n) for n in ("qktp", "qkt", "kmdve", "kmact", "s1", "s1m", "s1e", "av1", "utc", "ttp", "ogr", "ogtp", "ogc"))
        backed = [sem(f"backed{n}") for n in range(2 * NT)]
        biased, m1mm, m1g = (sem(n) for n in ("biased", "m1mm", "m1g"))
        xq, xqr, xkm, xkr, xvm, xvr, xs, xsr, xsub, xe, xp, xtp, xtc, xav, xz = (sem("l_" + n) for n in (
            "xq", "xqr", "xkm", "xkr", "xvm", "xvr", "xs", "xsr", "xsub", "xe", "xp", "xtp", "xtc", "xav", "xz"))
        mixk, mixr, kmm, relu, kact, rmm, rsig = (sem(n) for n in ("mixk", "mixr", "kmm", "relu", "kact", "rmm", "rsig"))
        n3, n4 = Norm(memory, "n3", keep["x"], product=False, turned=False), Norm(memory, "n4", keep["x"], product=False)
        n5, n6, n7 = (Norm(memory, n, y) for n, y in (("n5", yb), ("n6", ya), ("n7", yb)))
        n8 = Norm(memory, "n8", ya, turned=False)
        HEADS = GB * H1
        FORMS = (4, 5, 2, 3, 0, 1)
        NE1, NW, NR = 5, 10, 5
        block = ctx.enter_context(nc.Block())

        def tok(t):
            return slice(t * P, (t + 1) * P)

        def x3(g, t):
            return keep["x"][:, bass.ds(NT * g + t, 1), :].rearrange("p o n -> p (o n)")

        @block.sync
        def _(sp):
            def load(done, pairs):
                for dst, src in pairs:
                    sp.dma_start(dst[:, :, :], dram[src].rearrange("(k p) n -> p k n", p=P)).then_inc(done, 16)

            sp.dma_start(bm1[:, :], dram["bm1"]).then_inc(rows, 16)
            sp.dma_start(cols[:, :, :], dram["cols"]).then_inc(rows, 16)
            sp.dma_start(rope[:, :, :], dram["rope"]).then_inc(rows, 16)
            sp.dma_start(headmask[:, :], dram["headmask"]).then_inc(rows, 16)
            sp.dma_start(brow[:, :, :], dram["rows"].rearrange("(o r) n -> o r n", o=1).to_broadcast([P, 3, D])).then_inc(rows, 16)
            load(early, ((wgate, "wgate"), (wclock, "wclock"), (wpp, "wpp"), (wqk, "wqk"), (wv1, "wv1")))
            sp.wait_ge(n4.stats, 1)
            load(weights, ((wout, "wout"), (wm1, "wm1"), (wm2, "wm2"), (wxq, "wxq"), (wxk, "wxk"), (wxv, "wxv"), (wxp, "wxp"),
                           (wr, "wr"), (wk2, "wk2"), (wv2, "wv2")))
            sp.sem_inc(free, 1)
            with sp.Fori(0, G) as g:
                for b in range(GB):
                    sp.dma_start(memt[:, :, b * S2:(b + 1) * S2], dram["ctxt"].rearrange("(g b) (k p) s -> g b p k s", b=GB, p=P)[g, b]).then_inc(loaded, 16)
                sp.wait_ge(n8.normed, NT * g + NT)
                sp.dma_start(dram["out"].rearrange("(g t p) n -> g p t n", p=P, t=NT)[g], xo[:, :, :]).then_inc(stored, 16)
                end_of_turn(sp, g, turn, alone)
                sp.wait_ge(stored, 16 * g + 16)
                sp.sem_inc(free, 1)

        @block.gpsimd
        def _(pool):
            pool.memset(ident[:, :], 0.0)
            pool.memset(minus_half[:, :], -0.5)
            pool.memset(eps[:, :], EPS)
            pool.memset(ones[:, :], 1.0)
            pool.memset(tiny[:, :], 1e-8)
            pool.memset(mask1[:, :], 3e38)
            pool.memset(maskx[:, :, :], 0.0)
            pool.memset(va[:, :, :, :], 0.0)
            pool.drain()
            pool.memset(va[:, :, :, DH1:DH1 + 1], 1.0)
            pool.affine_select(out=ident[:, :], in_=ident[:, :], compare_op=ALU.not_equal, fill=1.0, base=0,
                               pattern=[[-1, P]], channel_multiplier=1)
            for c in (0, S):
                pool.affine_select(out=mask1[:, c:c + P], in_=mask1[:, c:c + P], compare_op=ALU.is_ge,
                                   fill=-1e30, base=0, pattern=[[1, P]], channel_multiplier=-1)
            for h in range(HX):
                mh = maskx[:, 0, h * S2:(h + 1) * S2]
                pool.affine_select(out=mh, in_=mh, compare_op=ALU.is_ge, fill=-8e13, base=0,
                                   pattern=[[-1, S2]], channel_multiplier=1)
            pool.drain()
            pool.nop().then_inc(const, 1)
            pool.wait_ge(rows, NR * 16)

            def add_rows(g, src, r):
                for t in range(NT):
                    last = pool.tensor_tensor(xb[:, t, :], src(t), brow[:, r, :], ALU.add)
                return last

            def gather(g):
                pool.tensor_copy(at[:, :, :], keep["slot"][:, :, bass.ds(g * NT, NT)])
                pool.drain()
                for n in range(2 * NT):
                    pool.indirect_dma_start(back[:, n, :], None, dram["y2"][:, :],
                                            bass.IndirectOffsetOnAxis(ap=at[:, n % 2, n // 2:n // 2 + 1], axis=0)).then_inc(backed[n], 16)

            gather(0)
            norm_rstd(pool, 0, n3, eps[:, :], minus_half[:, 0:NT])
            norm_rstd(pool, 0, n4, eps[:, :], minus_half[:, 0:NT])
            pool.wait_ge(n3.normed, NT)
            with pool.Fori(0, G) as g:
                pool.wait_ge(free, g + 1)
                pool.sem_inc(alone, 1)
                add_rows(g, lambda t: x3(g, t), 0).then_inc(biased, 1)
                for t in range(NT):
                    pool.wait_ge(qnr, NT * g + t + 1)
                    pool.tensor_tensor(ra[:, t, :].rearrange("p (h d) -> p h d", d=DH1),
                                       qn[:, t, :].rearrange("p (h d) -> p h d", d=DH1),
                                       rope[:, t % 2:t % 2 + 1, 0:DH1].to_broadcast([P, 32, DH1]), ALU.mult)
                pool.drain()
                for t in range(NT):
                    pool.wait_ge(rar, NT * g + t + 1)
                    pool.tensor_tensor(rb[:, t, :], rb[:, t, :], ra[:, t, :], ALU.add).then_inc(roped, 1)
                norm_rstd(pool, g, n5, eps[:, :], minus_half[:, 0:NT])
                gather((g + 1) % G)
                norm_rstd(pool, g + 1, n3, eps[:, :], minus_half[:, 0:NT])
                norm_rstd(pool, g + 1, n4, eps[:, :], minus_half[:, 0:NT])
                pool.drain()
                add_rows(g, lambda t: x3(g, t), 1)
                pool.drain()
                pool.tensor_tensor(xb[:, :, :], xb[:, :, :], yb[:, :, :], ALU.add).then_inc(biased, 1)
                norm_rstd(pool, g, n6, eps[:, :], minus_half[:, 0:NT])
                pool.drain()
                pool.wait_ge(n6.normed, NT * g + NT)
                add_rows(g, lambda t: x4[:, t, :], 2).then_inc(biased, 1)
                norm_rstd(pool, g, n7, eps[:, :], minus_half[:, 0:NT])
                norm_rstd(pool, g, n8, eps[:, :], minus_half[:, 0:NT])
                end_of_turn(pool, g, turn, alone)

        @block.tensor
        def _(pe):
            def product(out, pairs):
                for i, (w, r) in enumerate(pairs):
                    last = pe.matmul(out, w, r, start=i == 0, stop=i == len(pairs) - 1)
                return last

            pe.wait_ge(early, NE1 * 16)
            pe.wait_ge(const, 1)
            with pe.Fori(0, G) as g:
                norm_turn(pe, g, n4, lambda t: xn[:, t, :], bank[6:8], ident[:, :])
                pe.wait_ge(n4.copied, NT * g + NT)
                for i, c in enumerate(FORMS):
                    if i >= 2:
                        pe.wait_ge(fmread, 6 * g + i - 1)
                    w = (wpp, wclock, wgate)[c // 2]
                    product(bank[6 + i % 2][:, :], [(w[:, k, tok(c % 2)], xnt[:, k, :]) for k in range(KD)]).then_inc(fmm, 1)
                for t in range(NT):
                    product(bank[t][:, :], [(xnt[:, k, tok(t)], wqk[:, k, :]) for k in range(KD)]).then_inc(qkmm, 1)
                for t in range(NT):
                    if t >= 2:
                        pe.wait_ge(vcop, NT * g + t - 1)
                    product(bank[4 + t % 2][:, 0:D], [(xnt[:, k, tok(t)], wv1[:, k, :]) for k in range(KD)]).then_inc(vmm, 1)
                for t in range(NT):
                    pe.wait_ge(roped, NT * g + t + 1)
                    for c in range(4):
                        last = pe.transpose(bank[t][:, tok(c)], rb[:, t, tok(c)], ident[:, :])
                    last.then_inc(qktp, 1)
                for i in range(HEADS + 2):
                    if i < HEADS:
                        b, h = i // H1, i % H1
                        m, k0 = h // 8, h // 8 * GT + b * S
                        if i < 4:
                            pe.wait_ge(kmdve, 4 * g + i + 1)
                        elif i < 8:
                            pe.wait_ge(kmact, 4 * g + i - 3)
                        if i >= 2:
                            pe.wait_ge(s1m, HEADS * g + i - 1)
                        pe.matmul(bank[i % 2][:, 0:S], ktm[:, h % 8, k0:k0 + P],
                                  qt[:, m, b * S:(b + 1) * S], start=True, stop=True)
                        pe.matmul(bank[i % 2][:, S:S + P], ktm[:, h % 8, k0 + P:k0 + S],
                                  qt[:, m, b * S + P:(b + 1) * S], start=True, stop=True).then_inc(s1, 1)
                    j = i - 2
                    if j >= 0:
                        b, h = j // H1, j % H1
                        pe.wait_ge(s1e, HEADS * g + j + 1)
                        if j == 0:
                            pe.wait_ge(vcop, NT * g + NT)
                        if j % 4 == 0 and j >= 8:
                            pe.wait_ge(utc, HEADS // 4 * g + j // 4 - 1)
                        o = bank[4 + j // 4 % 2][32 * (h % 4):32 * (h % 4) + 32, :]
                        pe.matmul(o[:, 0:S], va[:, 2 * b, h, :], es[:, j % 4, 0:S], start=True, stop=False)
                        pe.matmul(o[:, P:S], va[:, 2 * b + 1, h, :], es[:, j % 4, S:S + P],
                                  start=False, stop=True).then_inc(av1, 1)
                pe.wait_ge(utc, HEADS // 4 * (g + 1))
                pe.wait_ge(weights, NW * 16)
                for t in range(NT + 1):
                    if t < NT:
                        if t >= 2:
                            pe.wait_ge(ogr, NT * g + t - 1)
                        for c in range(4):
                            last = pe.transpose(bank[2 + t % 2][:, tok(c)], ut[:, c, tok(t)], ident[:, :])
                        last.then_inc(ttp, 1)
                    if t >= 1:
                        j = t - 1
                        pe.wait_ge(ogr, NT * g + j + 1)
                        if j >= 2:
                            pe.wait_ge(ogc, NT * g + j - 1)
                        for k in range(KD):
                            last = pe.transpose(bank[6 + j % 2][:, tok(k)], og[:, j, tok(k)], ident[:, :])
                        last.then_inc(ogtp, 1)
                for t in range(NT):
                    pe.wait_ge(ogc, NT * g + t + 1)
                    if t >= 2:
                        pe.wait_ge(n5.added, NT * g + t - 1)
                    product(bank[4 + t % 2][:, 0:D], [(ogt[:, k, tok(t)], wout[:, k, :]) for k in range(KD)]).then_inc(n5.product, 1)
                norm_turn(pe, g, n5, lambda t: h5[:, t, :], bank[2:4], ident[:, :])
                pe.wait_ge(n5.copied, NT * g + NT)
                for c in range(MC):
                    if c >= 4:
                        pe.wait_ge(m1g, MC * g + c - 3)
                    product(bank[(0, 1, 4, 5)[c % 4]][:, :], [(wm1[:, k, tok(c)], h5t[:, k, :]) for k in range(KD)]).then_inc(m1mm, 1)
                pe.wait_ge(m1g, MC * g + MC)
                for t in range(NT):
                    if t >= 2:
                        pe.wait_ge(n6.added, NT * g + t - 1)
                    product(bank[6 + t % 2][:, 0:D], [(m1t[:, k, tok(t)], wm2[:, k, :]) for k in range(MC)]).then_inc(n6.product, 1)
                pe.wait_ge(loaded, 32 * g + 32)
                for c in range(KD):
                    product(bank[4 + c][:, 0:GB * S2], [(wxk[:, k, tok(c)], memt[:, k, :]) for k in range(KD)]).then_inc(xkm, 1)
                norm_turn(pe, g, n6, lambda t: x4[:, t, :], bank[2:4], ident[:, :])
                for b in range(GB):
                    product(bank[6 + b][0:S2, 0:D], [(memt[:, k, b * S2:(b + 1) * S2], wxv[:, k, :]) for k in range(KD)]).then_inc(xvm, 1)
                pe.wait_ge(n6.copied, NT * g + NT)
                for c in range(KD):
                    product(bank[c][:, :], [(wxq[:, k, tok(c)], x4t[:, k, :]) for k in range(KD)]).then_inc(xq, 1)
                pe.wait_ge(xqr, KD * g + KD)
                pe.wait_ge(xkr, KD * g + KD)
                for t in range(NT + 2):
                    if t < NT:
                        if t >= 2:
                            pe.wait_ge(xsr, NT * g + t - 1)
                        for h in range(HX):
                            r = slice(DHX * (h % 2), DHX * (h % 2) + DHX)
                            last = pe.matmul(bank[t % 2 + 2 * (h % 2)][:, h // 2 * S2:(h // 2 + 1) * S2], qxt[r, h // 2, tok(t)],
                                             kxt[r, h // 2, t // 2 * S2:(t // 2 + 1) * S2], start=True, stop=True)
                        last.then_inc(xs, 1)
                    if t >= 2:
                        j = t - 2
                        pe.wait_ge(xp, NT * g + j + 1)
                        if j >= 2:
                            pe.wait_ge(xtc, NT * g + j - 1)
                        for h in range(HX):
                            last = pe.transpose(bank[4 + j % 2][0:S2, tok(h)], sm[:, j, h * S2:(h + 1) * S2], ident[:, :])
                        last.then_inc(xtp, 1)
                pe.wait_ge(xtc, NT * g + NT)
                pe.wait_ge(xvr, GB * g + GB)
                for q in range(GB * KD):
                    b, m = q // KD, q % KD
                    if q >= 2:
                        pe.wait_ge(xz, 4 * g + q - 1)
                    for hh in range(2):
                        h = 2 * m + hh
                        last = pe.matmul(bank[6 + q % 2][DHX * hh:DHX * (hh + 1), 0:S], vx[:, b, h * DHX:(h + 1) * DHX],
                                         pxt[:, b, h, :], start=True, stop=True)
                    last.then_inc(xav, 1)
                pe.wait_ge(xz, 4 * g + 4)
                for t in range(NT):
                    if t >= 2:
                        pe.wait_ge(n7.added, NT * g + t - 1)
                    product(bank[t % 2][:, 0:D], [(zxt[:, k, tok(t)], wxp[:, k, :]) for k in range(KD)]).then_inc(n7.product, 1)
                norm_turn(pe, g, n7, lambda t: x5[:, t, :], bank[2:4], ident[:, :])
                pe.wait_ge(mixk, g + 1)
                for c in range(KD):
                    product(bank[c][:, :], [(wk2[:, k, tok(c)], xk[:, k, :]) for k in range(KD)]).then_inc(kmm, 1)
                pe.wait_ge(mixr, g + 1)
                for t in range(NT):
                    if t >= 2:
                        pe.wait_ge(rsig, NT * g + t - 1)
                    product(bank[4 + t % 2][:, 0:D], [(xr[:, k, tok(t)], wr[:, k, :]) for k in range(KD)]).then_inc(rmm, 1)
                pe.wait_ge(kact, KD * g + KD)
                for t in range(NT):
                    if t >= 2:
                        pe.wait_ge(n8.added, NT * g + t - 1)
                    product(bank[6 + t % 2][:, 0:D], [(ka[:, k, tok(t)], wv2[:, k, :]) for k in range(KD)]).then_inc(n8.product, 1)
                end_of_turn(pe, g, turn, alone)

        @block.scalar
        def _(act):
            act.wait_ge(rows, NR * 16)

            def affine_copy(g, n, banks, gain, bias):
                for t in range(NT):
                    act.wait_ge(n.turned, NT * g + t + 1)
                    for k in range(KD):
                        last = act.activation(xnt[:, k, tok(t)], banks[t % 2][:, tok(k)], ACT.Identity,
                                              bias=cols[:, bias, k:k + 1], scale=cols[:, gain, k:k + 1])
                    last.then_inc(n.copied, 1)

            with act.Fori(0, G) as g:
                affine_copy(g, n4, bank[6:8], G1, B1)
                def square(t):
                    act.wait_ge(qkmm, NT * g + t + 1)
                    if t >= 2:
                        act.wait_ge(sqred, NT * g + t - 1)
                    act.activation(sq[:, t % 2, :], bank[t][:, :], ACT.Square).then_inc(sqd, 1)

                def form(i):
                    c = FORMS[i]
                    act.wait_ge(fmm, 6 * g + i + 1)
                    act.activation(fm[:, c, :], bank[6 + i % 2][:, :], ACT.Identity,
                                   bias=cols[:, (BP, BCLK, BGATE)[c // 2], c % 2:c % 2 + 1]).then_inc(fmread, 1)

                def small(c, done):
                    act.drain()
                    act.activation(ee[:, c:c + 2, :], fm[:, c + 2:c + 4, :], ACT.Abs)
                    act.drain()
                    act.activation(ee[:, c:c + 2, :], ee[:, c:c + 2, :], ACT.Exp, scale=-1.0).then_inc(done, 1)

                form(0)
                form(1)
                small(2, egate)
                form(2)
                form(3)
                act.wait_ge(ugate, g + 1)
                act.activation(uu[:, 2:4, :], uu[:, 2:4, :], ACT.Ln).then_inc(lgate, 1)
                form(4)
                form(5)
                small(0, eready)
                act.wait_ge(npm, g + 1)
                for c in range(KD * GB):
                    pc = fm[:, c // GB, c % GB * S:(c % GB + 1) * S]
                    last = act.activation(pc, pc, ACT.Exp, bias=pmax[:, c:c + 1])
                last.then_inc(pexp, 1)
                act.wait_ge(clr, g + 1)
                act.activation(uu[:, 2:4, :], ee[:, 2:4, :], ACT.Exp, scale=-1.0).then_inc(gcr, 1)
                act.wait_ge(uready, g + 1)
                act.activation(uu[:, 0:2, :], uu[:, 0:2, :], ACT.Ln).then_inc(lready, 1)
                act.drain()
                act.activation(ee[:, 0:2, :], uu[:, 2:4, :], ACT.Ln, bias=tiny[:, :])
                for t in range(NT):
                    square(t)
                for t in range(NT):
                    act.wait_ge(vmm, NT * g + t + 1)
                    act.activation(va[:, t, :, 0:DH1], bank[4 + t % 2][:, 0:D].rearrange("p (h d) -> p h d", d=DH1),
                                   ACT.Copy).then_inc(vcop, 1)
                act.wait_ge(sumr, g + 1)
                act.activation(ee[:, 2:4, :], dd, ACT.Ln, bias=tiny[:, :])
                act.wait_ge(ssready, g + 1)
                act.activation(rn[:, :], ss[:, :], ACT.Sqrt).then_inc(rnr, 1)
                act.drain()
                act.activation(ee, ee, ACT.Exp, scale=-1.0).then_inc(first, 1)
                act.wait_ge(qkt, NT * g + NT)
                for o in range(4, 8):
                    act.activation(ktm[:, o, :], kt[:, :, :].rearrange("p k n -> p (k n)"), ACT.Identity,
                                   scale=headmask[:, o:o + 1]).then_inc(kmact, 1)
                for i in range(HEADS):
                    act.wait_ge(s1m, HEADS * g + i + 1)
                    act.activation(es[:, i % 4, :], es[:, i % 4, :], ACT.Exp, scale=DH1 ** -0.5).then_inc(s1e, 1)
                for t in range(NT):
                    act.wait_ge(ogtp, NT * g + t + 1)
                    act.activation(ogt[:, :, tok(t)], bank[6 + t % 2][:, 0:D].rearrange("p (k n) -> p k n", k=KD),
                                   ACT.Copy).then_inc(ogc, 1)
                affine_copy(g, n5, bank[2:4], G2, B2)
                for c in range(MC):
                    act.wait_ge(m1mm, MC * g + c + 1)
                    act.activation(m1t[:, c, :], bank[(0, 1, 4, 5)[c % 4]][:, :], ACT.Gelu, bias=bm1[:, c:c + 1]).then_inc(m1g, 1)
                norm_copy(act, g, n6, bank[2:4], lambda t: x4t[:, :, tok(t)])
                for b in range(GB):
                    act.wait_ge(xvm, GB * g + b + 1)
                    act.activation(vx[:, b, :], bank[6 + b][0:S2, 0:D], ACT.Copy).then_inc(xvr, 1)
                for c in range(KD):
                    act.wait_ge(xq, KD * g + c + 1)
                    act.activation(qxt[:, c, :], bank[c][:, :], ACT.Copy).then_inc(xqr, 1)
                for t in range(NT + 1):
                    if t < NT:
                        act.wait_ge(xsub, NT * g + t + 1)
                        act.activation(sm[:, t, :], sm[:, t, :], ACT.Exp, scale=DHX ** -0.5).then_inc(xe, 1)
                    if t >= 1:
                        j = t - 1
                        act.wait_ge(xtp, NT * g + j + 1)
                        act.activation(pxt[:, j // 2, :, tok(j % 2)], bank[4 + j % 2][0:S2, :].rearrange("p (h n) -> p h n", h=HX),
                                       ACT.Copy).then_inc(xtc, 1)
                norm_copy(act, g, n7, bank[2:4], lambda t: x5t[:, :, t // 2, 1 + t % 2 * P:1 + (t % 2 + 1) * P])
                for c in range(KD):
                    act.wait_ge(kmm, KD * g + c + 1)
                    act.activation(rl[:, c, :], bank[c][:, :], ACT.Relu).then_inc(relu, 1)
                for t in range(NT):
                    act.wait_ge(rmm, NT * g + t + 1)
                    act.activation(rs[:, t, :], bank[4 + t % 2][:, 0:D], ACT.Sigmoid).then_inc(rsig, 1)
                end_of_turn(act, g, turn, alone)

        @block.vector
        def _(dve):
            dve.wait_ge(const, 1)
            dve.wait_ge(rows, NR * 16)
            dve.tensor_scalar(unmu[:, :, :], cols[:, MUR:MUK + 1, :], -1.0, 1.0, ALU.mult, ALU.add)

            def add_product(g, n, banks):
                for t in range(NT):
                    dve.wait_ge(n.product, NT * g + t + 1)
                    dve.tensor_tensor(n.y[:, t, :], banks[t % 2][:, 0:D], xb[:, t, :], ALU.add).then_inc(n.added, 1)
                    norm_tile_stats(dve, g, n, t)

            def begin(turn, g):
                for n in range(2 * NT):
                    t = n // 2
                    if n % 2:
                        dve.drain()
                    dve.wait_ge(backed[n], 16 * turn + 16)
                    dve.sem_inc(alone, 1)
                    dve.scalar_tensor_tensor(x3(g, t), back[:, n, :], keep["weight"][:, bass.ds(NT * g + t, 1), n % 2],
                                             x3(g, t), ALU.mult, ALU.add)
                for norm in (n3, n4):
                    for t in range(NT):
                        dve.drain()
                        dve.bn_stats(norm.bn[:, t, :], x3(g, t))
                    dve.drain()
                    for t in range(NT):
                        last = dve.bn_aggr(norm.mv[:, t, :], norm.bn[:, t, :])
                    last.then_inc(norm.stats, 1)
                    if norm is n3:
                        dve.drain()
                        dve.wait_ge(n3.rstd, turn + 1)
                        for t in range(NT):
                            dve.tensor_scalar(x3(g, t), x3(g, t), n3.mv[:, t, 0:1], n3.inv[:, t:t + 1],
                                              ALU.subtract, ALU.mult).then_inc(n3.normed, 1)

            begin(0, 0)
            with dve.Fori(0, G) as g:
                dve.drain()
                dve.wait_ge(n4.rstd, g + 1)
                for t in range(NT):
                    dve.tensor_scalar(xn[:, t, :], x3(g, t), n4.mv[:, t, 0:1], n4.inv[:, t:t + 1],
                                      ALU.subtract, ALU.mult).then_inc(n4.normed, 1)
                dve.wait_ge(egate, g + 1)
                dve.tensor_scalar(uu[:, 2:4, :], ee[:, 2:4, :], 1.0, None, ALU.add)
                dve.drain()
                dve.scalar_tensor_tensor(dd, uu[:, 2:4, :], -1.0, ee[:, 2:4, :], ALU.add, ALU.subtract).then_inc(ugate, 1)
                dve.drain()
                dve.scalar_tensor_tensor(dd, fm[:, 4:6, :], 0.0, dd, ALU.max, ALU.subtract)
                dve.drain()
                dve.wait_ge(lgate, g + 1)
                dve.tensor_tensor(dd, dd, uu[:, 2:4, :], ALU.add)
                dve.drain()
                for m in range(KD):
                    for b in range(GB):
                        dve.tensor_tensor_scan(ee[:, 2 + m, b * S:(b + 1) * S], ones[:, :], dd[:, m, b * S:(b + 1) * S],
                                               0.0, ALU.mult, ALU.add)
                dve.drain()
                dve.tensor_scalar(ee[:, 2:4, :], ee[:, 2:4, :], -50.0, 60.0, ALU.max, ALU.min).then_inc(clr, 1)
                dve.wait_ge(fmread, 6 * g + 6)
                dve.tensor_reduce(pmax[:, :], fm[:, 0:2, :].rearrange("p m (b s) -> p (m b) s", b=GB), AX.X, ALU.max)
                dve.drain()
                dve.tensor_scalar(pmax[:, :], pmax[:, :], -1.0, None, ALU.mult).then_inc(npm, 1)
                dve.wait_ge(eready, g + 1)
                dve.tensor_scalar(uu[:, 0:2, :], ee[:, 0:2, :], 1.0, None, ALU.add)
                dve.drain()
                dve.scalar_tensor_tensor(dd, uu[:, 0:2, :], -1.0, ee[:, 0:2, :], ALU.add, ALU.subtract).then_inc(uready, 1)
                dve.drain()
                dve.scalar_tensor_tensor(fm[:, 2:4, :], fm[:, 2:4, :], 0.0, dd, ALU.max, ALU.subtract)
                dve.drain()
                dve.wait_ge(lready, g + 1)
                dve.tensor_tensor(fm[:, 2:4, :], fm[:, 2:4, :], uu[:, 0:2, :], ALU.add)
                dve.drain()
                dve.wait_ge(pexp, g + 1)
                dve.tensor_tensor(fm[:, 0:2, :], fm[:, 0:2, :], fm[:, 2:4, :], ALU.mult)
                dve.drain()
                for m in range(KD):
                    for b in range(GB):
                        dve.tensor_tensor_scan(dd[:, m, b * S:(b + 1) * S], ones[:, :], fm[:, m, b * S:(b + 1) * S],
                                               0.0, ALU.mult, ALU.add)
                dve.drain()
                dve.nop().then_inc(sumr, 1)
                for t in range(NT):
                    dve.wait_ge(sqd, NT * g + t + 1)
                    dve.tensor_reduce(ss[:, t * 32:(t + 1) * 32], sq[:, t % 2, :].rearrange("p (h d) -> p h d", d=DH1),
                                      AX.X, ALU.add).then_inc(sqred, 1)
                dve.drain()
                dve.tensor_scalar(ss[:, :], ss[:, :], 1e-24, None, ALU.max).then_inc(ssready, 1)
                dve.wait_ge(rnr, g + 1)
                dve.reciprocal(rn[:, :], rn[:, :])
                dve.drain()
                dve.tensor_tensor(r2[:, :], rn[:, :], rn[:, :], ALU.mult)
                dve.drain()
                dve.tensor_tensor(r2[:, :], r2[:, :], ss[:, :], ALU.mult)
                dve.drain()
                dve.tensor_scalar(r2[:, :], r2[:, :], -0.5, 1.5, ALU.mult, ALU.add)
                dve.drain()
                dve.tensor_tensor(rn[:, :], rn[:, :], r2[:, :], ALU.mult)
                dve.drain()
                for t in range(NT):
                    dve.tensor_tensor(qn[:, t, :].rearrange("p (h d) -> p h d", d=DH1),
                                      bank[t][:, :].rearrange("p (h d) -> p h d", d=DH1),
                                      rn[:, t * 32:(t + 1) * 32].unsqueeze(2).to_broadcast([P, 32, DH1]), ALU.mult).then_inc(qnr, 1)
                dve.drain()
                for t in range(NT):
                    q4 = qn[:, t, :].rearrange("p (h d two) -> p h d two", d=DH1 // 2, two=2)
                    r4 = rb[:, t, :].rearrange("p (h d two) -> p h d two", d=DH1 // 2, two=2)
                    for o in range(2):
                        last = dve.tensor_tensor(r4[:, :, :, o], q4[:, :, :, 1 - o],
                                                 rope[:, t % 2:t % 2 + 1, DH1 + 8 * o:DH1 + 8 * o + 8].to_broadcast([P, 32, 8]), ALU.mult)
                    last.then_inc(rar, 1)
                dve.wait_ge(first, g + 1)
                for f, x, y, other in ((kf, uu[:, 2:4, :], ee[:, 0:2, :], fm[:, 0:2, :]), (qf, dd, ee[:, 2:4, :], uu[:, 2:4, :])):
                    dve.scalar_tensor_tensor(f[:, :, :], x, 1e-8, y, ALU.add, ALU.mult)
                    dve.drain()
                    dve.scalar_tensor_tensor(f[:, :, :], f[:, :, :], 2.0, y, ALU.subtract, ALU.mult)
                    dve.drain()
                    dve.tensor_tensor(f[:, :, :], f[:, :, :], other, ALU.mult)
                dve.drain()
                for t in range(NT):
                    dve.wait_ge(qktp, NT * g + t + 1)
                    qk = bank[t][:, :].rearrange("p (c n) -> p c n", c=4)
                    dve.tensor_tensor(kt[:, :, tok(t)], qk[:, 2:4, :], kf[:, :, tok(t)], ALU.mult)
                    dve.tensor_tensor(qt[:, :, tok(t)], qk[:, 0:2, :], qf[:, :, tok(t)], ALU.mult).then_inc(qkt, 1)
                dve.drain()
                for o in range(4):
                    dve.tensor_scalar(ktm[:, o, :], kt[:, :, :].rearrange("p k n -> p (k n)"), headmask[:, o:o + 1], None,
                                      ALU.mult).then_inc(kmdve, 1)
                for i in range(HEADS + 3):
                    if i < HEADS:
                        dve.wait_ge(s1, HEADS * g + i + 1)
                        if i >= 4:
                            dve.wait_ge(av1, HEADS * g + i - 3)
                        dve.tensor_tensor(es[:, i % 4, :], bank[i % 2][:, 0:CAUSAL], mask1[:, :], ALU.min).then_inc(s1m, 1)
                    j = i - 3
                    if j >= 0 and j % 4 == 3:
                        q = j // 4
                        dve.wait_ge(av1, HEADS * g + j + 1)
                        dve.tensor_copy(ut[:, q % 4, q // 4 * S:(q // 4 + 1) * S], bank[4 + q % 2][:, 0:S]).then_inc(utc, 1)
                for t in range(NT):
                    dve.wait_ge(ttp, NT * g + t + 1)
                    heads = bank[2 + t % 2][:, :].rearrange("p (h d) -> p h d", d=32)
                    dve.reciprocal(rden[:, t, :], heads[:, :, DH1])
                    dve.drain()
                    dve.tensor_tensor(og[:, t, :].rearrange("p (h d) -> p h d", d=DH1), heads[:, :, 0:DH1],
                                      rden[:, t, :].unsqueeze(2).to_broadcast([P, H1, DH1]), ALU.mult).then_inc(ogr, 1)
                dve.wait_ge(biased, 3 * g + 1)
                add_product(g, n5, bank[4:6])
                norm_rows(dve, g, n5, lambda t: h5[:, t, :])
                begin(g + 1, (g + 1) % G)
                dve.wait_ge(biased, 3 * g + 2)
                add_product(g, n6, bank[6:8])
                for c in range(KD):
                    dve.wait_ge(xkm, KD * g + c + 1)
                    dve.tensor_copy(kxt[:, c, :], bank[4 + c][:, 0:GB * S2]).then_inc(xkr, 1)
                norm_rows(dve, g, n6, lambda t: x4[:, t, :])
                for t in range(NT + 1):
                    if t < NT:
                        dve.wait_ge(xs, NT * g + t + 1)
                        for o in range(2):
                            last = dve.tensor_tensor(sm[:, t, :].rearrange("p (h two n) -> p h two n", two=2, n=S2)[:, :, o, :],
                                                     bank[t % 2 + 2 * o][:, 0:2 * S2].rearrange("p (h n) -> p h n", n=S2),
                                                     maskx[:, t % 2, 0:2 * S2].rearrange("p (h n) -> p h n", n=S2), ALU.add)
                        last.then_inc(xsr, 1)
                        dve.drain()
                        s3 = sm[:, t, :].rearrange("p (h n) -> p h n", h=HX)
                        dve.tensor_reduce(xmax[:, t, :], s3, AX.X, ALU.max)
                        dve.drain()
                        dve.tensor_tensor(s3, s3, xmax[:, t, :].unsqueeze(2).to_broadcast([P, HX, S2]), ALU.subtract).then_inc(xsub, 1)
                    if t >= 1:
                        j = t - 1
                        s3 = sm[:, j, :].rearrange("p (h n) -> p h n", h=HX)
                        dve.wait_ge(xe, NT * g + j + 1)
                        dve.tensor_reduce(xsum[:, j, :], s3, AX.X, ALU.add)
                        dve.drain()
                        dve.reciprocal(xinv[:, j, :], xsum[:, j, :])
                        dve.drain()
                        dve.tensor_tensor(s3, s3, xinv[:, j, :].unsqueeze(2).to_broadcast([P, HX, S2]), ALU.mult).then_inc(xp, 1)
                for q in range(GB * KD):
                    dve.wait_ge(xav, 4 * g + q + 1)
                    dve.tensor_copy(zxt[:, q % KD, q // KD * S:(q // KD + 1) * S], bank[6 + q % 2][:, 0:S]).then_inc(xz, 1)
                dve.wait_ge(biased, 3 * g + 3)
                add_product(g, n7, bank[0:2])
                norm_rows(dve, g, n7, lambda t: x5[:, t, :])
                dve.memset(x5t[:, :, :, 0:1], 0.0)
                dve.drain()
                dve.wait_ge(n7.copied, NT * g + NT)
                for mu, dst, done in ((MUK, xk, mixk), (MUR, xr, mixr)):
                    for k in range(KD):
                        dve.tensor_scalar(shift[:, k, :].rearrange("p (b s) -> p b s", b=GB), x5t[:, k, :, 0:S],
                                          unmu[:, mu - MUR, k:k + 1], None, ALU.mult)
                    dve.drain()
                    for k in range(KD):
                        last = dve.scalar_tensor_tensor(dst[:, k, :].rearrange("p (b s) -> p b s", b=GB), x5t[:, k, :, 1:S + 1],
                                                        cols[:, mu, k:k + 1], shift[:, k, :].rearrange("p (b s) -> p b s", b=GB),
                                                        ALU.mult, ALU.add)
                    last.then_inc(done, 1)
                    dve.drain()
                for c in range(KD):
                    dve.wait_ge(relu, KD * g + c + 1)
                    dve.tensor_tensor(ka[:, c, :], bank[c][:, :], rl[:, c, :], ALU.mult).then_inc(kact, 1)
                dve.wait_ge(rsig, NT * g + NT)
                for t in range(NT):
                    dve.wait_ge(n8.product, NT * g + t + 1)
                    dve.tensor_tensor(rs[:, t, :], bank[6 + t % 2][:, 0:D], rs[:, t, :], ALU.mult).then_inc(n8.added, 1)
                    dve.drain()
                    dve.tensor_tensor(n8.y[:, t, :], rs[:, t, :], x5[:, t, :], ALU.add)
                    norm_tile_stats(dve, g, n8, t)
                norm_rows(dve, g, n8, lambda t: xo[:, t, :])
                end_of_turn(dve, g, turn, alone)


def decoder(nc, dram):
    with ExitStack() as ctx:
        memory = Memory(nc, ctx)
        keep = {"x": memory.take([P, TILES, D])}
        keep["weight"] = memory.take([P, TILES, 2])
        keep["slot"] = memory.take([P, 2, TILES], I32)
        last = memory.mark
        keep["pick"] = memory.take([P, TILES, NE])
        keep["at"] = memory.take([P, TILES, 2])
        first = memory.mark
        attention_layers(nc, dram, memory, keep)
        memory.mark = first
        memory.clear()
        expert_layer(nc, dram, memory, keep)
        memory.mark = last
        last_layers(nc, dram, memory, keep)


def laid_out(a):
    def t(x):
        return x.T

    def columns(v):
        return v.reshape(-1, P).T

    w1, b1 = a["L0_ffn_dense_1_w"], a["L0_ffn_dense_1_b"]
    x = a["x"].reshape(B * S, D)
    half = DH1 // 2
    freqs = np.exp(-np.arange(half, dtype=np.float32) * np.float32(np.log(10000.0) / half)).astype(np.float32)
    theta = (np.arange(S, dtype=np.float32)[:, None] * freqs[None, :]).astype(np.float32)
    cos, sin = np.cos(theta), np.sin(theta)
    rope = np.concatenate([np.repeat(cos, 2, 1), -sin, sin], 1).astype(np.float32)
    return {
        "x": x, "xt": t(x), "mask": a["mask_BxSxS2_ik0"].reshape(B * S, S2),
        "ctx": a["ctx_1024"], "ctxt": a["ctx_1024"].transpose(0, 2, 1),
        "wq0": t(a["L0_attn_W_Q"].reshape(E0, D)), "wk0": t(a["L0_attn_W_K"].reshape(E0, D)),
        "wv0": t(a["L0_attn_W_V"].reshape(E0, D)), "wo0": a["L0_attn_W_O"].transpose(0, 2, 1).reshape(E0, D),
        "wx0": t(a["L0_xattn_W"]), "bx0": columns(a["L0_xattn_b"]), "gate": a["L0_ffn_gate_w"],
        "w1": np.concatenate([w1[:, 0::2], w1[:, 1::2]], 1).transpose(0, 2, 1),
        "w2": a["L0_ffn_dense_2_w"].transpose(0, 2, 1),
        "b1": np.concatenate([b1[:, 0::2], b1[:, 1::2]], 1),
        "b2": a["L0_ffn_dense_2_b"],
        "wqk": np.concatenate([a["L1_attn_Wq"], a["L1_attn_Wk"]], 1), "wv1": a["L1_attn_Wv"],
        "wgate": a["L1_attn_gate_w"], "wpp": a["L1_attn_p_w"], "wclock": np.repeat(a["L1_attn_clock_w"], DH1, 1),
        "wout": a["L1_attn_out_w"], "wm1": a["L1_attn_mlp_w1"], "wm2": a["L1_attn_mlp_w2"],
        "bm1": columns(a["L1_attn_mlp_b1"]),
        "cols": np.stack([columns(v) for v in (
            a["L1_attn_p_b"], np.repeat(a["L1_attn_clock_b"], DH1), a["L1_attn_gate_b"], a["L1_attn_ln1_g"],
            a["L1_attn_ln1_b"], a["L1_attn_ln2_g"], a["L1_attn_ln2_b"], a["L1_ffn_mu_r"], a["L1_ffn_mu_k"])], 1),
        "rows": np.stack([a["L1_attn_out_b"], a["L1_attn_mlp_b2"], a["L1_xattn_bp"]]),
        "wxq": t(a["L1_xattn_Wq"]), "wxk": t(a["L1_xattn_Wk"]), "wxv": t(a["L1_xattn_Wv"]), "wxp": t(a["L1_xattn_Wp"]),
        "wr": t(a["L1_ffn_W_r"]), "wk2": t(a["L1_ffn_W_k"]), "wv2": t(a["L1_ffn_W_v"]),
        "rope": rope.reshape(2, P, 2 * DH1).transpose(1, 0, 2), "headmask": (np.arange(P)[:, None] // DH1 == np.arange(8)).astype(np.float32),
    }


def kernel(**inputs):
    import concourse.bacc as bacc
    from concourse.bass_utils import run_bass_kernel_spmd

    nc = bacc.Bacc("TRN2", target_bir_lowering=False, num_devices=1)
    arrays, dram = {}, {}
    for name, a in laid_out({k: np.asarray(v) for k, v in inputs.items()}).items():
        a = np.ascontiguousarray(a)
        arrays[f"in_{name}"] = a
        dram[name] = nc.dram_tensor(f"in_{name}", a.shape, mybir.dt.from_np(a.dtype), kind="ExternalInput").ap()
    dram["x2"] = nc.dram_tensor("x2_rows", (B * S, D), F32, kind="Internal").ap()
    dram["y2"] = nc.dram_tensor("y2_slots", (SLOTS, D), F32, kind="Internal").ap()
    dram["out"] = nc.dram_tensor("out_x", (B * S, D), F32, kind="ExternalOutput").ap()
    decoder(nc, dram)
    result = run_bass_kernel_spmd(nc, [arrays], core_ids=[0])
    return result.results[0]["out_x"].reshape(B, S, D)
```
